# Optimizing a Trainium2 kernel written in Bass

```python
import numpy as np
import jax
import jax.numpy as jnp

def _softmax(x, axis=-1):
    return jax.nn.softmax(x, axis=axis)

def _gelu(x):
    return jax.nn.gelu(x, approximate=True)

def _silu(x):
    return jax.nn.silu(x)

def _sigmoid(x):
    return jax.nn.sigmoid(x)

def _layernorm(x, axis=-1, eps=1e-05):
    m = jnp.mean(x, axis=axis, keepdims=True)
    v = jnp.var(x, axis=axis, keepdims=True)
    return (x - m) / jnp.sqrt(v + eps)

def _scatter_add(tgt, idx, src, axis=0):
    return tgt.at[idx].add(src)

def _segment_sum(src, seg, n):
    return jax.ops.segment_sum(src, seg, n)
kernel_name = 'mk_adj_resnorm_d4_adj_r2_d69749'

def setup_inputs(seed: int=0):
    np.random.seed(seed)
    _w = jnp.asarray

    def _rec_inputs():
        import jax
        import jax.numpy as jnp
        _gk = jax.random.key(seed)
        x = 7.22e-05 + 1 * jax.random.normal(jax.random.fold_in(_gk, 1), (16, 512, 128), jnp.float32)
        _w = (1.0 + jnp.arange(512, dtype=jnp.float32)) ** (-0.5)
        _w = _w / _w.mean()
        _pij = jnp.clip(0.015625 * _w[:, None] * _w[None, :], 0.0, 1.0)
        _a = jax.random.uniform(jax.random.fold_in(_gk, 2), (16, 512, 512)) < _pij
        _a = jnp.logical_or(_a, jnp.eye(512, dtype=bool))
        _af = _a.astype(jnp.float32)
        _af = _af * jax.random.uniform(jax.random.fold_in(_gk, 3), (16, 512, 512), jnp.float32, 0.05, 1)
        adj = _af
        return (x, adj)
    x, adj = _rec_inputs()

    def _L0_gnn_setup():
        import jax, jax.numpy as jnp
        import numpy as np
        D_IN = 128
        D_HID = 256
        key = jax.random.key(seed)
        k1, k2, k3, k4, k5, k6 = jax.random.split(key, 6)
        x = jax.random.normal(k1, (8, 2048, D_IN), dtype=jnp.float32)
        adj = jax.random.uniform(k2, (8, 2048, 2048), dtype=jnp.float32)
        s1 = 1.0 / np.sqrt(D_IN)
        s2 = 1.0 / np.sqrt(D_HID)
        W1 = jax.random.uniform(k3, (D_IN, D_HID), dtype=jnp.float32, minval=-s1, maxval=s1)
        b1 = jax.random.uniform(k4, (D_HID,), dtype=jnp.float32, minval=-s1, maxval=s1)
        W2 = jax.random.uniform(k5, (D_HID, D_IN), dtype=jnp.float32, minval=-s2, maxval=s2)
        b2 = jax.random.uniform(k6, (D_IN,), dtype=jnp.float32, minval=-s2, maxval=s2)
        eps = jnp.zeros((1,), dtype=jnp.float32)
        return {'x': x, 'adj': adj, 'eps': eps, 'W1': W1, 'b1': b1, 'W2': W2, 'b2': b2}
    _L0_gnn_all = _L0_gnn_setup()
    _L0_gnn_in = {k: v for k, v in _L0_gnn_all.items() if k in ('eps', 'W1', 'b1', 'W2', 'b2')}
    del _L0_gnn_all

    def _L1_gnn_setup():
        import jax, jax.numpy as jnp
        import numpy as np
        from jax import lax
        DIM = 128
        EPS = 1e-05

        def _bn(h, g, b, m, v):
            scale = g / jnp.sqrt(v + EPS)
            return h * scale[None, :, None] + (b - m * scale)[None, :, None]

        def _conv1d(h, w, pad):
            return lax.conv_general_dilated(h, w, window_strides=(1,), padding=[(pad, pad)], dimension_numbers=('NCH', 'OIH', 'NCH'))
        key = jax.random.key(seed)
        ks = jax.random.split(key, 16)
        bs, n, d = (16, 1024, DIM)
        s = 0.05
        return {'x': jax.random.normal(ks[0], (bs, n, d), jnp.float32), 'mask': jnp.ones((bs, n, n), jnp.float32), 'w_se': jax.random.normal(ks[1], (3, d), jnp.float32) * s, 'b_se': jnp.zeros((3,), jnp.float32), 'conv1_w': jax.random.normal(ks[2], (d, d, 1), jnp.float32) * s, 'bn1_g': jnp.ones((d,), jnp.float32), 'bn1_b': jnp.zeros((d,), jnp.float32), 'bn1_m': jnp.zeros((d,), jnp.float32), 'bn1_v': jnp.ones((d,), jnp.float32), 'conv2_w': jax.random.normal(ks[3], (d, d, 17), jnp.float32) * s, 'bn2_g': jnp.ones((d,), jnp.float32), 'bn2_b': jnp.zeros((d,), jnp.float32), 'bn2_m': jnp.zeros((d,), jnp.float32), 'bn2_v': jnp.ones((d,), jnp.float32), 'w_msg': jax.random.normal(ks[4], (d, d), jnp.float32) * s, 'b_msg': jnp.zeros((d,), jnp.float32), 'w_ih': jax.random.normal(ks[5], (3 * d, 2 * d), jnp.float32) * s, 'b_ih': jnp.zeros((3 * d,), jnp.float32), 'w_hh': jax.random.normal(ks[6], (3 * d, d), jnp.float32) * s, 'b_hh': jnp.zeros((3 * d,), jnp.float32)}
    _L1_gnn_all = _L1_gnn_setup()
    _L1_gnn_in = {k: v for k, v in _L1_gnn_all.items() if k in ('w_se', 'b_se', 'conv1_w', 'bn1_g', 'bn1_b', 'bn1_m', 'bn1_v', 'conv2_w', 'bn2_g', 'bn2_b', 'bn2_m', 'bn2_v', 'w_msg', 'b_msg', 'w_ih', 'b_ih', 'w_hh', 'b_hh')}
    del _L1_gnn_all

    def _L2_gnn_setup():
        import jax, jax.numpy as jnp
        import numpy as np
        EPS = 1e-05
        ALPHA = 0.2

        def _bn(x, gamma, beta):
            red = tuple(range(x.ndim - 1))
            mean = jnp.mean(x, axis=red, keepdims=True)
            var = jnp.mean(jnp.square(x - mean), axis=red, keepdims=True)
            return (x - mean) * jax.lax.rsqrt(var + EPS) * gamma + beta
        key = jax.random.key(seed)
        ks = jax.random.split(key, 5)
        B, N, Fin, Fout = (32, 512, 128, 128)
        h = jax.random.normal(ks[0], (B, N, Fin), dtype=jnp.float32)
        adj = (jax.random.uniform(ks[1], (B, N, N), dtype=jnp.float32) > 0.9).astype(jnp.float32)
        W = jax.random.normal(ks[2], (Fout, Fin), dtype=jnp.float32) * (1.0 / np.sqrt(Fin))
        a1 = jax.random.normal(ks[3], (Fout,), dtype=jnp.float32) * 0.1
        a2 = jax.random.normal(ks[4], (Fout,), dtype=jnp.float32) * 0.1
        return {'h': h, 'adj': adj, 'W': W, 'a1': a1, 'a2': a2, 'g1': jnp.ones((N,), jnp.float32), 'b1': jnp.zeros((N,), jnp.float32), 'g2': jnp.ones((N,), jnp.float32), 'b2': jnp.zeros((N,), jnp.float32), 'g3': jnp.ones((Fout,), jnp.float32), 'b3': jnp.zeros((Fout,), jnp.float32)}
    _L2_gnn_all = _L2_gnn_setup()
    _L2_gnn_in = {k: v for k, v in _L2_gnn_all.items() if k in ('W', 'a1', 'a2', 'g1', 'b1', 'g2', 'b2', 'g3', 'b3')}
    del _L2_gnn_all

    def _L3_gnn_setup():
        import jax, jax.numpy as jnp
        import numpy as np
        B, N, D = (2, 2048, 128)
        key = jax.random.key(seed)
        ks = jax.random.split(key, 6)
        return {'hidden': jax.random.normal(ks[0], (B, N, D), dtype=jnp.float32), 'mask': jax.random.uniform(ks[1], (B, N, N), dtype=jnp.float32), 'W_w': jax.random.normal(ks[2], (D, D), dtype=jnp.float32) * 0.05, 'W_b': jax.random.normal(ks[3], (D,), dtype=jnp.float32) * 0.05, 'a_w': jax.random.normal(ks[4], (2 * D,), dtype=jnp.float32) * 0.05, 'a_b': jax.random.normal(ks[5], (1,), dtype=jnp.float32) * 0.05}
    _L3_gnn_all = _L3_gnn_setup()
    _L3_gnn_in = {k: v for k, v in _L3_gnn_all.items() if k in ('W_w', 'W_b', 'a_w', 'a_b')}
    del _L3_gnn_all
    return {'x': x, 'adj': adj, 'L0_gnn_eps': _L0_gnn_in['eps'], 'L0_gnn_W1': _L0_gnn_in['W1'], 'L0_gnn_b1': _L0_gnn_in['b1'], 'L0_gnn_W2': _L0_gnn_in['W2'], 'L0_gnn_b2': _L0_gnn_in['b2'], 'L1_gnn_w_se': _L1_gnn_in['w_se'], 'L1_gnn_b_se': _L1_gnn_in['b_se'], 'L1_gnn_conv1_w': _L1_gnn_in['conv1_w'], 'L1_gnn_bn1_g': _L1_gnn_in['bn1_g'], 'L1_gnn_bn1_b': _L1_gnn_in['bn1_b'], 'L1_gnn_bn1_m': _L1_gnn_in['bn1_m'], 'L1_gnn_bn1_v': _L1_gnn_in['bn1_v'], 'L1_gnn_conv2_w': _L1_gnn_in['conv2_w'], 'L1_gnn_bn2_g': _L1_gnn_in['bn2_g'], 'L1_gnn_bn2_b': _L1_gnn_in['bn2_b'], 'L1_gnn_bn2_m': _L1_gnn_in['bn2_m'], 'L1_gnn_bn2_v': _L1_gnn_in['bn2_v'], 'L1_gnn_w_msg': _L1_gnn_in['w_msg'], 'L1_gnn_b_msg': _L1_gnn_in['b_msg'], 'L1_gnn_w_ih': _L1_gnn_in['w_ih'], 'L1_gnn_b_ih': _L1_gnn_in['b_ih'], 'L1_gnn_w_hh': _L1_gnn_in['w_hh'], 'L1_gnn_b_hh': _L1_gnn_in['b_hh'], 'L2_gnn_W': _L2_gnn_in['W'], 'L2_gnn_a1': _L2_gnn_in['a1'], 'L2_gnn_a2': _L2_gnn_in['a2'], 'L2_gnn_g1': _L2_gnn_in['g1'], 'L2_gnn_b1': _L2_gnn_in['b1'], 'L2_gnn_g2': _L2_gnn_in['g2'], 'L2_gnn_b2': _L2_gnn_in['b2'], 'L2_gnn_g3': _L2_gnn_in['g3'], 'L2_gnn_b3': _L2_gnn_in['b3'], 'L3_gnn_W_w': _L3_gnn_in['W_w'], 'L3_gnn_W_b': _L3_gnn_in['W_b'], 'L3_gnn_a_w': _L3_gnn_in['a_w'], 'L3_gnn_a_b': _L3_gnn_in['a_b']}

def reference(x, adj, L0_gnn_eps, L0_gnn_W1, L0_gnn_b1, L0_gnn_W2, L0_gnn_b2, L1_gnn_w_se, L1_gnn_b_se, L1_gnn_conv1_w, L1_gnn_bn1_g, L1_gnn_bn1_b, L1_gnn_bn1_m, L1_gnn_bn1_v, L1_gnn_conv2_w, L1_gnn_bn2_g, L1_gnn_bn2_b, L1_gnn_bn2_m, L1_gnn_bn2_v, L1_gnn_w_msg, L1_gnn_b_msg, L1_gnn_w_ih, L1_gnn_b_ih, L1_gnn_w_hh, L1_gnn_b_hh, L2_gnn_W, L2_gnn_a1, L2_gnn_a2, L2_gnn_g1, L2_gnn_b1, L2_gnn_g2, L2_gnn_b2, L2_gnn_g3, L2_gnn_b3, L3_gnn_W_w, L3_gnn_W_b, L3_gnn_a_w, L3_gnn_a_b):
    import jax
    import jax.numpy as jnp

    def _L0_gnn_ref(x, adj, eps, W1, b1, W2, b2):
        import jax, jax.numpy as jnp
        import numpy as np
        D_IN = 128
        D_HID = 256
        aggregated = jnp.einsum('bnm,bmd->bnd', adj, x)
        h = (1.0 + eps) * x + aggregated
        h = jax.nn.relu(h @ W1 + b1)
        return h @ W2 + b2

    def _L1_gnn_ref(x, mask, w_se, b_se, conv1_w, bn1_g, bn1_b, bn1_m, bn1_v, conv2_w, bn2_g, bn2_b, bn2_m, bn2_v, w_msg, b_msg, w_ih, b_ih, w_hh, b_hh):
        import jax, jax.numpy as jnp
        import numpy as np
        from jax import lax
        DIM = 128
        EPS = 1e-05

        def _bn(h, g, b, m, v):
            scale = g / jnp.sqrt(v + EPS)
            return h * scale[None, :, None] + (b - m * scale)[None, :, None]

        def _conv1d(h, w, pad):
            return lax.conv_general_dilated(h, w, window_strides=(1,), padding=[(pad, pad)], dimension_numbers=('NCH', 'OIH', 'NCH'))
        d = x.shape[-1]
        xc = jnp.transpose(x, (0, 2, 1))
        h = _bn(_conv1d(xc, conv1_w, 0), bn1_g, bn1_b, bn1_m, bn1_v)
        h = jax.nn.relu(h)
        h = _bn(_conv1d(h, conv2_w, 8), bn2_g, bn2_b, bn2_m, bn2_v)
        x_conv = jnp.transpose(jax.nn.relu(h + xc), (0, 2, 1))
        s = x @ w_se.T + b_se
        sq = jnp.sum(s * s, axis=-1)
        dist = sq[:, :, None] + sq[:, None, :] - 2.0 * jnp.einsum('bnd,bmd->bnm', s, s)
        A = jnp.exp(-dist) * mask
        msg = jax.nn.relu(x @ w_msg.T + b_msg)
        x_nmp = jnp.einsum('bnm,bmd->bnd', A, msg)
        x_in = jnp.concatenate([x_conv, x_nmp], axis=-1)
        gi = x_in @ w_ih.T + b_ih
        gh = x @ w_hh.T + b_hh
        gi_r, gi_z, gi_n = (gi[..., :d], gi[..., d:2 * d], gi[..., 2 * d:])
        gh_r, gh_z, gh_n = (gh[..., :d], gh[..., d:2 * d], gh[..., 2 * d:])
        r = jax.nn.sigmoid(gi_r + gh_r)
        z = jax.nn.sigmoid(gi_z + gh_z)
        nn_ = jnp.tanh(gi_n + r * gh_n)
        return (1.0 - z) * nn_ + z * x

    def _L2_gnn_ref(h, adj, W, a1, a2, g1, b1, g2, b2, g3, b3):
        import jax, jax.numpy as jnp
        import numpy as np
        EPS = 1e-05
        ALPHA = 0.2

        def _bn(x, gamma, beta):
            red = tuple(range(x.ndim - 1))
            mean = jnp.mean(x, axis=red, keepdims=True)
            var = jnp.mean(jnp.square(x - mean), axis=red, keepdims=True)
            return (x - mean) * jax.lax.rsqrt(var + EPS) * gamma + beta
        Wh = jnp.einsum('bnf,of->bno', h, W)
        ei = Wh @ a1
        ej = Wh @ a2
        att = ei[:, :, None] + ej[:, None, :]
        att = _bn(att, g1, b1)
        att = jnp.where(att >= 0, att, ALPHA * att)
        att = _bn(att, g2, b2)
        att = jax.nn.softmax(att, axis=2)
        att = att * adj
        h_prime = jnp.einsum('bij,bjo->bio', att, Wh)
        h_prime = _bn(h_prime, g3, b3)
        return jax.nn.elu(h_prime)

    def _L3_gnn_ref(hidden, mask, W_w, W_b, a_w, a_b):
        import jax, jax.numpy as jnp
        import numpy as np
        B, N, D = (2, 2048, 128)
        h = jnp.einsum('bnd,ed->bne', hidden, W_w) + W_b
        Dh = h.shape[-1]
        a1, a2 = (a_w[:Dh], a_w[Dh:])
        e = h @ a1
        f = h @ a2
        logits = e[:, :, None] + f[:, None, :] + a_b[0]
        u = mask * jnp.exp(logits)
        a = u / jnp.sum(u, axis=2, keepdims=True)
        h_prime = jnp.einsum('bnm,bmd->bnd', a, h)
        return h_prime
    x = _layernorm(x + _L0_gnn_ref(x, adj, L0_gnn_eps, L0_gnn_W1, L0_gnn_b1, L0_gnn_W2, L0_gnn_b2), axis=-1)
    x = _layernorm(x + _L1_gnn_ref(x, adj, L1_gnn_w_se, L1_gnn_b_se, L1_gnn_conv1_w, L1_gnn_bn1_g, L1_gnn_bn1_b, L1_gnn_bn1_m, L1_gnn_bn1_v, L1_gnn_conv2_w, L1_gnn_bn2_g, L1_gnn_bn2_b, L1_gnn_bn2_m, L1_gnn_bn2_v, L1_gnn_w_msg, L1_gnn_b_msg, L1_gnn_w_ih, L1_gnn_b_ih, L1_gnn_w_hh, L1_gnn_b_hh), axis=-1)
    x = _layernorm(x + _L2_gnn_ref(x, adj, L2_gnn_W, L2_gnn_a1, L2_gnn_a2, L2_gnn_g1, L2_gnn_b1, L2_gnn_g2, L2_gnn_b2, L2_gnn_g3, L2_gnn_b3), axis=-1)
    x = _layernorm(x + _L3_gnn_ref(x, adj, L3_gnn_W_w, L3_gnn_W_b, L3_gnn_a_w, L3_gnn_a_b), axis=-1)
    return x

_drawn_inputs = setup_inputs


def setup_inputs(seed=0):
    import zlib

    import numpy as np

    out = dict(_drawn_inputs(seed))
    spreads = {'L1_gnn_b_se': (0.0, 0.8),
     'L1_gnn_bn1_g': (1.0, 0.6),
     'L1_gnn_bn1_b': (0.0, 0.413),
     'L1_gnn_bn1_m': (0.0, 0.367),
     'L1_gnn_bn1_v': (1.0, 0.6),
     'L1_gnn_bn2_g': (1.0, 0.599),
     'L1_gnn_bn2_b': (0.0, 0.719),
     'L1_gnn_bn2_m': (0.0, 0.543),
     'L1_gnn_bn2_v': (1.0, 0.6),
     'L1_gnn_b_msg': (0.0, 0.307),
     'L1_gnn_b_ih': (0.0, 0.272),
     'L1_gnn_b_hh': (0.0, 0.379),
     'L2_gnn_g1': (1.0, 0.6),
     'L2_gnn_b1': (0.0, 0.487),
     'L2_gnn_g2': (1.0, 0.2),
     'L2_gnn_b2': (0.0, 0.1),
     'L2_gnn_g3': (1.0, 0.2),
     'L2_gnn_b3': (0.0, 0.1)}
    factors = {'L0_gnn_b1': 2.859}
    for name, (base, spread) in spreads.items():
        noise = np.random.default_rng([zlib.crc32(name.encode()), seed]).standard_normal(out[name].shape)
        drawn = base * np.exp(spread * noise) if base else spread * noise
        out[name] = jnp.asarray(drawn.astype(out[name].dtype))
    for name, factor in factors.items():
        out[name] = (out[name] * factor).astype(out[name].dtype)
    return out
```

```python
from contextlib import ExitStack

import numpy as np
import concourse.bass as bass
from concourse import mybir

P = 128
ALU = mybir.AluOpType
ACT = mybir.ActivationFunctionType
AX = mybir.AxisListType
F32 = mybir.dt.float32
I32 = mybir.dt.int32

LN_EPS = 1e-5
SLOPE = 0.2
RSQRT_MAGIC = float(0x5F3759DF)
RSQRT_STEPS = 11
LN_STEPS = 4 + 1 + 4 + RSQRT_STEPS + 4

COLS = ["b1_0", "b1_1", "bn1_v", "bn2_v", "bn1_g", "bn2_g", "bn1_m", "bn2_m", "bn1_b", "bn2_b",
        "b_ih_r", "b_ih_z", "b_ih_n", "b_hh_r", "b_hh_z", "b_hh_n", "g3", "b3", "a1", "a2",
        "g1_0", "g1_1", "g1_2", "g1_3", "be1_0", "be1_1", "be1_2", "be1_3",
        "g2_0", "g2_1", "g2_2", "g2_3", "be2_0", "be2_1", "be2_2", "be2_3"]
CI = {n: i for i, n in enumerate(COLS)}
ROWS = ["b2", "b_msg", "W_b", "l3_a1", "l3_a2"]
RI = {n: i for i, n in enumerate(ROWS)}


class Steps:

    def __init__(self, eng, sem, b, per_batch):
        self.eng, self.sem, self.base, self.per, self.k = eng, sem, b * per_batch, per_batch, 0

    def did(self, ins):
        ins.then_inc(self.sem, 1)
        self.k += 1

    def wait(self):
        self.eng.wait_ge(self.sem, self.base + self.k)

    def end(self):
        assert self.k == self.per, (self.k, self.per)


def rsqrt(eng, st, v, y, tmp, var, eps):
    st.did(eng.tensor_scalar(v, var, eps, None, ALU.add))
    st.wait()
    st.did(eng.tensor_scalar(y.bitcast(I32), v.bitcast(I32), -0.5, RSQRT_MAGIC, ALU.mult, ALU.add))
    for _ in range(3):
        st.wait()
        st.did(eng.scalar_tensor_tensor(out=tmp, in0=y, scalar=-0.5, in1=y, op0=ALU.mult, op1=ALU.mult))
        st.wait()
        st.did(eng.tensor_tensor(tmp, tmp, v, ALU.mult))
        st.wait()
        st.did(eng.scalar_tensor_tensor(out=y, in0=tmp, scalar=1.5, in1=y, op0=ALU.add, op1=ALU.mult))
    st.wait()


def layer_norm(eng, st, dst, src, bn, mv, v, r, tmp):
    for c in range(4):
        st.did(eng.bn_stats(bn[:, c, :], src[:, c, :]))
    st.wait()
    st.did(eng.memset(tmp[:, 0:1], 0.0))
    for c in range(4):
        st.did(eng.bn_aggr(mv[:, c, :], bn[:, c, :]))
    st.wait()
    rsqrt(eng, st, v[:, :], r[:, :], tmp[:, :], mv[:, :, 1], LN_EPS)
    for c in range(4):
        st.did(eng.tensor_scalar(dst[:, c, :], src[:, c, :], mv[:, c, 0:1], r[:, c:c + 1],
                                 ALU.subtract, ALU.mult))


def build(nc, x_tok, x_fm, adj_t, w1, w2, cols, rows, scal, b_se, w_se, conv1, conv2, w_msg, w_ih, w_hh,
          l2_w, l2_wt, l3_wt, ident_in, out):
    B, N, D = x_tok.shape
    C = N // P
    TAPS = conv2.shape[1]
    PAD = TAPS // 2
    BN = B * N

    with ExitStack() as ctx:
        def sb(name, shape, dt=F32):
            return ctx.enter_context(nc.sbuf_tensor(name, shape, dt))

        def sem(name):
            return ctx.enter_context(nc.semaphore(name))

        x2_dram = nc.dram_tensor("x2_dram", (B, P, C * D), F32).ap()
        wh_dram = nc.dram_tensor("wh_dram", (B, P, C * D), F32).ap()
        hp_dram = nc.dram_tensor("hp_dram", (B, P, N), F32).ap()
        ei_dram = nc.dram_tensor("ei_dram", (B, 1, N), F32).ap()

        bank = [ctx.enter_context(nc.psum_tensor(f"bank{i}", [P, 512], F32)) for i in range(8)]

        def tok(t):
            return t[:, :].rearrange("p (c d) -> p c d", c=C)

        adj = sb("adj", [P, B, C, N])
        xk = sb("xk", [P, C, D])
        xT = sb("xT", [P, N])
        w1s = sb("w1s", [P, 2 * D])
        w2s = sb("w2s", [P, 2, D])
        col = sb("col", [P, len(COLS)])
        row = sb("row", [P, len(ROWS), D])
        sc = sb("sc", [P, 2])
        bse = sb("bse", [3, 1])
        wse = sb("wse", [P, 3])
        conv1s = sb("conv1s", [P, D])
        conv2s = sb("conv2s", [P, TAPS, D])
        wmsg = sb("wmsg", [P, D])
        wih = sb("wih", [P, 2, 3 * D])
        whh = sb("whh", [P, 3 * D])
        l2w = sb("l2w", [P, D])
        l2wt = sb("l2wt", [P, D])
        l3wt = sb("l3wt", [P, D])
        ident = sb("ident", [P, P])
        ones = sb("ones", [P, P])

        eps1 = sb("eps1", [P, 1])
        bnv = sb("bnv", [P, 2])
        bnr = sb("bnr", [P, 2])
        bnt = sb("bnt", [P, 2])
        bnsc = sb("bnsc", [P, 2])
        bnbi = sb("bnbi", [P, 2])
        half_b = sb("half_b", [P, 2])
        v12 = sb("v12", [P, 2])
        negsel = sb("negsel", [64, 1])

        h0T = sb("h0T", [P, N])
        hidT = sb("hidT", [P, 2, N])
        yk = sb("yk", [P, C, D])
        x1T = sb("x1T", [P, 2, N])
        c1T = sb("c1T", [P, N + 2 * PAD])
        SR = sb("SR", [64, N])
        SL = sb("SL", [64, N])
        nsq = sb("nsq", [P, C])
        zero = sb("zero", [P, 1])
        gate = sb("gate", [P, 1])
        msg = sb("msg", [P, C, D])
        AT = sb("AT", [P, C, N])
        xcT = sb("xcT", [P, N])
        xnT = sb("xnT", [P, N])
        trT = sb("trT", [P, N])
        tzT = sb("tzT", [P, N])
        ghT = sb("ghT", [P, N])
        nT = sb("nT", [P, N])
        vT = sb("vT", [P, N])
        x2k = sb("x2k", [P, C, D])
        x2T = sb("x2T", [P, N])
        whk = sb("whk", [P, C, D])
        E12 = sb("E12", [P, B, C, 2])
        bn = sb("bn", [P, C, 6])
        mv = sb("mv", [P, C, 2])
        lv = sb("lv", [P, C])
        lr = sb("lr", [P, C])
        lt = sb("lt", [P, C])

        ET = sb("ET", [B * C, P])
        e1 = sb("e1", [P, B * C])
        ejT = sb("ejT", [P, C, B])
        mb = sb("mb", [P, B])
        mtot = sb("mtot", [P, 1])
        e1c = sb("e1c", [P, B * C])
        vare = sb("vare", [P, 1])
        mbc = sb("mbc", [P, B])
        mj = sb("mj", [P, C])
        dj = sb("dj", [P, C, B])
        djq = sb("djq", [P, C, B])
        vj = sb("vj", [P, C])
        s1 = sb("s1", [P, C])
        t1 = sb("t1", [P, C, B])
        tt1 = sb("tt1", [P, B, C])
        st2 = c1T[:, 0:C * B * 6].rearrange("p (c b s) -> p c b s", c=C, b=B)
        mv2 = sb("mv2", [P, C, 2])
        c2 = sb("c2", [P, C])
        d2 = sb("d2", [P, C])
        st3 = sb("st3", [P, B, 6])
        mv3 = sb("mv3", [P, 2])
        a3 = sb("a3", [P, 4])
        nmax = sb("nmax", [P, C])
        rsum = sb("rsum", [P, C])
        rrec = sb("rrec", [P, C])

        ebc = [h0T, vT]
        LT = AT
        zT = conv2s[:, 0:C * C, :].rearrange("p (c k) d -> p c (k d)", c=C)
        PTs = [xcT, xnT, trT, tzT]
        hpT = nT

        s_w = sem("s_w")
        s_adj = sem("s_adj")
        s_x = sem("s_x")
        s_pre = sem("s_pre")
        s_prep = sem("s_prep")
        s_half = sem("s_half")
        s_agg = sem("s_agg")
        s_h0 = sem("s_h0")
        s_hid = sem("s_hid")
        s_hidr = sem("s_hidr")
        s_y = sem("s_y")
        s_xb = sem("s_xb")
        s_ysb = sem("s_ysb")
        s_ln1 = sem("s_ln1")
        s_x1t = sem("s_x1t")
        s_x1T = sem("s_x1T")
        s_s = sem("s_s")
        s_srow = sem("s_srow")
        s_slr = sem("s_slr")
        s_nsq = sem("s_nsq")
        s_nsqc = sem("s_nsqc")
        s_c1 = sem("s_c1")
        s_c1T = sem("s_c1T")
        s_msg = sem("s_msg")
        s_msgb = sem("s_msgb")
        s_msgr = sem("s_msgr")
        s_dist = sem("s_dist")
        s_exp = sem("s_exp")
        s_A = sem("s_A")
        s_cv = sem("s_cv")
        s_cvx = sem("s_cvx")
        s_xc = sem("s_xc")
        s_nmp = sem("s_nmp")
        s_xn = sem("s_xn")
        s_gate = sem("s_gate")
        s_gh = sem("s_gh")
        s_tr = sem("s_tr")
        s_tz = sem("s_tz")
        s_gru = sem("s_gru")
        s_n = sem("s_n")
        s_tv = sem("s_tv")
        s_ln2 = sem("s_ln2")
        s_x2t = sem("s_x2t")
        s_x2T = sem("s_x2T")
        s_wh = sem("s_wh")
        s_whk = sem("s_whk")
        s_e = sem("s_e")
        s_ec = sem("s_ec")
        s_x2st = sem("s_x2st")
        s_whst = sem("s_whst")

        DIST = [6, 7, 1, 2]
        STAT3 = 1 + RSQRT_STEPS + 4
        STAT1 = 22 + RSQRT_STEPS
        PB = [4, 5, 6, 4]
        PA = [yk[:].rearrange("p c d -> p (c d)"), x2k[:].rearrange("p c d -> p (c d)"), x1T[:, 0, :], x1T[:, 1, :]]

        block = ctx.enter_context(nc.Block())
        N_WLOAD = 18
        PRE_STEPS = 8 + 2 + RSQRT_STEPS + 4
        GATES = 4

        def iterations(eng, iteration):
            iteration(0, 0, True, False)
            with eng.Fori(0, (B - 2) // 2) as i:
                iteration(i * 2 + 1, 1, False, False)
                iteration(i * 2 + 2, 0, False, False)
            iteration(B - 1, 1, False, True)

        s_ET = sem("s_ET")
        s_ETc = sem("s_ETc")
        s_eist = sem("s_eist")
        s_mbp = sem("s_mbp")
        s_st = sem("s_st")
        s_vp = sem("s_vp")
        s_ebc = sem("s_ebc")
        s_lB = sem("s_lB")
        s_bB = sem("s_bB")
        s_mB = sem("s_mB")
        s_mC = sem("s_mC")
        s_st2 = sem("s_st2")
        s_ebcC = sem("s_ebcC")
        s_whl = sem("s_whl")
        s_lC = sem("s_lC")
        s_z = sem("s_z")
        s_zt = sem("s_zt")
        s_mx = sem("s_mx")
        s_ex = sem("s_ex")
        s_rr = sem("s_rr")
        s_pn = sem("s_pn")
        s_pt = sem("s_pt")
        s_pa = sem("s_pa")
        s_hp = sem("s_hp")
        s_hpe = sem("s_hpe")
        s_hps = sem("s_hps")
        s_hpst = sem("s_hpst")
        s_st3 = sem("s_st3")
        s_hl = sem("s_hl")
        s_x2l = sem("s_x2l")
        s_elu = sem("s_elu")
        s_el = sem("s_el")
        s_et = sem("s_et")
        s_y3 = sem("s_y3")
        s_ln3 = sem("s_ln3")
        s_x3t = sem("s_x3t")
        s_x3T = sem("s_x3T")
        s_h3 = sem("s_h3")
        s_hb = sem("s_hb")
        s_ef = sem("s_ef")
        s_efx = sem("s_efx")
        s_g = sem("s_g")
        s_num = sem("s_num")
        s_den = sem("s_den")
        s_numc = sem("s_numc")
        s_denc = sem("s_denc")
        s_nt = sem("s_nt")
        s_dt = sem("s_dt")
        s_wr = sem("s_wr")
        s_y4 = sem("s_y4")
        s_ln4 = sem("s_ln4")
        s_out = sem("s_out")
        s_on = sem("s_on")

        hT, x2l, elT, pT4, eT4, y3, x3k = xT, xk, hidT[:, 0, :], hidT[:, 1, :], zT[:, 0, :], yk, x2k
        x3T = x1T[:, 0, :]
        hB = msg
        gB = whk
        numT = x1T[:, 1, :]
        ftmp = AT[:, 2:4, :].rearrange("p k (c d) -> p k c d", c=C)
        fe = sb("fe", [P, 2, C])
        fx = sb("fx", [P, 2, C])
        fw = sb("fw", [P, 3, C])
        denr = SR
        y4 = AT[:, 1, :].rearrange("p (c d) -> p c d", c=C)
        outk = AT[:, 0, :].rearrange("p (c d) -> p c d", c=C)

        @block.sync
        def _(sp):
            for dst, src in ((w1s[:], w1), (w2s[:], w2.rearrange("(h p) d -> p h d", p=P)), (col[:], cols),
                             (bse[:], b_se), (wse[:], w_se), (conv1s[:], conv1), (conv2s[:], conv2),
                             (wmsg[:], w_msg), (wih[:], w_ih.rearrange("(q p) g -> p q g", p=P)),
                             (whh[:], w_hh), (l2w[:], l2_w), (l2wt[:], l2_wt), (l3wt[:], l3_wt),
                             (ident[:], ident_in),
                             (row[:, :, :], rows.rearrange("(a r) d -> a r d", a=1).broadcast_to((P, len(ROWS), D))),
                             (sc[:, :], scal.rearrange("(a r) -> a r", a=1).broadcast_to((P, 2)))):
                sp.dma_start(dst, src).then_inc(s_w, 16)

            def load_adj(b):
                sp.dma_start(adj[:, b], adj_t[b].rearrange("(c p) i -> p c i", p=P)).then_inc(s_adj, 16)

            def load_x(b):
                sp.dma_start(xk[:], x_tok[b].rearrange("(c p) d -> p c d", p=P)).then_inc(s_x, 16)
                sp.dma_start(xT[:], x_fm[b]).then_inc(s_x, 16)

            load_adj(0)
            load_x(0)
            sp.wait_ge(s_adj, 16)
            load_adj(1)

            def store_x2(b):
                sp.wait_ge(s_ln2, LN_STEPS * (b + 1))
                sp.dma_start(x2_dram[b], x2k[:].rearrange("p c d -> p (c d)")).then_inc(s_x2st, 16)

            def store_wh(b):
                sp.wait_ge(s_whk, b + 1)
                sp.dma_start(wh_dram[b], whk[:].rearrange("p c d -> p (c d)")).then_inc(s_whst, 16)

            def sp_iteration(t, p, first, last):
                if not last:
                    sp.wait_ge(s_ysb, t + 1)
                    load_x(t + 1)
                if not first:
                    if not last:
                        sp.wait_ge(s_adj, 16 * (t + 1))
                        load_adj(t + 1)
                    store_x2(t - 1)
                    store_wh(t - 1)

            iterations(sp, sp_iteration)
            store_x2(B - 1)
            store_wh(B - 1)

            sp.wait_ge(s_ETc, 1)
            sp.dma_start(ei_dram.rearrange("b a (c p) -> (b a c) p", p=P), ET[:]).then_inc(s_eist, 16)
            sp.wait_ge(s_eist, 16)
            sp.wait_ge(s_whst, 16 * B)
            sp.wait_ge(s_x2st, 16 * B)

            def load_ebc(b, p, s):
                sp.dma_start(ebc[p][:], ei_dram[b].broadcast_to((P, N))).then_inc(s, 16)

            load_ebc(0, 0, s_ebc)
            sp.wait_ge(s_ebc, 16)
            load_ebc(1, 1, s_ebc)
            with sp.Fori(0, (B - 2) // 2) as i:
                b = i * 2 + 2
                for p in range(2):
                    sp.wait_ge(s_lB, C * (b + p - 1))
                    sp.wait_ge(s_ebc, 16 * (b + p))
                    load_ebc(b + p, p, s_ebc)

            def load_C(b, p):
                load_ebc(b, p, s_ebcC)

            sp.wait_ge(s_lB, C * B)
            load_ebc(0, 0, s_ebcC)
            sp.dma_start(whk[:].rearrange("p c d -> p (c d)"), wh_dram[0]).then_inc(s_whl, 16)
            sp.wait_ge(s_ebcC, 16)
            load_ebc(1, 1, s_ebcC)

            def third(t, p, more):
                sp.wait_ge(s_hpe, t + 1)
                sp.dma_start(hp_dram[t], hpT[:]).then_inc(s_hpst, 16)
                if more > 0:
                    sp.dma_start(whk[:].rearrange("p c d -> p (c d)"), wh_dram[t + 1]).then_inc(s_whl, 16)
                if more > 1:
                    sp.wait_ge(s_lC, C * (t + 1))
                    sp.wait_ge(s_ebcC, 16 * (t + 2))
                    load_ebc(t + 2, p, s_ebcC)

            with sp.Fori(0, (B - 2) // 2) as i:
                third(i * 2, 0, 2)
                third(i * 2 + 1, 1, 2)
            third(B - 2, 0, 1)
            third(B - 1, 1, 0)

            sp.wait_ge(s_hpst, 16 * B)

            def fourth(t, first, last):
                if not last:
                    sp.wait_ge(s_elu, 3 * (t + 1))
                    sp.dma_start(hT[:], hp_dram[t + 1]).then_inc(s_hl, 16)
                    sp.wait_ge(s_y3, t + 1)
                    sp.dma_start(x2l[:].rearrange("p c d -> p (c d)"), x2_dram[t + 1]).then_inc(s_x2l, 16)
                sp.wait_ge(s_ln4, LN_STEPS * (t + 1))
                sp.dma_start(out[t].rearrange("(c p) d -> p c d", p=P), outk).then_inc(s_out, 16)

            sp.dma_start(hT[:], hp_dram[0]).then_inc(s_hl, 16)
            sp.dma_start(x2l[:].rearrange("p c d -> p (c d)"), x2_dram[0]).then_inc(s_x2l, 16)
            with sp.Fori(0, B - 1) as t:
                fourth(t, False, False)
            fourth(B - 1, False, True)
            sp.wait_ge(s_out, 16 * B)

        @block.gpsimd
        def _(pool):
            pool.wait_ge(s_w, 16 * 16)

            pool.wait_ge(s_pre, PRE_STEPS)

            def make_xb(b):
                pool.wait_ge(s_x, 32 * (b + 1))
                pool.wait_ge(s_agg, b + 1)
                pool.tensor_tensor(xk[:], xk[:], row[:, RI["b2"]:RI["b2"] + 1, :].broadcast_to((P, C, D)),
                                   ALU.add).then_inc(s_xb, 1)

            def relu_msg(b):
                pool.wait_ge(s_msgb, b + 1)
                pool.tensor_tensor(gate[:], zero[:], zero[:], ALU.add)
                pool.tensor_scalar(msg[:], msg[:], 0.0, None, ALU.max).then_inc(s_msgr, 1)

            def iteration(t, p, first, last):
                relu_msg(t)
                if not last:
                    make_xb(t + 1)

            make_xb(0)
            iterations(pool, iteration)

            pool.wait_ge(s_st2, 1)

            def third(t):
                for c in range(C):
                    pool.wait_ge(s_mC, C * t + c + 1)
                    if not isinstance(t, int):
                        pool.wait_ge(s_zt, C * t)
                    if c or not isinstance(t, int):
                        pool.wait_ge(s_z, C * t + c)
                    pool.tensor_tensor(gate[:], zero[:], zero[:], ALU.add)
                    pool.tensor_scalar(zT[:, c, :], LT[:, c, :], c2[:, c:c + 1], d2[:, c:c + 1],
                                       ALU.mult, ALU.add).then_inc(s_z, 1)

            third(0)
            with pool.Fori(1, B) as t:
                third(t)

        @block.scalar
        def _(act):
            act.wait_ge(s_w, 16 * 16)
            act.wait_ge(s_pre, PRE_STEPS)

            def hidden(b):
                for h in range(2):
                    act.wait_ge(s_hid, 2 * b + h + 1)
                    if not (isinstance(b, int) and b == 0):
                        act.wait_ge(s_y, b)
                    act.activation(hidT[:, h, :], bank[3 + h][:], ACT.Relu,
                                   bias=col[:, CI["b1_0"] + h:CI["b1_0"] + h + 1]).then_inc(s_hidr, 1)

            def x1_t(b, p, old):
                act.wait_ge(s_x1t, b + 1)
                if old:
                    act.wait_ge(s_gru, 6 * (b - 1))
                act.copy(x1T[:, p, :], bank[3][:]).then_inc(s_x1T, 1)

            def x2_t(b):
                act.wait_ge(s_x2t, b + 1)
                if not (isinstance(b, int) and b == 0):
                    act.wait_ge(s_e, b)
                act.copy(x2T[:], bank[5][:]).then_inc(s_x2T, 1)

            def iteration(t, p, first, last):
                act.wait_ge(s_s, t + 1)
                if not first:
                    act.wait_ge(s_dist, C * t)
                act.activation(SR[0:3, :], bank[1][0:3, :], ACT.Identity, bias=bse[:, 0:1]).then_inc(s_srow, 1)
                act.wait_ge(s_c1, t + 1)
                if not first:
                    act.wait_ge(s_cv, t)
                act.activation(c1T[:, PAD:PAD + N], bank[2][:], ACT.Relu, bias=bnbi[:, 0:1],
                               scale=bnsc[:, 0:1]).then_inc(s_c1T, 1)
                for c in range(C):
                    act.wait_ge(s_dist, C * t + c + 1)
                    act.wait_ge(s_nsqc, t + 1)
                    if not first:
                        act.wait_ge(s_nmp, t)
                    act.activation(AT[:, c, :], bank[DIST[c]][:], ACT.Exp, bias=nsq[:, c:c + 1]).then_inc(s_exp, 1)
                if not last:
                    hidden(t + 1)
                if not first:
                    x2_t(t - 1)
                act.wait_ge(s_cvx, t + 1)
                if not first:
                    act.wait_ge(s_gate, GATES * t)
                act.activation(xcT[:], xcT[:], ACT.Relu, bias=bnbi[:, 1:2]).then_inc(s_xc, 1)
                act.wait_ge(s_nmp, t + 1)
                act.copy(xnT[:], bank[2][:]).then_inc(s_xn, 1)
                if not last:
                    x1_t(t + 1, 1 - p, not first)
                act.wait_ge(s_gate, GATES * t + 1)
                act.activation(ghT[:], bank[7][:], ACT.Identity,
                               bias=col[:, CI["b_hh_n"]:CI["b_hh_n"] + 1]).then_inc(s_gh, 1)
                act.wait_ge(s_gate, GATES * t + 2)
                act.activation(trT[:], bank[4][:], ACT.Tanh, bias=half_b[:, 0:1], scale=0.5).then_inc(s_tr, 1)
                act.wait_ge(s_gate, GATES * t + 3)
                act.activation(tzT[:], bank[5][:], ACT.Tanh, bias=half_b[:, 1:2], scale=0.5).then_inc(s_tz, 1)
                act.wait_ge(s_gru, 6 * t + 2)
                act.activation(nT[:], nT[:], ACT.Tanh,
                               bias=col[:, CI["b_ih_n"]:CI["b_ih_n"] + 1]).then_inc(s_n, 1)

            hidden(0)
            x1_t(0, 0, False)
            iterations(act, iteration)
            x2_t(B - 1)

            act.wait_ge(s_ET, 1)
            act.copy(ET[:], bank[0][0:B * C, 0:P]).then_inc(s_ETc, 1)

            def normed(b, p, c, s):
                act.activation(LT[:, c, :], ebc[p][:], ACT.Identity, bias=tt1[:, b, c:c + 1],
                               scale=s1[:, c:c + 1]).then_inc(s, 1)

            act.wait_ge(s_st, STAT1)
            def stats_tiles(b, p, first):
                act.wait_ge(s_ebc, 16 * (b + 1))
                for c in range(C):
                    if not first:
                        act.wait_ge(s_bB, C * (b - 1) + c + 1)
                    normed(b, p, c, s_lB)

            stats_tiles(0, 0, True)
            stats_tiles(1, 1, False)
            with act.Fori(0, (B - 2) // 2) as i:
                stats_tiles(i * 2 + 2, 0, False)
                stats_tiles(i * 2 + 3, 1, False)

            def normed_all(b, p):
                act.wait_ge(s_ebcC, 16 * (b + 1))
                for c in range(C):
                    if not (isinstance(b, int) and b == 0):
                        act.wait_ge(s_z, C * (b - 1) + c + 1)
                    normed(b, p, c, s_lC)

            def third(t, p, last):
                if not last:
                    normed_all(t + 1, 1 - p)
                for c in range(C):
                    act.wait_ge(s_mx, C * t + c + 1)
                    if not (isinstance(t, int) and t == 0):
                        act.wait_ge(s_pt, C * t)
                    act.activation(PTs[c][:], bank[c][:], ACT.Exp, bias=nmax[:, c:c + 1],
                                   accum_out=rsum[:, c:c + 1]).then_inc(s_ex, 1)
                act.wait_ge(s_hp, t + 1)
                if not (isinstance(t, int) and t == 0):
                    act.wait_ge(s_hpst, 16 * t)
                act.copy(hpT[:], bank[7][:]).then_inc(s_hpe, 1)

            act.wait_ge(s_bB, C * B)
            normed_all(0, 0)
            third(0, 0, False)
            with act.Fori(0, (B - 2) // 2) as i:
                third(i * 2 + 1, 1, False)
                third(i * 2 + 2, 0, False)
            third(B - 1, 1, True)

            act.wait_ge(s_st3, STAT3)

            def fourth(t, first):
                act.wait_ge(s_hl, 16 * (t + 1))
                if not first:
                    act.wait_ge(s_el, t)
                act.activation(pT4, hT[:], ACT.Relu, bias=a3[:, 1:2], scale=a3[:, 0:1]).then_inc(s_elu, 1)
                act.activation(eT4, hT[:], ACT.Relu, bias=a3[:, 3:4], scale=a3[:, 2:3]).then_inc(s_elu, 1)
                act.wait_ge(s_elu, 3 * t + 2)
                act.activation(eT4, eT4, ACT.Exp, scale=-1.0).then_inc(s_elu, 1)
                act.wait_ge(s_x3t, t + 1)
                if not first:
                    act.wait_ge(s_h3, t)
                act.copy(x3T, bank[1][:]).then_inc(s_x3T, 1)
                act.wait_ge(s_ef, 2 * C * (t + 1))
                act.activation(fx[:, 0, :], fe[:, 0, :], ACT.Exp, bias=sc[:, 1:2]).then_inc(s_efx, 1)
                act.activation(fx[:, 1, :], fe[:, 1, :], ACT.Exp).then_inc(s_efx, 1)
                act.wait_ge(s_num, t + 1)
                if not first:
                    act.wait_ge(s_nt, t)
                act.copy(numT, bank[3][:]).then_inc(s_numc, 1)
                act.wait_ge(s_den, t + 1)
                if not first:
                    act.wait_ge(s_dt, t)
                act.copy(denr[0:1, :], bank[4][0:1, :]).then_inc(s_denc, 1)

            fourth(0, True)
            with act.Fori(1, B) as t:
                fourth(t, False)

        @block.vector
        def _(dve):
            pre = Steps(dve, s_pre, 0, PRE_STEPS)
            pre.did(dve.memset(ones[:], 1.0))
            pre.did(dve.memset(zero[:], 0.0))
            pre.did(dve.memset(SL[:], 0.0))
            pre.did(dve.memset(SR[:], 0.0))
            pre.did(dve.memset(c1T[:], 0.0))
            pre.did(dve.memset(negsel[:], 0.0))
            pre.wait()
            pre.did(dve.memset(SL[32:35, :], -1.0))
            pre.did(dve.memset(negsel[32:35, :], -1.0))
            dve.wait_ge(s_w, 16 * 16)
            pre.did(dve.tensor_scalar(eps1[:], sc[:, 0:1], 1.0, None, ALU.add))
            pre.did(dve.tensor_tensor(half_b[:], col[:, CI["b_ih_r"]:CI["b_ih_r"] + 2],
                                      col[:, CI["b_hh_r"]:CI["b_hh_r"] + 2], ALU.add))
            rsqrt(dve, pre, bnv[:], bnr[:], bnt[:], col[:, CI["bn1_v"]:CI["bn1_v"] + 2], LN_EPS)
            pre.did(dve.tensor_tensor(bnsc[:], bnr[:], col[:, CI["bn1_g"]:CI["bn1_g"] + 2], ALU.mult))
            pre.wait()
            pre.did(dve.tensor_tensor(bnt[:], bnsc[:], col[:, CI["bn1_m"]:CI["bn1_m"] + 2], ALU.mult))
            pre.wait()
            dve.wait_ge(s_prep, 1)
            dve.tensor_copy(v12[:], bank[7][:, 0:2]).then_inc(s_half, 1)
            pre.did(dve.tensor_tensor(bnbi[:], col[:, CI["bn1_b"]:CI["bn1_b"] + 2], bnt[:], ALU.subtract))
            pre.did(dve.tensor_scalar(half_b[:], half_b[:], 0.5, None, ALU.mult))
            pre.end()

            def make_h0(b):
                dve.wait_ge(s_agg, b + 1)
                dve.wait_ge(s_x, 32 * (b + 1))
                if not (isinstance(b, int) and b == 0):
                    dve.wait_ge(s_hid, 2 * b)
                dve.scalar_tensor_tensor(out=h0T[:], in0=xT[:], scalar=eps1[:, 0:1], in1=bank[4][:],
                                         op0=ALU.mult, op1=ALU.add).then_inc(s_h0, 1)

            def make_x1(b):
                dve.wait_ge(s_y, b + 1)
                dve.wait_ge(s_xb, b + 1)
                if not (isinstance(b, int) and b == 0):
                    dve.wait_ge(s_x1t, b)
                dve.tensor_tensor(yk[:], tok(bank[6]), xk[:], ALU.add).then_inc(s_ysb, 1)
                dve.wait_ge(s_ysb, b + 1)
                st = Steps(dve, s_ln1, b, LN_STEPS)
                layer_norm(dve, st, yk, yk, bn, mv, lv, lr, lt)
                st.end()

            def make_x2(b):
                dve.wait_ge(s_tv, b + 1)
                if not (isinstance(b, int) and b == 0):
                    dve.wait_ge(s_x2st, 16 * b)
                    dve.wait_ge(s_x2t, b)
                st = Steps(dve, s_ln2, b, LN_STEPS)
                layer_norm(dve, st, x2k, tok(bank[5]), bn, mv, lv, lr, lt)
                st.end()

            def keep_wh(b):
                dve.wait_ge(s_wh, b + 1)
                if not (isinstance(b, int) and b == 0):
                    dve.wait_ge(s_whst, 16 * b)
                dve.tensor_copy(whk[:], tok(bank[7])).then_inc(s_whk, 1)
                dve.wait_ge(s_e, b + 1)
                dve.tensor_copy(E12[:, b], bank[1][:, 0:2 * C].rearrange("p (c k) -> p c k", c=C)).then_inc(s_ec, 1)

            def iteration(t, p, first, last):
                dve.wait_ge(s_srow, t + 1)
                dve.tensor_scalar(SL[0:3, :], SR[0:3, :], 2.0, None, ALU.mult).then_inc(s_slr, 1)
                dve.tensor_tensor(SR[32:35, :], SR[0:3, :], SR[0:3, :], ALU.mult).then_inc(s_slr, 1)
                dve.wait_ge(s_msg, t + 1)
                if not first:
                    dve.wait_ge(s_nmp, t)
                dve.tensor_tensor(msg[:], tok(bank[3]), row[:, RI["b_msg"]:RI["b_msg"] + 1, :].broadcast_to((P, C, D)),
                                  ALU.add).then_inc(s_msgb, 1)
                if not last:
                    make_h0(t + 1)
                dve.wait_ge(s_nsq, t + 1)
                if not first:
                    dve.wait_ge(s_exp, C * t)
                dve.tensor_copy(nsq[:], bank[0][:, 0:C]).then_inc(s_nsqc, 1)
                if not first:
                    make_x2(t - 1)
                for c in range(C):
                    dve.wait_ge(s_exp, C * t + c + 1)
                    dve.wait_ge(s_adj, 16 * (t + 1))
                    dve.tensor_tensor(AT[:, c, :], AT[:, c, :], adj[:, t, c, :], ALU.mult).then_inc(s_A, 1)
                if not last:
                    make_x1(t + 1)
                if not first:
                    keep_wh(t - 1)
                dve.wait_ge(s_cv, t + 1)
                if not first:
                    dve.wait_ge(s_gate, GATES * t)
                dve.scalar_tensor_tensor(out=xcT[:], in0=bank[0][:], scalar=bnsc[:, 1:2], in1=x1T[:, p, :],
                                         op0=ALU.mult, op1=ALU.add).then_inc(s_cvx, 1)
                st = Steps(dve, s_gru, t, 6)
                dve.wait_ge(s_gh, t + 1)
                dve.wait_ge(s_tr, t + 1)
                st.did(dve.scalar_tensor_tensor(out=nT[:], in0=trT[:], scalar=1.0, in1=ghT[:],
                                                op0=ALU.add, op1=ALU.mult))
                st.wait()
                dve.wait_ge(s_gate, GATES * (t + 1))
                st.did(dve.scalar_tensor_tensor(out=nT[:], in0=nT[:], scalar=0.5, in1=bank[6][:],
                                                op0=ALU.mult, op1=ALU.add))
                dve.wait_ge(s_n, t + 1)
                st.did(dve.tensor_tensor(ghT[:], x1T[:, p, :], nT[:], ALU.subtract))
                st.wait()
                dve.wait_ge(s_tz, t + 1)
                st.did(dve.scalar_tensor_tensor(out=ghT[:], in0=tzT[:], scalar=1.0, in1=ghT[:],
                                                op0=ALU.add, op1=ALU.mult))
                st.did(dve.tensor_tensor(nT[:], x1T[:, p, :], nT[:], ALU.add))
                st.wait()
                if not first:
                    dve.wait_ge(s_tv, t)
                st.did(dve.scalar_tensor_tensor(out=vT[:], in0=ghT[:], scalar=0.5, in1=nT[:],
                                                op0=ALU.mult, op1=ALU.add))
                st.end()

            make_h0(0)
            make_x1(0)
            iterations(dve, iteration)
            make_x2(B - 1)
            keep_wh(B - 1)

            st = Steps(dve, s_st, 0, STAT1)
            dve.wait_ge(s_ec, B)
            st.did(dve.tensor_copy(e1[:], E12[:, :, :, 0].rearrange("p b c -> p (b c)")))
            st.did(dve.tensor_copy(ejT[:], E12[:, :, :, 1].rearrange("p b c -> p c b")))
            st.wait()
            dve.wait_ge(s_mbp, 1)
            st.did(dve.tensor_reduce(mb[:], bank[1][:, 0:B * C].rearrange("p (b c) -> p b c", c=C), AX.X, ALU.add))
            st.wait()
            st.did(dve.tensor_scalar(mb[:], mb[:], 1.0 / N, None, ALU.mult))
            st.wait()
            st.did(dve.tensor_reduce(mtot[:], mb[:], AX.X, ALU.add))
            st.wait()
            st.did(dve.tensor_scalar(mtot[:], mtot[:], 1.0 / B, None, ALU.mult))
            st.wait()
            st.did(dve.tensor_scalar(e1c[:], e1[:], mtot[:, 0:1], None, ALU.subtract))
            st.did(dve.tensor_scalar(mbc[:], mb[:], mtot[:, 0:1], None, ALU.subtract))
            st.wait()
            st.did(dve.tensor_tensor(e1c[:], e1c[:], e1c[:], ALU.mult))
            st.did(dve.tensor_reduce(mj[:], ejT[:], AX.X, ALU.add))
            st.wait()
            st.did(dve.tensor_scalar(mj[:], mj[:], 1.0 / B, None, ALU.mult))
            st.wait()
            st.did(dve.tensor_tensor(dj[:], ejT[:], mj[:].rearrange("p (c a) -> p c a", a=1).broadcast_to((P, C, B)),
                                     ALU.subtract))
            st.wait()
            st.did(dve.scalar_tensor_tensor(out=djq[:], in0=mbc[:].rearrange("p (a b) -> p a b", a=1).broadcast_to((P, C, B)),
                                            scalar=2.0, in1=dj[:], op0=ALU.mult, op1=ALU.add))
            st.wait()
            st.did(dve.tensor_tensor(djq[:], djq[:], dj[:], ALU.mult))
            dve.wait_ge(s_vp, 1)
            st.did(dve.tensor_reduce(vare[:], bank[2][:, 0:B * C], AX.X, ALU.add))
            st.wait()
            st.did(dve.tensor_reduce(vj[:], djq[:], AX.X, ALU.add))
            st.did(dve.tensor_scalar(vare[:], vare[:], 1.0 / BN, None, ALU.mult))
            st.wait()
            st.did(dve.tensor_scalar(vj[:], vj[:], 1.0 / B, vare[:, 0:1], ALU.mult, ALU.add))
            st.wait()
            rsqrt(dve, st, lv[:], lr[:], lt[:], vj[:], LN_EPS)
            st.did(dve.tensor_tensor(s1[:], lr[:], col[:, CI["g1_0"]:CI["g1_0"] + C], ALU.mult))
            st.did(dve.tensor_scalar(t1[:], dj[:], mtot[:, 0:1], None, ALU.subtract))
            st.wait()
            st.did(dve.tensor_tensor(t1[:], t1[:], s1[:].rearrange("p (c a) -> p c a", a=1).broadcast_to((P, C, B)),
                                     ALU.mult))
            st.wait()
            st.did(dve.tensor_tensor(tt1[:], t1[:].rearrange("p c b -> p b c"),
                                     col[:, CI["be1_0"]:CI["be1_0"] + C].rearrange("p (a c) -> p a c", a=1)
                                     .broadcast_to((P, B, C)), ALU.add))
            st.end()

            def leaky(b, c, made, done):
                dve.wait_ge(made, C * b + c + 1)
                dve.scalar_tensor_tensor(out=LT[:, c, :], in0=LT[:, c, :], scalar=SLOPE, in1=LT[:, c, :],
                                         op0=ALU.mult, op1=ALU.max).then_inc(done, 1)

            with dve.Fori(0, B) as b:
                for c in range(C):
                    leaky(b, c, s_lB, s_mB)
                    dve.wait_ge(s_mB, C * b + c + 1)
                    dve.bn_stats(st2[:, c, b, :], LT[:, c, :]).then_inc(s_bB, 1)
            dve.wait_ge(s_bB, C * B)
            s2 = Steps(dve, s_on, 0, C + RSQRT_STEPS + 2)
            for c in range(C):
                s2.did(dve.bn_aggr(mv2[:, c, :], st2[:, c, :, :].rearrange("p b s -> p (b s)")))
            s2.wait()
            rsqrt(dve, s2, lv[:], lr[:], lt[:], mv2[:, :, 1], LN_EPS)
            s2.did(dve.tensor_tensor(c2[:], lr[:], col[:, CI["g2_0"]:CI["g2_0"] + C], ALU.mult))
            s2.wait()
            s2.did(dve.tensor_tensor(d2[:], c2[:], mv2[:, :, 0], ALU.mult))
            s2.wait()
            dve.tensor_tensor(d2[:], col[:, CI["be2_0"]:CI["be2_0"] + C], d2[:], ALU.subtract).then_inc(s_st2, 1)
            s2.end()

            def third_max(t, first):
                for c in range(C):
                    dve.wait_ge(s_zt, C * t + c + 1)
                    if not first:
                        dve.wait_ge(s_ex, C * t)
                    dve.tensor_reduce(nmax[:, c:c + 1], bank[c][:], AX.X, ALU.max, negate=True).then_inc(s_mx, 1)

            def third_rest(t):
                for c in range(C):
                    dve.wait_ge(s_ex, C * t + c + 1)
                    dve.reciprocal(rrec[:, c:c + 1], rsum[:, c:c + 1]).then_inc(s_rr, 1)
                    dve.wait_ge(s_rr, C * t + c + 1)
                    dve.tensor_scalar(PTs[c][:], PTs[c][:], rrec[:, c:c + 1], None, ALU.mult).then_inc(s_pn, 1)
                for c in range(C):
                    dve.wait_ge(s_pt, C * t + c + 1)
                    dve.tensor_tensor(PA[c], bank[PB[c]][:], adj[:, t, c, :], ALU.mult).then_inc(s_pa, 1)
                dve.wait_ge(s_hp, t + 1)
                dve.wait_ge(s_hpe, t + 1)
                dve.bn_stats(st3[:, t, :], hpT[:]).then_inc(s_hps, 1)

            def third_leaky(t):
                for c in range(C):
                    leaky(t, c, s_lC, s_mC)

            third_leaky(0)
            third_max(0, True)
            third_leaky(1)
            third_rest(0)
            with dve.Fori(1, B - 1) as t:
                third_max(t, False)
                third_leaky(t + 1)
                third_rest(t)
            third_max(B - 1, False)
            third_rest(B - 1)

            s3 = Steps(dve, s_st3, 0, STAT3)
            dve.wait_ge(s_hps, B)
            s3.did(dve.bn_aggr(mv3[:], st3[:, :, :].rearrange("p b s -> p (b s)")))
            s3.wait()
            rsqrt(dve, s3, lv[:, 0:1], lr[:, 0:1], lt[:, 0:1], mv3[:, 1:2], LN_EPS)
            s3.did(dve.tensor_tensor(a3[:, 0:1], lr[:, 0:1], col[:, CI["g3"]:CI["g3"] + 1], ALU.mult))
            s3.wait()
            s3.did(dve.tensor_tensor(lt[:, 0:1], a3[:, 0:1], mv3[:, 0:1], ALU.mult))
            s3.wait()
            s3.did(dve.tensor_tensor(a3[:, 1:2], col[:, CI["b3"]:CI["b3"] + 1], lt[:, 0:1], ALU.subtract))
            s3.wait()
            s3.did(dve.tensor_scalar(a3[:, 2:4], a3[:, 0:2], -1.0, None, ALU.mult))
            s3.end()

            def fourth(t, first):
                dve.wait_ge(s_elu, 3 * (t + 1))
                if not first:
                    dve.wait_ge(s_et, t)
                dve.scalar_tensor_tensor(out=elT, in0=eT4, scalar=-1.0, in1=pT4, op0=ALU.add,
                                         op1=ALU.add).then_inc(s_el, 1)
                dve.wait_ge(s_et, t + 1)
                dve.wait_ge(s_x2l, 16 * (t + 1))
                dve.tensor_tensor(y3[:], tok(bank[0]), x2l[:], ALU.add).then_inc(s_y3, 1)
                dve.wait_ge(s_y3, t + 1)
                st = Steps(dve, s_ln3, t, LN_STEPS)
                layer_norm(dve, st, x3k, y3, bn, mv, lv, lr, lt)
                st.end()
                dve.wait_ge(s_h3, t + 1)
                dve.tensor_tensor(hB[:], tok(bank[2]), row[:, RI["W_b"]:RI["W_b"] + 1, :].broadcast_to((P, C, D)),
                                  ALU.add).then_inc(s_hb, 1)
                dve.wait_ge(s_hb, t + 1)
                for k in range(2):
                    for c in range(C):
                        dve.scalar_tensor_tensor(out=ftmp[:, k, c, :], in0=hB[:, c, :], scalar=1.0,
                                                 in1=row[:, RI["l3_a1"] + k, :], op0=ALU.mult, op1=ALU.mult,
                                                 accum_out=fe[:, k, c:c + 1]).then_inc(s_ef, 1)
                dve.wait_ge(s_efx, 2 * (t + 1))
                for c in range(C):
                    dve.tensor_scalar(gB[:, c, :], hB[:, c, :], fx[:, 1, c:c + 1], None, ALU.mult).then_inc(s_g, 1)
                dve.wait_ge(s_dt, t + 1)
                dve.tensor_tensor(fw[:, 0, :], bank[6][:, 0:C], fx[:, 0, :], ALU.mult).then_inc(s_wr, 1)
                dve.wait_ge(s_wr, 3 * t + 1)
                dve.reciprocal(fw[:, 1, :], fw[:, 0, :]).then_inc(s_wr, 1)
                dve.wait_ge(s_wr, 3 * t + 2)
                dve.tensor_tensor(fw[:, 2, :], fw[:, 1, :], fx[:, 0, :], ALU.mult).then_inc(s_wr, 1)
                dve.wait_ge(s_wr, 3 * t + 3)
                dve.wait_ge(s_nt, t + 1)
                for c in range(C):
                    dve.scalar_tensor_tensor(out=y4[:, c, :], in0=tok(bank[5])[:, c, :], scalar=fw[:, 2, c:c + 1],
                                             in1=x3k[:, c, :], op0=ALU.mult, op1=ALU.add).then_inc(s_y4, 1)
                dve.wait_ge(s_y4, C * (t + 1))
                if not first:
                    dve.wait_ge(s_out, 16 * t)
                st = Steps(dve, s_ln4, t, LN_STEPS)
                layer_norm(dve, st, outk, y4, bn, mv, lv, lr, lt)
                st.end()

            fourth(0, True)
            with dve.Fori(1, B) as t:
                fourth(t, False)

        @block.tensor
        def _(pe):
            def mm(out_, w, x, start, stop):
                return pe.matmul(out_, w, x, start=start, stop=stop)

            def turn4(dst, src):
                for c in range(C):
                    ins = pe.transpose(dst[:, c * P:(c + 1) * P], src[:, c * P:(c + 1) * P], ident[:])
                return ins

            def flat(t):
                return t[:].rearrange("p c d -> p (c d)")

            pe.wait_ge(s_w, 16 * 16)
            pe.wait_ge(s_pre, 3)
            mm(bank[7][:, 0:2], l2w[:], col[:, CI["a1"]:CI["a1"] + 2], True, True).then_inc(s_prep, 1)
            pe.wait_ge(s_pre, PRE_STEPS)
            pe.wait_ge(s_half, 1)

            def aggregate(b):
                pe.wait_ge(s_adj, 16 * (b + 1))
                pe.wait_ge(s_x, 32 * (b + 1))
                for c in range(C):
                    ins = mm(bank[4][:], xk[:, c, :], adj[:, b, c, :], c == 0, c == C - 1)
                ins.then_inc(s_agg, 1)

            def hid(b):
                pe.wait_ge(s_h0, b + 1)
                if not (isinstance(b, int) and b == 0):
                    pe.wait_ge(s_msgb, b)
                for h in range(2):
                    mm(bank[3 + h][:], w1s[:, h * D:(h + 1) * D], h0T[:], True, True).then_inc(s_hid, 1)

            def y_rows(b):
                pe.wait_ge(s_hidr, 2 * (b + 1))
                if not (isinstance(b, int) and b == 0):
                    pe.wait_ge(s_exp, C * (b - 1) + 1)
                for c in range(C):
                    for h in range(2):
                        ins = mm(bank[6][:, c * D:(c + 1) * D], hidT[:, h, c * P:(c + 1) * P], w2s[:, h, :],
                                 h == 0, h == 1)
                ins.then_inc(s_y, 1)

            def turn_x1(b):
                pe.wait_ge(s_ln1, LN_STEPS * (b + 1))
                turn4(bank[3], flat(yk)).then_inc(s_x1t, 1)

            def turn_v(b):
                pe.wait_ge(s_gru, 6 * (b + 1))
                turn4(bank[5], vT).then_inc(s_tv, 1)

            def turn_x2(b):
                pe.wait_ge(s_ln2, LN_STEPS * (b + 1))
                turn4(bank[5], flat(x2k)).then_inc(s_x2t, 1)

            def third_in(b):
                pe.wait_ge(s_x2T, b + 1)
                if isinstance(b, int) and b == B - 1:
                    pe.wait_ge(s_gh, B)
                else:
                    pe.wait_ge(s_exp, C * (b + 1) + 3)
                for c in range(C):
                    ins = mm(bank[7][:, c * D:(c + 1) * D], x2T[:, c * P:(c + 1) * P], l2wt[:], True, True)
                ins.then_inc(s_wh, 1)
                for c in range(C):
                    ins = mm(bank[1][:, 2 * c:2 * c + 2], x2T[:, c * P:(c + 1) * P], v12[:], True, True)
                ins.then_inc(s_e, 1)

            def iteration(t, p, first, last):
                xT1 = x1T[:, p, :]
                pe.wait_ge(s_x1T, t + 1)
                mm(bank[1][0:3, :], wse[:], xT1, True, True).then_inc(s_s, 1)
                if not first:
                    pe.wait_ge(s_xn, t)
                mm(bank[2][:], conv1s[:], xT1, True, True).then_inc(s_c1, 1)
                for c in range(C):
                    ins = mm(bank[3][:, c * D:(c + 1) * D], xT1[:, c * P:(c + 1) * P], wmsg[:], True, True)
                ins.then_inc(s_msg, 1)
                if not last:
                    if not first:
                        pe.wait_ge(s_tr, t)
                    aggregate(t + 1)
                pe.wait_ge(s_slr, 2 * (t + 1))
                if not first:
                    pe.wait_ge(s_cvx, t)
                for c in range(C):
                    ins = mm(bank[0][:, c:c + 1], SR[:, c * P:(c + 1) * P], negsel[:], True, True)
                ins.then_inc(s_nsq, 1)
                if not first:
                    turn_v(t - 1)
                    pe.wait_ge(s_gru, 6 * t)
                    pe.wait_ge(s_gh, t)
                for c in range(C):
                    if c == 2:
                        pe.wait_ge(s_srow, t + 1)
                    if c == 3:
                        pe.wait_ge(s_c1T, t + 1)
                    mm(bank[DIST[c]][:], SL[:, c * P:(c + 1) * P], SR[:], True, True).then_inc(s_dist, 1)
                if not last:
                    hid(t + 1)
                pe.wait_ge(s_c1T, t + 1)
                pe.wait_ge(s_nsqc, t + 1)

                def conv(k0, k1):
                    for k in range(k0, k1):
                        ins = mm(bank[0][:], conv2s[:, k, :], c1T[:, k:k + N], k == 0, k == TAPS - 1)
                    return ins

                conv(0, 9)
                if not first:
                    turn_x2(t - 1)
                if not last:
                    y_rows(t + 1)
                conv(9, TAPS).then_inc(s_cv, 1)
                if not first:
                    third_in(t - 1)
                pe.wait_ge(s_A, C * (t + 1))
                pe.wait_ge(s_msgr, t + 1)
                for c in range(C):
                    ins = mm(bank[2][:], msg[:, c, :], AT[:, c, :], c == 0, c == C - 1)
                ins.then_inc(s_nmp, 1)
                if not last:
                    turn_x1(t + 1)
                if not first:
                    pe.wait_ge(s_whk, t)
                    pe.wait_ge(s_x2T, t)
                else:
                    pe.wait_ge(s_exp, C)
                mm(bank[7][:], whh[:, 2 * D:3 * D], xT1, True, True).then_inc(s_gate, 1)
                pe.wait_ge(s_xc, t + 1)
                pe.wait_ge(s_xn, t + 1)
                if not last:
                    pe.wait_ge(s_hidr, 2 * (t + 2))
                    pe.wait_ge(s_ysb, t + 2)
                for g in range(3):
                    o = bank[4 + g][:]
                    gs = slice(g * D, (g + 1) * D)
                    if g < 2:
                        mm(o, whh[:, gs], xT1, True, False)
                    mm(o, wih[:, 0, gs], xcT[:], g == 2, False)
                    mm(o, wih[:, 1, gs], xnT[:], False, True).then_inc(s_gate, 1)

            aggregate(0)
            hid(0)
            y_rows(0)
            turn_x1(0)
            iterations(pe, iteration)
            turn_v(B - 1)
            turn_x2(B - 1)
            third_in(B - 1)

            pe.wait_ge(s_st, 2)
            mm(bank[1][:, 0:B * C], ones[:], e1[:], True, True).then_inc(s_mbp, 1)
            pe.transpose(bank[0][0:B * C, 0:P], e1[:], ident[:]).then_inc(s_ET, 1)
            pe.wait_ge(s_st, 9)
            mm(bank[2][:, 0:B * C], ones[:], e1c[:], True, True).then_inc(s_vp, 1)

            def third_turn(t, first):
                for c in range(C):
                    if not first:
                        pe.wait_ge(s_ex, C * (t - 1) + c + 1)
                    pe.wait_ge(s_z, C * (t + 1))
                    for k in range(C):
                        ins = pe.transpose(bank[c][:, k * P:(k + 1) * P], zT[:, k, c * P:(c + 1) * P], ident[:])
                    ins.then_inc(s_zt, 1)

            def third_product(t, first):
                pe.wait_ge(s_pn, C * (t + 1))
                for c in range(C):
                    if c == 3:
                        pe.wait_ge(s_pa, C * t + 1)
                    elif not first:
                        pe.wait_ge(s_pa, C * t)
                    for k in range(C):
                        ins = pe.transpose(bank[PB[c]][:, k * P:(k + 1) * P], PTs[k][:, c * P:(c + 1) * P], ident[:])
                    ins.then_inc(s_pt, 1)
                pe.wait_ge(s_whl, 16 * (t + 1))
                if not first:
                    pe.wait_ge(s_hpe, t)
                for c in range(C):
                    pe.wait_ge(s_pa, C * t + c + 1)
                    ins = mm(bank[7][:], whk[:, c, :], PA[c], c == 0, c == C - 1)
                ins.then_inc(s_hp, 1)

            third_turn(0, True)
            third_product(0, True)
            with pe.Fori(1, B) as t:
                third_turn(t, False)
                third_product(t, False)

            def fourth(t, first):
                pe.wait_ge(s_el, t + 1)
                if not first:
                    pe.wait_ge(s_y3, t)
                turn4(bank[0], elT).then_inc(s_et, 1)
                pe.wait_ge(s_ln3, LN_STEPS * (t + 1))
                turn4(bank[1], flat(x3k)).then_inc(s_x3t, 1)
                pe.wait_ge(s_x3T, t + 1)
                for c in range(C):
                    ins = mm(bank[2][:, c * D:(c + 1) * D], x3T[:, c * P:(c + 1) * P], l3wt[:], True, True)
                ins.then_inc(s_h3, 1)
                pe.wait_ge(s_g, C * (t + 1))
                for c in range(C):
                    ins = mm(bank[3][:], gB[:, c, :], adj[:, t, c, :], c == 0, c == C - 1)
                ins.then_inc(s_num, 1)
                for c in range(C):
                    ins = mm(bank[4][0:1, :], fx[:, 1, c:c + 1], adj[:, t, c, :], c == 0, c == C - 1)
                ins.then_inc(s_den, 1)
                pe.wait_ge(s_numc, t + 1)
                if not first:
                    pe.wait_ge(s_y4, C * t)
                turn4(bank[5], numT).then_inc(s_nt, 1)
                pe.wait_ge(s_denc, t + 1)
                for c in range(C):
                    ins = mm(bank[6][:, c:c + 1], denr[0:1, c * P:(c + 1) * P], ones[0:1, 0:1], True, True)
                ins.then_inc(s_dt, 1)

            fourth(0, True)
            with pe.Fori(1, B) as t:
                fourth(t, False)


def kernel(**inputs):
    import concourse.bacc as bacc
    from concourse.bass_utils import run_bass_kernel_spmd

    a = {k: np.asarray(v) for k, v in inputs.items()}
    B, N, D = a["x"].shape

    def parts(v, n):
        return [v[i * P:(i + 1) * P] for i in range(n)]

    cols = {"g3": a["L2_gnn_g3"], "b3": a["L2_gnn_b3"], "a1": a["L2_gnn_a1"], "a2": a["L2_gnn_a2"]}
    for i, v in enumerate(parts(a["L0_gnn_b1"], 2)):
        cols[f"b1_{i}"] = v
    for k in ("bn1", "bn2"):
        for s in "gbmv":
            cols[f"{k}_{s}"] = a[f"L1_gnn_{k}_{s}"]
    for k in ("b_ih", "b_hh"):
        for g, v in zip("rzn", parts(a[f"L1_gnn_{k}"], 3)):
            cols[f"{k}_{g}"] = v
    for new, old in (("g1", "g1"), ("be1", "b1"), ("g2", "g2"), ("be2", "b2")):
        for i, v in enumerate(parts(a[f"L2_gnn_{old}"], N // P)):
            cols[f"{new}_{i}"] = v
    arrays = {
        "x_tok": a["x"], "x_fm": a["x"].transpose(0, 2, 1), "adj_t": a["adj"].transpose(0, 2, 1),
        "w1": a["L0_gnn_W1"], "w2": a["L0_gnn_W2"],
        "cols": np.stack([cols[c] for c in COLS], axis=1),
        "rows": np.stack([a["L0_gnn_b2"], a["L1_gnn_b_msg"], a["L3_gnn_W_b"], a["L3_gnn_a_w"][:D],
                          a["L3_gnn_a_w"][D:]]),
        "scal": np.concatenate([a["L0_gnn_eps"], a["L3_gnn_a_b"]]),
        "b_se": a["L1_gnn_b_se"].reshape(-1, 1), "w_se": a["L1_gnn_w_se"].T,
        "conv1": a["L1_gnn_conv1_w"][:, :, 0].T, "conv2": a["L1_gnn_conv2_w"].transpose(1, 2, 0),
        "w_msg": a["L1_gnn_w_msg"].T, "w_ih": a["L1_gnn_w_ih"].T, "w_hh": a["L1_gnn_w_hh"].T,
        "l2_w": a["L2_gnn_W"], "l2_wt": a["L2_gnn_W"].T, "l3_wt": a["L3_gnn_W_w"].T,
        "ident_in": np.eye(P, dtype=np.float32),
    }
    arrays = {k: np.ascontiguousarray(v) for k, v in arrays.items()}
    nc = bacc.Bacc("TRN2", target_bir_lowering=False, num_devices=1)
    args = [nc.dram_tensor(k, v.shape, mybir.dt.from_np(v.dtype), kind="ExternalInput").ap()
            for k, v in arrays.items()]
    out = nc.dram_tensor("out", (B, N, D), F32, kind="ExternalOutput").ap()
    build(nc, *args, out)
    r = run_bass_kernel_spmd(nc, [arrays], core_ids=[0])
    return r.results[0]["out"]
```

```python
from contextlib import ExitStack

import numpy as np
import concourse.bass as bass
from concourse import mybir

P = 128
ALU = mybir.AluOpType
ACT = mybir.ActivationFunctionType
AX = mybir.AxisListType
F32 = mybir.dt.float32
F32R = mybir.dt.float32r
I32 = mybir.dt.int32

LN_EPS = 1e-5
SLOPE = 0.2
RSQRT_MAGIC = float(0x5F3759DF)
RSQRT_STEPS = 11
STAT_STEPS = 4 + 1 + 4 + 3
ROOT_STEPS = 12

COLS = ["b1_0", "b1_1", "bn1_v", "bn2_v", "bn1_g", "bn2_g", "bn1_m", "bn2_m", "bn1_b", "bn2_b",
        "b_ih_r", "b_ih_z", "b_ih_n", "b_hh_r", "b_hh_z", "b_hh_n", "g3", "b3", "a1", "a2", "l3_a1", "l3_a2", "W_b",
        "g1_0", "g1_1", "g1_2", "g1_3", "be1_0", "be1_1", "be1_2", "be1_3",
        "g2_0", "g2_1", "g2_2", "g2_3", "be2_0", "be2_1", "be2_2", "be2_3"]
CI = {n: i for i, n in enumerate(COLS)}
ROWS = ["b2", "b_msg", "W_b"]
RI = {n: i for i, n in enumerate(ROWS)}


class Steps:

    def __init__(self, eng, sem, b, per_batch):
        self.eng, self.sem, self.base, self.per, self.k = eng, sem, b * per_batch, per_batch, 0

    def did(self, ins):
        ins.then_inc(self.sem, 1)
        self.k += 1

    def wait(self):
        self.eng.wait_ge(self.sem, self.base + self.k)

    def end(self):
        assert self.k == self.per, (self.k, self.per)


class NormTiles:

    def __init__(self, bn, mv, v, y, h, a):
        self.bn, self.mv, self.v, self.y, self.h, self.a = bn, mv, v, y, h, a


def rsqrt(eng, st, v, y, tmp, var, eps):
    st.did(eng.tensor_scalar(v, var, eps, None, ALU.add))
    st.wait()
    st.did(eng.tensor_scalar(y.bitcast(I32), v.bitcast(I32), -0.5, RSQRT_MAGIC, ALU.mult, ALU.add))
    for _ in range(3):
        st.wait()
        st.did(eng.scalar_tensor_tensor(out=tmp, in0=y, scalar=-0.5, in1=y, op0=ALU.mult, op1=ALU.mult))
        st.wait()
        st.did(eng.tensor_tensor(tmp, tmp, v, ALU.mult))
        st.wait()
        st.did(eng.scalar_tensor_tensor(out=y, in0=tmp, scalar=1.5, in1=y, op0=ALU.add, op1=ALU.mult))
    st.wait()


def norm_stats(eng, st, src, t):
    for c in range(4):
        st.did(eng.bn_stats(t.bn[:, c, :], src[:, c, :]))
    st.wait()
    st.did(eng.memset(t.v[:, 0:1], 0.0))
    for c in range(4):
        st.did(eng.bn_aggr(t.mv[:, c, :], t.bn[:, c, :]))
    st.wait()
    st.did(eng.tensor_scalar(t.v[:, :], t.mv[:, :, 1], LN_EPS, None, ALU.add))
    st.wait()
    st.did(eng.tensor_scalar(t.y[:, :].bitcast(I32), t.v[:, :].bitcast(I32), -0.5, RSQRT_MAGIC, ALU.mult, ALU.add))
    st.did(eng.tensor_scalar(t.h[:, :], t.v[:, :], -0.5, None, ALU.mult))
    st.end()


def norm_root(pool, st, t, c15):
    for i in range(3):
        if i:
            st.wait()
        st.did(pool.tensor_tensor(t.a[:, :], t.y[:, :], t.y[:, :], ALU.mult))
        st.wait()
        st.did(pool.tensor_tensor(t.a[:, :], t.a[:, :], t.h[:, :], ALU.mult))
        st.wait()
        st.did(pool.tensor_tensor(t.a[:, :], t.a[:, :], c15[:, :], ALU.add))
        st.wait()
        st.did(pool.tensor_tensor(t.y[:, :], t.y[:, :], t.a[:, :], ALU.mult))


def norm_shift(pool, st, t, zero):
    st.wait()
    st.did(pool.tensor_tensor(t.a[:, :], t.mv[:, :, 0], t.y[:, :], ALU.mult))
    st.wait()
    st.did(pool.tensor_tensor(t.h[:, :], zero[:, :], t.a[:, :], ALU.subtract))
    st.end()


def norm_apply(eng, sem, dst, src, t):
    for c in range(4):
        eng.tensor_scalar(dst[:, c, :], src[:, c, :], t.mv[:, c, 0:1], t.y[:, c:c + 1],
                          ALU.subtract, ALU.mult).then_inc(sem, 1)


def build(nc, x_tok, x_fm, adj_t, w1, w2, cols, rows, scal, masks, w_se, conv1, conv2, w_msg, w_ih, w_hh,
          l2_w, l2_wt, l3_w, l3_wt, ident_in, out):
    B, N, D = x_tok.shape
    C = N // P
    TAPS = conv2.shape[1]
    PAD = TAPS // 2
    BN = B * N

    with ExitStack() as ctx:
        def sb(name, shape, dt=F32):
            return ctx.enter_context(nc.sbuf_tensor(name, shape, dt))

        def sem(name):
            return ctx.enter_context(nc.semaphore(name))

        x2_dram = nc.dram_tensor("x2_dram", (B, P, C * D), F32).ap()
        wh_dram = nc.dram_tensor("wh_dram", (B, P, C * D), F32).ap()
        hp_dram = nc.dram_tensor("hp_dram", (B, P, N), F32).ap()
        ei_dram = nc.dram_tensor("ei_dram", (B, 1, N), F32).ap()

        bank = [ctx.enter_context(nc.psum_tensor(f"bank{i}", [P, 512], F32)) for i in range(8)]

        def tok(t):
            return t[:, :].rearrange("p (c d) -> p c d", c=C)

        def pair(name, shape):
            return tmp.enter_context(nc.sbuf_tensor(name + "_hi", shape, F32R)), \
                tmp.enter_context(nc.sbuf_tensor(name + "_lo", shape, F32R))

        with ExitStack() as tmp:
            w1p = pair("w1", [P, 2 * D])
            conv1p = pair("conv1", [P, D])
            conv2p = pair("conv2", [P, TAPS, D])
            wihp = pair("wih", [P, 2, 3 * D])
            whhp = pair("whh", [P, 3 * D])
            w2s = tmp.enter_context(nc.sbuf_tensor("w2s", [P, 2, D], F32))
            wmsg = tmp.enter_context(nc.sbuf_tensor("wmsg", [P, D], F32))
        WSLOTS = 4
        RING = B - WSLOTS

        def adj_slot(b):
            return (b + RING - WSLOTS) % RING + WSLOTS

        adj = sb("adj", [P, B, C, N])

        with ExitStack() as tmp:
            h0p = pair("h0", [P, N])
            x1p = [pair(f"x1_{i}", [P, N]) for i in range(2)]
            c1p = pair("c1", [P, N + 2 * PAD])
            xcp = pair("xc", [P, N])
            xnp_ = pair("xn", [P, N])
        zT = sb("zT", [P, C, N])
        PTs = [sb(f"PT{i}", [P, N]) for i in range(C)]
        ebc = [sb(f"ebc{i}", [P, N]) for i in range(2)]
        outk_ = sb("outk", [P, C, D])
        st2_ = sb("st2", [P, C, B, 6])
        ET = sb("ET", [B * C, P])
        e1c = sb("e1c", [P, B * C])
        dj = sb("dj", [P, C, B])
        xk = sb("xk", [P, C, D])
        xT = sb("xT", [P, N])
        col = sb("col", [P, len(COLS)])
        row = sb("row", [P, len(ROWS), D])
        sc = sb("sc", [P, 2])
        l2w = sb("l2w", [P, D])
        l2wt = sb("l2wt", [P, D])
        l3w = sb("l3w", [P, D])
        l3wt = sb("l3wt", [P, D])
        ident = sb("ident", [P, P])
        ones = sb("ones", [P, P])

        eps1 = sb("eps1", [P, 1])
        bnv = sb("bnv", [P, 2])
        bnr = sb("bnr", [P, 2])
        bnt = sb("bnt", [P, 2])
        bnsc = sb("bnsc", [P, 2])
        bnbi = sb("bnbi", [P, 2])
        half_b = sb("half_b", [P, 2])
        v12 = sb("v12", [P, 2])
        v34 = sb("v34", [P, 2])
        ec = sb("ec", [P, 2])

        wse = sb("wse", [P, 64])
        mask = sb("mask", [P, 7])
        Sx = sb("Sx", [P, N])
        Rt = sb("Rt", [P, N], F32R)
        Lt = sb("Lt", [P, N], F32R)

        hidT = sb("hidT", [P, 2, N])
        yk = sb("yk", [P, C, D])
        x1T = sb("x1T", [P, 2, N])
        zero = sb("zero", [P, 1])
        gate = sb("gate", [P, 1])
        msg = sb("msg", [P, C, D])
        AT = sb("AT", [P, C, N])
        trT = sb("trT", [P, N])
        tzT = sb("tzT", [P, N])
        ghT = sb("ghT", [P, N])
        nT = sb("nT", [P, N])
        x2k = sb("x2k", [P, C, D])
        x2T = sb("x2T", [P, N])
        whk = sb("whk", [P, C, D])
        E12 = sb("E12", [P, B, C, 2])
        c15 = sb("c15", [P, C])
        zero4 = sb("zero4", [P, C])

        def norm_tiles(name):
            return NormTiles(bn=sb(name + "_bn", [P, C, 6]), mv=sb(name + "_mv", [P, C, 2]),
                             v=sb(name + "_v", [P, C]), y=sb(name + "_y", [P, C]),
                             h=sb(name + "_h", [P, C]), a=sb(name + "_a", [P, C]))

        na = norm_tiles("na")
        nb = norm_tiles("nb")
        lv = sb("lv", [P, C])
        lr = sb("lr", [P, C])
        lt = sb("lt", [P, C])

        e1 = sb("e1", [P, B * C])
        ejT = sb("ejT", [P, C, B])
        mb = sb("mb", [P, B])
        mtot = sb("mtot", [P, 1])
        vare = sb("vare", [P, 1])
        mbc = sb("mbc", [P, B])
        mj = sb("mj", [P, C])
        djq = sb("djq", [P, C, B])
        vj = sb("vj", [P, C])
        s1 = sb("s1", [P, C])
        t1 = sb("t1", [P, C, B])
        tt1 = sb("tt1", [P, B, C])
        s1k = sb("s1k", [P, 2, C])
        tt1k = sb("tt1k", [P, 2, B, C])
        st2 = st2_
        mv2 = sb("mv2", [P, C, 2])
        c2 = sb("c2", [P, C])
        d2 = sb("d2", [P, C])
        st3 = sb("st3", [P, B, 6])
        mv3 = sb("mv3", [P, 2])
        a3 = sb("a3", [P, 4])
        nmax = sb("nmax", [P, C])
        rsum = sb("rsum", [P, C])
        rrec = sb("rrec", [P, C])

        h0T = x2T
        c1T = x2T
        xcT = trT
        vT = ghT
        LT = AT
        hpT = nT
        diag = tzT
        SE = slice(64, P)

        s_w = sem("s_w")
        s_adj = sem("s_adj")
        s_adj2 = sem("s_adj2")
        s_split = sem("s_split")
        s_x = sem("s_x")
        s_pre = sem("s_pre")
        s_prep = sem("s_prep")
        s_half = sem("s_half")
        s_agg = sem("s_agg")
        s_h0 = sem("s_h0")
        s_hid = sem("s_hid")
        s_hidr = sem("s_hidr")
        s_y = sem("s_y")
        s_xb = sem("s_xb")
        s_ysb = sem("s_ysb")
        s_ln1 = sem("s_ln1")
        s_st = {n: sem(f"s_stat{n}") for n in (1, 2, 3, 4)}
        s_rt = {n: sem(f"s_root{n}") for n in (1, 2, 3, 4)}
        s_x1t = sem("s_x1t")
        s_x1T = sem("s_x1T")
        s_s = sem("s_s")
        s_srow = sem("s_srow")
        s_slr = sem("s_slr")
        s_nsq = sem("s_nsq")
        s_nsqc = sem("s_nsqc")
        s_c1 = sem("s_c1")
        s_c1T = sem("s_c1T")
        s_c1l = sem("s_c1l")
        s_x1l = sem("s_x1l")
        s_h0p = sem("s_h0p")
        s_xcl = sem("s_xcl")
        s_xnl = sem("s_xnl")
        s_msg = sem("s_msg")
        s_msgb = sem("s_msgb")
        s_msgr = sem("s_msgr")
        s_dist = sem("s_dist")
        s_exp = sem("s_exp")
        s_A = sem("s_A")
        s_cv = sem("s_cv")
        s_cvx = sem("s_cvx")
        s_xc = sem("s_xc")
        s_nmp = sem("s_nmp")
        s_xn = sem("s_xn")
        s_gate = sem("s_gate")
        s_gh = sem("s_gh")
        s_tr = sem("s_tr")
        s_tz = sem("s_tz")
        s_gru = sem("s_gru")
        s_n = sem("s_n")
        s_tv = sem("s_tv")
        s_ln2 = sem("s_ln2")
        s_x2t = sem("s_x2t")
        s_x2T = sem("s_x2T")
        s_wh = sem("s_wh")
        s_whk = sem("s_whk")
        s_e = sem("s_e")
        s_ec = sem("s_ec")
        s_x2st = sem("s_x2st")
        s_whst = sem("s_whst")

        DIST = [6, 7, 1, 2]
        STAT3 = 1 + RSQRT_STEPS + 4
        STAT1 = 22 + RSQRT_STEPS + 4
        LB = 2 + 2 * 2
        PB = [4, 5, 6, 4]
        PA = [yk[:].rearrange("p c d -> p (c d)"), x2k[:].rearrange("p c d -> p (c d)"), x1T[:, 0, :], x1T[:, 1, :]]

        block = ctx.enter_context(nc.Block())
        N_WLOAD = 17
        PRE_STEPS = 8 + 3 + RSQRT_STEPS + 4
        GATES = 4
        S_STEPS = 7

        def iterations(eng, iteration):
            iteration(0, 0, True, False)
            with eng.Fori(0, (B - 2) // 2) as i:
                iteration(i * 2 + 1, 1, False, False)
                iteration(i * 2 + 2, 0, False, False)
            iteration(B - 1, 1, False, True)

        def last_layer(eng, iteration):
            for t in range(3):
                iteration(t, t % 2, t, 4)
            with eng.Fori(0, (B - 8) // 2) as i:
                iteration(i * 2 + 3, 1, 3, 4)
                iteration(i * 2 + 4, 0, 3, 4)
            for t in range(B - 5, B):
                iteration(t, t % 2, 3, B - 1 - t)

        s_ET = sem("s_ET")
        s_ETc = sem("s_ETc")
        s_eist = sem("s_eist")
        s_mbp = sem("s_mbp")
        s_ps = sem("s_ps")
        s_vp = sem("s_vp")
        s_ebc = sem("s_ebc")
        s_lB = sem("s_lB")
        s_bB = sem("s_bB")
        s_mB = sem("s_mB")
        s_aB = sem("s_aB")
        s_mC = sem("s_mC")
        s_st2 = sem("s_st2")
        s_ebcC = sem("s_ebcC")
        s_whl = sem("s_whl")
        s_lC = sem("s_lC")
        s_z = sem("s_z")
        s_zt = sem("s_zt")
        s_mx = sem("s_mx")
        s_ex = sem("s_ex")
        s_rr = sem("s_rr")
        s_dg = sem("s_dg")
        s_pt = sem("s_pt")
        s_pa = sem("s_pa")
        s_hp = sem("s_hp")
        s_hpe = sem("s_hpe")
        s_hps = sem("s_hps")
        s_hpst = sem("s_hpst")
        s_st3 = sem("s_st3")
        s_hl = sem("s_hl")
        s_x2l = sem("s_x2l")
        s_elu = sem("s_elu")
        s_el = sem("s_el")
        s_et = sem("s_et")
        s_y3 = sem("s_y3")
        s_ln3 = sem("s_ln3")
        s_x3t = sem("s_x3t")
        s_x3T = sem("s_x3T")
        s_h3 = sem("s_h3")
        s_e3 = sem("s_e3")
        s_efx = sem("s_efx")
        s_g = sem("s_g")
        s_num = sem("s_num")
        s_den = sem("s_den")
        s_numc = sem("s_numc")
        s_nt = sem("s_nt")
        s_dt = sem("s_dt")
        s_wr = sem("s_wr")
        s_y4 = sem("s_y4")
        s_ln4 = sem("s_ln4")
        s_out = sem("s_out")
        s_on = sem("s_on")

        hT, x2l, elT, pT4, eT4, y3 = xT, xk, hidT[:, 0, :], hidT[:, 1, :], zT[:, 0, :], yk
        x3T = x1T[:, 0, :]
        den = msg[:].rearrange("p c d -> p (c d)")
        gB = whk
        numT = x1T[:, 1, :]
        fx = sb("fx", [P, 2, 2, C])
        fw = sb("fw", [P, 3, C])
        y4 = [AT[:, i, :].rearrange("p (c d) -> p c d", c=C) for i in (1, 3)]
        outk = outk_[:, :, :]
        x3k = [x2k, AT[:, 2, :].rearrange("p (c d) -> p c d", c=C)]

        def raw(at, n):
            return adj[:, WSLOTS:WSLOTS + 2].rearrange("p s c n -> p (s c n)")[:, at:at + n]

        SPLITS = ((w1p, 0), (conv1p, 2 * D), (whhp, 3 * D), (wihp, 6 * D), (conv2p, 12 * D))

        def flat_of(t):
            return t[:, :] if len(t.shape) == 2 else t[:, :, :].rearrange("p a b -> p (a b)")

        def hi_size(t):
            return int(np.prod(t.shape[1:]))

        @block.sync
        def _(sp):
            for dst, src in ((raw(0, 2 * D), w1), (raw(2 * D, D), conv1), (raw(3 * D, 3 * D), w_hh),
                             (raw(6 * D, 6 * D).rearrange("p (q g) -> p q g", q=2),
                              w_ih.rearrange("(q p) g -> p q g", p=P)),
                             (raw(12 * D, TAPS * D).rearrange("p (k d) -> p k d", d=D), conv2),
                             (w2s[:], w2.rearrange("(h p) d -> p h d", p=P)), (col[:], cols),
                             (mask[SE, :], masks), (wse[:], w_se), (wmsg[:], w_msg),
                             (l2w[:], l2_w), (l2wt[:], l2_wt), (l3wt[:], l3_wt), (l3w[:], l3_w), (ident[:], ident_in),
                             (row[:, :, :], rows.rearrange("(a r) d -> a r d", a=1).broadcast_to((P, len(ROWS), D))),
                             (sc[:, :], scal.rearrange("(a r) -> a r", a=1).broadcast_to((P, 2)))):
                sp.dma_start(dst, src).then_inc(s_w, 16)

            def load_adj(b):
                sp.dma_start(adj[:, adj_slot(b)], adj_t[b].rearrange("(c p) i -> p c i", p=P)).then_inc(s_adj, 16)

            def load_x(b):
                sp.dma_start(xk[:], x_tok[b].rearrange("(c p) d -> p c d", p=P)).then_inc(s_x, 16)
                sp.dma_start(xT[:], x_fm[b]).then_inc(s_x, 16)

            load_adj(0)
            load_x(0)
            sp.wait_ge(s_adj, 16)
            load_adj(1)
            sp.wait_ge(s_split, 2 * len(SPLITS))

            def store_x2(b):
                sp.wait_ge(s_ln2, C * (b + 1))
                sp.dma_start(x2_dram[b], x2k[:].rearrange("p c d -> p (c d)")).then_inc(s_x2st, 16)

            def store_wh(b):
                sp.wait_ge(s_whk, b + 1)
                sp.dma_start(wh_dram[b], whk[:].rearrange("p c d -> p (c d)")).then_inc(s_whst, 16)

            def sp_iteration(t, p, first, last):
                if not last:
                    sp.wait_ge(s_ysb, t + 1)
                    load_x(t + 1)
                if not first:
                    if not last:
                        sp.wait_ge(s_adj, 16 * (t + 1))
                        load_adj(t + 1)
                    store_x2(t - 1)
                    store_wh(t - 1)

            iterations(sp, sp_iteration)
            store_x2(B - 1)
            store_wh(B - 1)

            sp.wait_ge(s_ETc, 1)
            sp.dma_start(ei_dram.rearrange("b a (c p) -> (b a c) p", p=P), ET[:]).then_inc(s_eist, 16)
            sp.wait_ge(s_eist, 16)
            sp.wait_ge(s_whst, 16 * B)
            sp.wait_ge(s_x2st, 16 * B)

            def load_ebc(b, p, s):
                sp.dma_start(ebc[p][:], ei_dram[b].broadcast_to((P, N))).then_inc(s, 16)

            load_ebc(0, 0, s_ebc)
            sp.wait_ge(s_ebc, 16)
            load_ebc(1, 1, s_ebc)

            def load_ebc_pair(b):
                for p in range(2):
                    sp.wait_ge(s_lB, LB * (b + p - 1))
                    sp.wait_ge(s_ebc, 16 * (b + p))
                    load_ebc(b + p, p, s_ebc)

            sp.wait_ge(s_gate, GATES * B)
            with sp.Fori(0, WSLOTS) as i:
                load_ebc_pair(i * 2 + 2)
                sp.dma_start(adj[:, i], adj_t[i].rearrange("(c p) i -> p c i", p=P)).then_inc(s_adj2, 16)
            with sp.Fori(WSLOTS, (B - 2) // 2) as i:
                load_ebc_pair(i * 2 + 2)

            sp.wait_ge(s_lB, LB * B)
            load_ebc(0, 0, s_ebcC)
            sp.dma_start(whk[:].rearrange("p c d -> p (c d)"), wh_dram[0]).then_inc(s_whl, 16)
            sp.wait_ge(s_ebcC, 16)
            load_ebc(1, 1, s_ebcC)

            def load_ebc_again(b, p):
                sp.wait_ge(s_lC, C * (b - 1))
                sp.wait_ge(s_ebcC, 16 * b)
                load_ebc(b, p, s_ebcC)

            load_ebc_again(2, 0)

            def third(t, p, more):
                if more > 1:
                    load_ebc_again(t + 3, 1 - p)
                sp.wait_ge(s_hpe, t + 1)
                sp.dma_start(hp_dram[t], hpT[:]).then_inc(s_hpst, 16)
                if more > 0:
                    sp.dma_start(whk[:].rearrange("p c d -> p (c d)"), wh_dram[t + 1]).then_inc(s_whl, 16)

            with sp.Fori(0, (B - 4) // 2) as i:
                third(i * 2, 0, 2)
                third(i * 2 + 1, 1, 2)
            third(B - 4, 0, 2)
            third(B - 3, 1, 1)
            third(B - 2, 0, 1)
            third(B - 1, 1, 0)

            sp.wait_ge(s_hpst, 16 * B)

            def load_h(b):
                if not (isinstance(b, int) and b == 0):
                    sp.wait_ge(s_elu, 3 * b)
                sp.dma_start(hT[:], hp_dram[b]).then_inc(s_hl, 16)

            def load_x2(b):
                if not (isinstance(b, int) and b == 0):
                    sp.wait_ge(s_y3, b)
                sp.dma_start(x2l[:].rearrange("p c d -> p (c d)"), x2_dram[b]).then_inc(s_x2l, 16)

            def fourth(t, p, age, left):
                if left > 2:
                    load_x2(t + 3)
                if left > 3:
                    load_h(t + 4)
                if age > 1:
                    store_out(t - 2)

            def store_out(b):
                sp.wait_ge(s_ln4, C * (b + 1))
                sp.dma_start(out[b].rearrange("(c p) d -> p c d", p=P), outk).then_inc(s_out, 16)

            for b in range(3):
                load_h(b)
                load_x2(b)
            load_h(3)
            last_layer(sp, fourth)
            store_out(B - 2)
            store_out(B - 1)
            sp.wait_ge(s_out, 16 * B)

        @block.gpsimd
        def _(pool):
            pool.wait_ge(s_w, 16 * N_WLOAD)

            pool.wait_ge(s_pre, PRE_STEPS)

            def make_xb(b):
                pool.wait_ge(s_x, 32 * (b + 1))
                pool.wait_ge(s_agg, b + 1)
                pool.tensor_tensor(xk[:], xk[:], row[:, RI["b2"]:RI["b2"] + 1, :].broadcast_to((P, C, D)),
                                   ALU.add).then_inc(s_xb, 1)

            def x1_low(b, p):
                pool.wait_ge(s_x1T, 2 * (b + 1))
                pool.tensor_tensor(x1p[p][1][:], x1T[:, p, :], x1p[p][0][:].bitcast(F32),
                                   ALU.subtract).then_inc(s_x1l, 1)

            def c1_low(b):
                pool.wait_ge(s_c1T, 2 * (b + 1))
                pool.tensor_tensor(c1p[1][:, PAD:PAD + N], c1T[:], c1p[0][:, PAD:PAD + N].bitcast(F32),
                                   ALU.subtract).then_inc(s_c1l, 1)

            def relu_msg(b):
                pool.wait_ge(s_msgb, b + 1)
                pool.tensor_tensor(gate[:], zero[:], zero[:], ALU.add)
                pool.tensor_scalar(msg[:], msg[:], 0.0, None, ALU.max).then_inc(s_msgr, 1)

            def root(n, b, tiles):
                pool.wait_ge(s_st[n], STAT_STEPS * (b + 1))
                st = Steps(pool, s_rt[n], b, ROOT_STEPS)
                norm_root(pool, st, tiles, c15)
                st.end()

            def root_shift(b):
                pool.wait_ge(s_st[4], STAT_STEPS * (b + 1))
                st = Steps(pool, s_rt[4], b, ROOT_STEPS + 2)
                norm_root(pool, st, nb, c15)
                norm_shift(pool, st, nb, zero4)

            def iteration(t, p, first, last):
                c1_low(t)
                relu_msg(t)
                if not last:
                    make_xb(t + 1)
                if not first:
                    root(2, t - 1, nb)
                if not last:
                    root(1, t + 1, na)
                    x1_low(t + 1, 1 - p)

            make_xb(0)
            root(1, 0, na)
            x1_low(0, 0)
            iterations(pool, iteration)
            root(2, B - 1, nb)

            with pool.Fori(0, B) as b:
                for i in range(2):
                    pool.wait_ge(s_lB, LB * b + 3 * (i + 1))
                    pool.tensor_tensor(LT[:, 2 + i, :], LT[:, 2 + i, :], zT[:, 2 + i, :], ALU.add).then_inc(s_aB, 1)

            pool.wait_ge(s_st2, 1)

            def scores(t):
                for c in range(C):
                    pool.wait_ge(s_mC, C * t + c + 1)
                    if not isinstance(t, int):
                        pool.wait_ge(s_zt, C * t)
                    if c or not isinstance(t, int):
                        pool.wait_ge(s_z, C * t + c)
                    pool.tensor_tensor(gate[:], zero[:], zero[:], ALU.add)
                    pool.tensor_scalar(zT[:, c, :], LT[:, c, :], c2[:, c:c + 1], d2[:, c:c + 1],
                                       ALU.mult, ALU.add).then_inc(s_z, 1)

            scores(0)
            with pool.Fori(1, B) as t:
                scores(t)

            def elu_sum(b):
                pool.wait_ge(s_elu, 3 * (b + 1))
                if not (isinstance(b, int) and b == 0):
                    pool.wait_ge(s_et, b)
                pool.tensor_tensor(elT, eT4, pT4, ALU.add).then_inc(s_el, 1)

            def fourth(t, p, age, left):
                if left > 1:
                    root(3, t + 2, na)
                if left > 2:
                    elu_sum(t + 3)
                if age:
                    root_shift(t - 1)

            elu_sum(0)
            root(3, 0, na)
            elu_sum(1)
            root(3, 1, na)
            elu_sum(2)
            last_layer(pool, fourth)
            root_shift(B - 1)

        @block.scalar
        def _(act):
            act.wait_ge(s_w, 16 * N_WLOAD)
            act.wait_ge(s_pre, PRE_STEPS)

            def hidden(b):
                for h in range(2):
                    act.wait_ge(s_hid, 2 * b + h + 1)
                    if not (isinstance(b, int) and b == 0):
                        act.wait_ge(s_y, b)
                    act.activation(hidT[:, h, :], bank[3 + h][:], ACT.Relu,
                                   bias=col[:, CI["b1_0"] + h:CI["b1_0"] + h + 1]).then_inc(s_hidr, 1)

            def x1_t(b, p, old):
                act.wait_ge(s_x1t, b + 1)
                if old:
                    act.wait_ge(s_gru, 6 * (b - 1))
                act.copy(x1p[p][0][:], bank[3][:]).then_inc(s_x1T, 1)
                act.copy(x1T[:, p, :], bank[3][:]).then_inc(s_x1T, 1)

            def x2_t(b):
                act.wait_ge(s_x2t, b + 1)
                if not (isinstance(b, int) and b == 0):
                    act.wait_ge(s_e, b)
                act.copy(x2T[:], bank[5][:]).then_inc(s_x2T, 1)

            def iteration(t, p, first, last):
                act.wait_ge(s_s, t + 1)
                if not first:
                    act.wait_ge(s_slr, S_STEPS * t)
                act.activation(Sx[SE, :], bank[1][SE, :], ACT.Identity, bias=mask[SE, 0:1]).then_inc(s_srow, 1)
                act.wait_ge(s_c1, t + 1)
                if not first:
                    act.wait_ge(s_cv, t)
                act.activation(c1p[0][:, PAD:PAD + N], bank[2][:], ACT.Relu, bias=bnbi[:, 0:1],
                               scale=bnsc[:, 0:1]).then_inc(s_c1T, 1)
                act.activation(c1T[:], bank[2][:], ACT.Relu, bias=bnbi[:, 0:1],
                               scale=bnsc[:, 0:1]).then_inc(s_c1T, 1)
                for c in range(C):
                    act.wait_ge(s_dist, C * t + c + 1)
                    if not first:
                        act.wait_ge(s_nmp, t)
                    act.activation(AT[:, c, :], bank[DIST[c]][:], ACT.Exp).then_inc(s_exp, 1)
                if not last:
                    hidden(t + 1)
                if not first:
                    x2_t(t - 1)
                act.wait_ge(s_cvx, t + 1)
                if not first:
                    act.wait_ge(s_gate, GATES * t)
                act.activation(xcp[0][:], xcT[:], ACT.Relu, bias=bnbi[:, 1:2]).then_inc(s_xc, 1)
                act.activation(xcT[:], xcT[:], ACT.Relu, bias=bnbi[:, 1:2]).then_inc(s_xc, 1)
                act.wait_ge(s_nmp, t + 1)
                act.copy(xnp_[0][:], bank[2][:]).then_inc(s_xn, 1)
                if not last:
                    x1_t(t + 1, 1 - p, not first)
                act.wait_ge(s_gate, GATES * t + 1)
                if not first:
                    act.wait_ge(s_tv, t)
                act.activation(ghT[:], bank[7][:], ACT.Identity,
                               bias=col[:, CI["b_hh_n"]:CI["b_hh_n"] + 1]).then_inc(s_gh, 1)
                act.wait_ge(s_gate, GATES * t + 2)
                act.wait_ge(s_xcl, t + 1)
                act.activation(trT[:], bank[4][:], ACT.Tanh, bias=half_b[:, 0:1], scale=0.5).then_inc(s_tr, 1)
                act.wait_ge(s_gate, GATES * t + 3)
                act.activation(tzT[:], bank[5][:], ACT.Tanh, bias=half_b[:, 1:2], scale=0.5).then_inc(s_tz, 1)
                act.wait_ge(s_gru, 6 * t + 2)
                act.activation(nT[:], nT[:], ACT.Tanh,
                               bias=col[:, CI["b_ih_n"]:CI["b_ih_n"] + 1]).then_inc(s_n, 1)

            hidden(0)
            x1_t(0, 0, False)
            iterations(act, iteration)
            x2_t(B - 1)

            act.wait_ge(s_ET, 1)
            act.copy(ET[:], bank[0][0:B * C, 0:P]).then_inc(s_ETc, 1)

            def normed(b, p, c, s):
                act.activation(LT[:, c, :], ebc[p][:], ACT.Identity, bias=tt1[:, b, c:c + 1],
                               scale=s1[:, c:c + 1]).then_inc(s, 1)

            act.wait_ge(s_ps, STAT1)

            def leaky_parts(b, p, c):
                for k, (dst, f) in enumerate(((LT, ACT.Identity), (zT, ACT.Relu))):
                    act.activation(dst[:, c, :], ebc[p][:], f, bias=tt1k[:, k, b, c:c + 1],
                                   scale=s1k[:, k, c:c + 1]).then_inc(s_lB, 1)

            def stats_tiles(b, p, first):
                act.wait_ge(s_ebc, 16 * (b + 1))
                for i, c in enumerate((0, 2, 1, 3)):
                    if not first:
                        act.wait_ge(s_bB, C * (b - 1) + i + 1)
                    if c < 2:
                        normed(b, p, c, s_lB)
                    else:
                        leaky_parts(b, p, c)

            stats_tiles(0, 0, True)
            stats_tiles(1, 1, False)
            with act.Fori(0, (B - 2) // 2) as i:
                stats_tiles(i * 2 + 2, 0, False)
                stats_tiles(i * 2 + 3, 1, False)

            def normed_all(b, p):
                act.wait_ge(s_ebcC, 16 * (b + 1))
                for c in range(C):
                    if not (isinstance(b, int) and b == 0):
                        act.wait_ge(s_z, C * (b - 1) + c + 1)
                    normed(b, p, c, s_lC)

            def product_out(t):
                act.wait_ge(s_hp, t + 1)
                if not (isinstance(t, int) and t == 0):
                    act.wait_ge(s_hpst, 16 * t)
                    act.wait_ge(s_hps, t)
                act.copy(hpT[:], bank[7][:]).then_inc(s_hpe, 1)

            def third(t, p, first, last):
                for c in range(C):
                    act.wait_ge(s_mx, C * t + c + 1)
                    if not first:
                        act.wait_ge(s_pt, C * t)
                    act.activation(PTs[c][:], bank[c][:], ACT.Exp, bias=nmax[:, c:c + 1],
                                   accum_out=rsum[:, c:c + 1]).then_inc(s_ex, 1)
                if not first:
                    product_out(t - 1)
                if not last:
                    normed_all(t + 2, p)

            act.wait_ge(s_bB, C * B)
            normed_all(0, 0)
            normed_all(1, 1)
            third(0, 0, True, False)
            third(1, 1, False, False)
            with act.Fori(0, (B - 4) // 2) as i:
                third(i * 2 + 2, 0, False, False)
                third(i * 2 + 3, 1, False, False)
            third(B - 2, 0, False, True)
            third(B - 1, 1, False, True)
            product_out(B - 1)

            act.wait_ge(s_st3, STAT3)

            def elu(b):
                act.wait_ge(s_hl, 16 * (b + 1))
                if not (isinstance(b, int) and b == 0):
                    act.wait_ge(s_el, b)
                act.activation(pT4, hT[:], ACT.Relu, bias=a3[:, 1:2], scale=a3[:, 0:1]).then_inc(s_elu, 1)
                act.activation(eT4, hT[:], ACT.Relu, bias=a3[:, 3:4], scale=a3[:, 2:3]).then_inc(s_elu, 1)
                act.wait_ge(s_elu, 3 * b + 2)
                act.activation(eT4, eT4, ACT.Exp, scale=-1.0).then_inc(s_elu, 1)

            def copy_x3(b):
                act.wait_ge(s_x3t, b + 1)
                if not (isinstance(b, int) and b == 0):
                    act.wait_ge(s_h3, b)
                act.copy(x3T, bank[1][:]).then_inc(s_x3T, 1)

            def head_e(b, p, old):
                act.wait_ge(s_e3, b + 1)
                if old:
                    act.wait_ge(s_y4, C * (b - 1))
                ef = bank[7][:, 0:2 * C].rearrange("p (c k) -> p c k", c=C)
                for k in range(2):
                    act.activation(fx[:, p, k, :], ef[:, :, k], ACT.Exp, bias=ec[:, k:k + 1]).then_inc(s_efx, 1)

            def weigh(b, p):
                act.wait_ge(s_h3, b + 1)
                act.wait_ge(s_efx, 2 * (b + 1))
                if not (isinstance(b, int) and b == 0):
                    act.wait_ge(s_num, b)
                for c in range(C):
                    act.activation(gB[:, c, :], tok(bank[2])[:, c, :], ACT.Copy,
                                   scale=fx[:, p, 1, c:c + 1]).then_inc(s_g, 1)

            def norm4(b, p, later):
                act.wait_ge(s_rt[4], (ROOT_STEPS + 2) * (b + 1))
                if later:
                    act.wait_ge(s_out, 16 * b)
                for c in range(C):
                    act.activation(outk[:, c, :], y4[p][:, c, :], ACT.Identity, bias=nb.h[:, c:c + 1],
                                   scale=nb.y[:, c:c + 1]).then_inc(s_ln4, 1)

            def fourth(t, p, age, left):
                if left > 2:
                    elu(t + 3)
                if left > 0:
                    copy_x3(t + 1)
                if age > 1:
                    norm4(t - 2, p, age > 2)
                act.wait_ge(s_num, t + 1)
                if age:
                    act.wait_ge(s_nt, t)
                act.copy(numT, bank[3][:]).then_inc(s_numc, 1)
                if left > 0:
                    head_e(t + 1, 1 - p, age)
                if left > 0:
                    weigh(t + 1, 1 - p)

            elu(0)
            elu(1)
            elu(2)
            copy_x3(0)
            head_e(0, 0, False)
            weigh(0, 0)
            last_layer(act, fourth)
            norm4(B - 2, 0, True)
            norm4(B - 1, 1, True)

        @block.vector
        def _(dve):
            pre = Steps(dve, s_pre, 0, PRE_STEPS)
            pre.did(dve.memset(ones[:], 1.0))
            pre.did(dve.memset(zero[:], 0.0))
            pre.did(dve.memset(c15[:], 1.5))
            pre.did(dve.memset(zero4[:], 0.0))
            for h in c1p:
                pre.did(dve.memset(h[:, 0:PAD].bitcast(F32), 0.0))
                pre.did(dve.memset(h[:, PAD + N:].bitcast(F32), 0.0))
            dve.wait_ge(s_w, 16 * N_WLOAD)
            pre.wait()
            pre.did(dve.tensor_scalar(eps1[:], sc[:, 0:1], 1.0, None, ALU.add))
            pre.did(dve.tensor_scalar(AT[:, 0, 0:P], ones[:], col[:, CI["W_b"]:CI["W_b"] + 1], None, ALU.mult))
            pre.did(dve.tensor_tensor(half_b[:], col[:, CI["b_ih_r"]:CI["b_ih_r"] + 2],
                                      col[:, CI["b_hh_r"]:CI["b_hh_r"] + 2], ALU.add))
            rsqrt(dve, pre, bnv[:], bnr[:], bnt[:], col[:, CI["bn1_v"]:CI["bn1_v"] + 2], LN_EPS)
            pre.did(dve.tensor_tensor(bnsc[:], bnr[:], col[:, CI["bn1_g"]:CI["bn1_g"] + 2], ALU.mult))
            pre.wait()
            pre.did(dve.tensor_tensor(bnt[:], bnsc[:], col[:, CI["bn1_m"]:CI["bn1_m"] + 2], ALU.mult))
            pre.wait()
            dve.wait_ge(s_prep, 1)
            dve.tensor_copy(v12[:], bank[7][:, 0:2]).then_inc(s_half, 1)
            dve.tensor_copy(v34[:], bank[7][:, 2:4]).then_inc(s_half, 1)
            dve.tensor_scalar(ec[:, 0:1], bank[7][:, 4:5], sc[:, 1:2], None, ALU.add).then_inc(s_half, 1)
            dve.tensor_copy(ec[:, 1:2], bank[7][:, 5:6]).then_inc(s_half, 1)
            pre.did(dve.tensor_tensor(bnbi[:], col[:, CI["bn1_b"]:CI["bn1_b"] + 2], bnt[:], ALU.subtract))
            pre.did(dve.tensor_scalar(half_b[:], half_b[:], 0.5, None, ALU.mult))
            pre.end()
            n = 0
            for (hi, lo), at in SPLITS:
                w = raw(at, hi_size(hi))
                hi, lo = flat_of(hi), flat_of(lo)
                n += 1
                dve.tensor_copy(hi, w).then_inc(s_split, 1)
                dve.wait_ge(s_split, n)
                n += 1
                dve.tensor_tensor(lo, w, hi.bitcast(F32), ALU.subtract).then_inc(s_split, 1)

            def make_h0(b):
                dve.wait_ge(s_agg, b + 1)
                if not (isinstance(b, int) and b == 0):
                    dve.wait_ge(s_c1l, b)
                dve.wait_ge(s_x, 32 * (b + 1))
                if not (isinstance(b, int) and b == 0):
                    dve.wait_ge(s_hid, 2 * b)
                dve.scalar_tensor_tensor(out=h0T[:], in0=xT[:], scalar=eps1[:, 0:1], in1=bank[4][:],
                                         op0=ALU.mult, op1=ALU.add).then_inc(s_h0, 1)
                dve.wait_ge(s_h0, b + 1)
                dve.tensor_copy(h0p[0][:], h0T[:]).then_inc(s_h0p, 1)
                dve.wait_ge(s_h0p, 2 * b + 1)
                dve.tensor_tensor(h0p[1][:], h0T[:], h0p[0][:].bitcast(F32), ALU.subtract).then_inc(s_h0p, 1)

            def make_x1(b):
                dve.wait_ge(s_y, b + 1)
                dve.wait_ge(s_xb, b + 1)
                if not (isinstance(b, int) and b == 0):
                    dve.wait_ge(s_x1t, b)
                dve.tensor_tensor(yk[:], tok(bank[6]), xk[:], ALU.add).then_inc(s_ysb, 1)
                dve.wait_ge(s_ysb, b + 1)
                norm_stats(dve, Steps(dve, s_st[1], b, STAT_STEPS), yk, na)

            def finish_x1(b):
                dve.wait_ge(s_rt[1], ROOT_STEPS * (b + 1))
                norm_apply(dve, s_ln1, yk, yk, na)

            def make_x2(b):
                dve.wait_ge(s_tv, b + 1)
                norm_stats(dve, Steps(dve, s_st[2], b, STAT_STEPS), tok(bank[5]), nb)

            def finish_x2(b):
                dve.wait_ge(s_rt[2], ROOT_STEPS * (b + 1))
                if not (isinstance(b, int) and b == 0):
                    dve.wait_ge(s_x2st, 16 * b)
                    dve.wait_ge(s_x2t, b)
                norm_apply(dve, s_ln2, x2k, tok(bank[5]), nb)

            def keep_wh(b):
                dve.wait_ge(s_wh, b + 1)
                if not (isinstance(b, int) and b == 0):
                    dve.wait_ge(s_whst, 16 * b)
                dve.tensor_copy(whk[:], tok(bank[7])).then_inc(s_whk, 1)
                dve.wait_ge(s_e, b + 1)
                dve.tensor_copy(E12[:, b], bank[1][:, 0:2 * C].rearrange("p (c k) -> p c k", c=C)).then_inc(s_ec, 1)

            def iteration(t, p, first, last):
                dve.wait_ge(s_srow, t + 1)
                if not first:
                    dve.wait_ge(s_dist, C * t)
                st = Steps(dve, s_slr, t, S_STEPS)
                st.did(dve.tensor_tensor(Sx[96:P, :], Sx[96:P, :], Sx[96:P, :], ALU.mult))
                st.wait()
                st.did(dve.tensor_copy(Rt[SE, :], Sx[SE, :]))
                st.wait()
                st.did(dve.tensor_tensor(Lt[SE, :], Sx[SE, :], Rt[SE, :].bitcast(F32), ALU.subtract))
                for side, k in ((Rt, 1), (Lt, 4)):
                    st.wait()
                    st.did(dve.tensor_scalar(Sx[SE, :], Rt[SE, :].bitcast(F32), mask[SE, k:k + 1],
                                             mask[SE, k + 2:k + 3], ALU.mult, ALU.add))
                    st.wait()
                    st.did(dve.scalar_tensor_tensor(out=side[0:64, :], in0=Lt[SE, :].bitcast(F32),
                                                    scalar=mask[SE, k + 1:k + 2], in1=Sx[SE, :],
                                                    op0=ALU.mult, op1=ALU.add))
                st.end()
                dve.wait_ge(s_msg, t + 1)
                if not first:
                    dve.wait_ge(s_nmp, t)
                dve.tensor_tensor(msg[:], tok(bank[3]), row[:, RI["b_msg"]:RI["b_msg"] + 1, :].broadcast_to((P, C, D)),
                                  ALU.add).then_inc(s_msgb, 1)
                if not last:
                    make_h0(t + 1)
                if not first:
                    make_x2(t - 1)
                for c in range(C):
                    if c == 3 and not first:
                        finish_x2(t - 1)
                    dve.wait_ge(s_exp, C * t + c + 1)
                    dve.wait_ge(s_adj, 16 * (t + 1))
                    dve.tensor_tensor(AT[:, c, :], AT[:, c, :], adj[:, adj_slot(t), c, :], ALU.mult).then_inc(s_A, 1)
                if not last:
                    make_x1(t + 1)
                    finish_x1(t + 1)
                if not first:
                    keep_wh(t - 1)
                dve.wait_ge(s_cv, t + 1)
                dve.scalar_tensor_tensor(out=xcT[:], in0=bank[0][:], scalar=bnsc[:, 1:2], in1=x1T[:, p, :],
                                         op0=ALU.mult, op1=ALU.add).then_inc(s_cvx, 1)
                dve.wait_ge(s_xc, 2 * (t + 1))
                if not first:
                    dve.wait_ge(s_gate, GATES * t)
                dve.tensor_tensor(xcp[1][:], xcT[:], xcp[0][:].bitcast(F32), ALU.subtract).then_inc(s_xcl, 1)
                dve.wait_ge(s_xn, t + 1)
                dve.tensor_tensor(xnp_[1][:], bank[2][:], xnp_[0][:].bitcast(F32), ALU.subtract).then_inc(s_xnl, 1)
                st = Steps(dve, s_gru, t, 6)
                dve.wait_ge(s_gh, t + 1)
                dve.wait_ge(s_tr, t + 1)
                st.did(dve.scalar_tensor_tensor(out=nT[:], in0=trT[:], scalar=1.0, in1=ghT[:],
                                                op0=ALU.add, op1=ALU.mult))
                st.wait()
                dve.wait_ge(s_gate, GATES * (t + 1))
                st.did(dve.scalar_tensor_tensor(out=nT[:], in0=nT[:], scalar=0.5, in1=bank[6][:],
                                                op0=ALU.mult, op1=ALU.add))
                dve.wait_ge(s_n, t + 1)
                st.did(dve.tensor_tensor(ghT[:], x1T[:, p, :], nT[:], ALU.subtract))
                st.wait()
                dve.wait_ge(s_tz, t + 1)
                st.did(dve.scalar_tensor_tensor(out=ghT[:], in0=tzT[:], scalar=1.0, in1=ghT[:],
                                                op0=ALU.add, op1=ALU.mult))
                st.did(dve.tensor_tensor(nT[:], x1T[:, p, :], nT[:], ALU.add))
                st.wait()
                if not first:
                    dve.wait_ge(s_tv, t)
                st.did(dve.scalar_tensor_tensor(out=vT[:], in0=ghT[:], scalar=0.5, in1=nT[:],
                                                op0=ALU.mult, op1=ALU.add))
                st.end()

            make_h0(0)
            make_x1(0)
            finish_x1(0)
            iterations(dve, iteration)
            make_x2(B - 1)
            finish_x2(B - 1)
            keep_wh(B - 1)

            st = Steps(dve, s_ps, 0, STAT1)
            dve.wait_ge(s_ec, B)
            st.did(dve.tensor_copy(e1[:], E12[:, :, :, 0].rearrange("p b c -> p (b c)")))
            st.did(dve.tensor_copy(ejT[:], E12[:, :, :, 1].rearrange("p b c -> p c b")))
            st.wait()
            dve.wait_ge(s_mbp, 1)
            st.did(dve.tensor_reduce(mb[:], bank[1][:, 0:B * C].rearrange("p (b c) -> p b c", c=C), AX.X, ALU.add))
            st.wait()
            st.did(dve.tensor_scalar(mb[:], mb[:], 1.0 / N, None, ALU.mult))
            st.wait()
            st.did(dve.tensor_reduce(mtot[:], mb[:], AX.X, ALU.add))
            st.wait()
            st.did(dve.tensor_scalar(mtot[:], mtot[:], 1.0 / B, None, ALU.mult))
            st.wait()
            st.did(dve.tensor_scalar(e1c[:], e1[:], mtot[:, 0:1], None, ALU.subtract))
            st.did(dve.tensor_scalar(mbc[:], mb[:], mtot[:, 0:1], None, ALU.subtract))
            st.wait()
            st.did(dve.tensor_tensor(e1c[:], e1c[:], e1c[:], ALU.mult))
            st.did(dve.tensor_reduce(mj[:], ejT[:], AX.X, ALU.add))
            st.wait()
            st.did(dve.tensor_scalar(mj[:], mj[:], 1.0 / B, None, ALU.mult))
            st.wait()
            st.did(dve.tensor_tensor(dj[:], ejT[:], mj[:].rearrange("p (c a) -> p c a", a=1).broadcast_to((P, C, B)),
                                     ALU.subtract))
            st.wait()
            st.did(dve.scalar_tensor_tensor(out=djq[:], in0=mbc[:].rearrange("p (a b) -> p a b", a=1).broadcast_to((P, C, B)),
                                            scalar=2.0, in1=dj[:], op0=ALU.mult, op1=ALU.add))
            st.wait()
            st.did(dve.tensor_tensor(djq[:], djq[:], dj[:], ALU.mult))
            dve.wait_ge(s_vp, 1)
            st.did(dve.tensor_reduce(vare[:], bank[2][:, 0:B * C], AX.X, ALU.add))
            st.wait()
            st.did(dve.tensor_reduce(vj[:], djq[:], AX.X, ALU.add))
            st.did(dve.tensor_scalar(vare[:], vare[:], 1.0 / BN, None, ALU.mult))
            st.wait()
            st.did(dve.tensor_scalar(vj[:], vj[:], 1.0 / B, vare[:, 0:1], ALU.mult, ALU.add))
            st.wait()
            rsqrt(dve, st, lv[:], lr[:], lt[:], vj[:], LN_EPS)
            st.did(dve.tensor_tensor(s1[:], lr[:], col[:, CI["g1_0"]:CI["g1_0"] + C], ALU.mult))
            st.did(dve.tensor_scalar(t1[:], dj[:], mtot[:, 0:1], None, ALU.subtract))
            st.wait()
            st.did(dve.tensor_tensor(t1[:], t1[:], s1[:].rearrange("p (c a) -> p c a", a=1).broadcast_to((P, C, B)),
                                     ALU.mult))
            st.wait()
            st.did(dve.tensor_tensor(tt1[:], t1[:].rearrange("p c b -> p b c"),
                                     col[:, CI["be1_0"]:CI["be1_0"] + C].rearrange("p (a c) -> p a c", a=1)
                                     .broadcast_to((P, B, C)), ALU.add))
            st.wait()
            for k, part in enumerate((SLOPE, 1 - SLOPE)):
                st.did(dve.tensor_scalar(s1k[:, k, :], s1[:], part, None, ALU.mult))
                st.did(dve.tensor_scalar(tt1k[:, k], tt1[:], part, None, ALU.mult))
            st.end()

            def leaky(c, done):
                dve.scalar_tensor_tensor(out=LT[:, c, :], in0=LT[:, c, :], scalar=SLOPE, in1=LT[:, c, :],
                                         op0=ALU.mult, op1=ALU.max).then_inc(done, 1)

            def counted(b, c):
                if c < 2:
                    dve.wait_ge(s_mB, 2 * b + c + 1)
                else:
                    dve.wait_ge(s_aB, 2 * b + c - 1)
                dve.bn_stats(st2[:, c, b, :], LT[:, c, :]).then_inc(s_bB, 1)

            def count_batch(b, first):
                dve.wait_ge(s_lB, LB * b + 1)
                leaky(0, s_mB)
                if not first:
                    counted(b - 1, 3)
                counted(b, 0)
                dve.wait_ge(s_lB, LB * b + 4)
                leaky(1, s_mB)
                counted(b, 2)
                counted(b, 1)

            count_batch(0, True)
            with dve.Fori(1, B) as b:
                count_batch(b, False)
            counted(B - 1, 3)
            dve.wait_ge(s_bB, C * B)
            s2 = Steps(dve, s_on, 0, C + RSQRT_STEPS + 2)
            for c in range(C):
                s2.did(dve.bn_aggr(mv2[:, c, :], st2[:, c, :, :].rearrange("p b s -> p (b s)")))
            s2.wait()
            rsqrt(dve, s2, lv[:], lr[:], lt[:], mv2[:, :, 1], LN_EPS)
            s2.did(dve.tensor_tensor(c2[:], lr[:], col[:, CI["g2_0"]:CI["g2_0"] + C], ALU.mult))
            s2.wait()
            s2.did(dve.tensor_tensor(d2[:], c2[:], mv2[:, :, 0], ALU.mult))
            s2.wait()
            dve.tensor_tensor(d2[:], col[:, CI["be2_0"]:CI["be2_0"] + C], d2[:], ALU.subtract).then_inc(s_st2, 1)
            s2.end()

            def third_leaky(t, c):
                dve.wait_ge(s_lC, C * t + c + 1)
                leaky(c, s_mC)

            def row_max(t, c, first):
                dve.wait_ge(s_zt, C * t + c + 1)
                if not first:
                    dve.wait_ge(s_ex, C * t)
                dve.tensor_reduce(nmax[:, c:c + 1], bank[c][:], AX.X, ALU.max, negate=True).then_inc(s_mx, 1)

            def row_diag(t, c):
                dve.wait_ge(s_ex, C * t + c + 1)
                dve.reciprocal(rrec[:, c:c + 1], rsum[:, c:c + 1]).then_inc(s_rr, 1)
                dve.wait_ge(s_rr, C * t + c + 1)
                dve.tensor_scalar(diag[:, c * P:(c + 1) * P], ident[:], rrec[:, c:c + 1], None,
                                  ALU.mult).then_inc(s_dg, 1)

            def masked(t, c):
                dve.wait_ge(s_pt, C * t + c + 1)
                dve.tensor_tensor(PA[c], bank[PB[c]][:], adj[:, t, c, :], ALU.mult).then_inc(s_pa, 1)

            def third_stats(t):
                dve.wait_ge(s_hpe, t + 1)
                dve.bn_stats(st3[:, t, :], hpT[:]).then_inc(s_hps, 1)

            def third(t, first, last):
                row_max(t, 0, first)
                row_max(t, 1, first)
                row_max(t, 2, first)
                row_diag(t, 0)
                row_max(t, 3, first)
                row_diag(t, 1)
                if not last:
                    third_leaky(t + 1, 0)
                row_diag(t, 2)
                if not last:
                    third_leaky(t + 1, 1)
                row_diag(t, 3)
                if not last:
                    third_leaky(t + 1, 2)
                    third_leaky(t + 1, 3)
                masked(t, 0)
                masked(t, 1)
                if not first:
                    third_stats(t - 1)
                masked(t, 2)
                masked(t, 3)

            dve.wait_ge(s_adj2, 16 * WSLOTS)
            for c in range(C):
                third_leaky(0, c)
            third(0, True, False)
            with dve.Fori(1, B - 1) as t:
                third(t, False, False)
            third(B - 1, False, True)
            third_stats(B - 1)

            s3 = Steps(dve, s_st3, 0, STAT3)
            dve.wait_ge(s_hps, B)
            s3.did(dve.bn_aggr(mv3[:], st3[:, :, :].rearrange("p b s -> p (b s)")))
            s3.wait()
            rsqrt(dve, s3, lv[:, 0:1], lr[:, 0:1], lt[:, 0:1], mv3[:, 1:2], LN_EPS)
            s3.did(dve.tensor_tensor(a3[:, 0:1], lr[:, 0:1], col[:, CI["g3"]:CI["g3"] + 1], ALU.mult))
            s3.wait()
            s3.did(dve.tensor_tensor(lt[:, 0:1], a3[:, 0:1], mv3[:, 0:1], ALU.mult))
            s3.wait()
            s3.did(dve.tensor_tensor(a3[:, 1:2], col[:, CI["b3"]:CI["b3"] + 1], lt[:, 0:1], ALU.subtract))
            s3.wait()
            s3.did(dve.tensor_scalar(a3[:, 2:4], a3[:, 0:2], -1.0, None, ALU.mult))
            s3.end()

            def head(b):
                if not (isinstance(b, int) and b == 0):
                    dve.wait_ge(s_ln3, C * b)
                dve.wait_ge(s_et, b + 1)
                dve.wait_ge(s_x2l, 16 * (b + 1))
                dve.scalar_tensor_tensor(out=y3[:], in0=tok(bank[0]), scalar=-1.0, in1=x2l[:], op0=ALU.add,
                                         op1=ALU.add).then_inc(s_y3, 1)
                dve.wait_ge(s_y3, b + 1)
                norm_stats(dve, Steps(dve, s_st[3], b, STAT_STEPS), y3, na)

            def head_x3(b, p):
                dve.wait_ge(s_rt[3], ROOT_STEPS * (b + 1))
                norm_apply(dve, s_ln3, x3k[p], y3, na)

            def denominator(b, p):
                dve.wait_ge(s_efx, 2 * (b + 1))
                if not (isinstance(b, int) and b == 0):
                    dve.wait_ge(s_dt, b)
                for c in range(C):
                    f = fx[:, p, 1, c:c + 1]
                    if c == 0:
                        dve.tensor_scalar(den, adj[:, b, c, :], f, None, ALU.mult).then_inc(s_den, 1)
                    else:
                        dve.wait_ge(s_den, C * b + c)
                        dve.scalar_tensor_tensor(out=den, in0=adj[:, b, c, :], scalar=f, in1=den, op0=ALU.mult,
                                                 op1=ALU.add).then_inc(s_den, 1)

            def weights(t, p):
                dve.wait_ge(s_dt, t + 1)
                dve.tensor_tensor(fw[:, 0, :], bank[6][:, 0:C], fx[:, p, 0, :], ALU.mult).then_inc(s_wr, 1)
                dve.wait_ge(s_wr, 3 * t + 1)
                dve.reciprocal(fw[:, 1, :], fw[:, 0, :]).then_inc(s_wr, 1)
                dve.wait_ge(s_wr, 3 * t + 2)
                dve.tensor_tensor(fw[:, 2, :], fw[:, 1, :], fx[:, p, 0, :], ALU.mult).then_inc(s_wr, 1)

            def tail(t, p, age):
                dve.wait_ge(s_wr, 3 * t + 3)
                dve.wait_ge(s_nt, t + 1)
                if age > 1:
                    dve.wait_ge(s_ln4, C * (t - 1))
                for c in range(C):
                    dve.scalar_tensor_tensor(out=y4[p][:, c, :], in0=tok(bank[5])[:, c, :], scalar=fw[:, 2, c:c + 1],
                                             in1=x3k[p][:, c, :], op0=ALU.mult, op1=ALU.add).then_inc(s_y4, 1)

            def tail_stats(b, p, age):
                dve.wait_ge(s_y4, C * (b + 1))
                if age > 1:
                    dve.wait_ge(s_ln4, C * b)
                norm_stats(dve, Steps(dve, s_st[4], b, STAT_STEPS), y4[p], nb)

            def fourth(t, p, age, left):
                if left > 1:
                    head(t + 2)
                denominator(t, p)
                if age:
                    tail_stats(t - 1, 1 - p, age)
                weights(t, p)
                tail(t, p, age)
                if left > 1:
                    dve.wait_ge(s_y4, C * (t + 1))
                    head_x3(t + 2, p)

            head(0)
            head_x3(0, 0)
            head(1)
            head_x3(1, 1)
            last_layer(dve, fourth)
            tail_stats(B - 1, 1, 3)

        @block.tensor
        def _(pe):
            def mm(out_, w, x, start, stop):
                return pe.matmul(out_, w, x, start=start, stop=stop)

            def mm3(out_, w, x, start, stop):
                pe.matmul(out_, w[0], x[0], start=start, stop=False)
                pe.matmul(out_, w[0], x[1], start=False, stop=False)
                return pe.matmul(out_, w[1], x[0], start=False, stop=stop)

            def turn4(dst, src):
                for c in range(C):
                    ins = pe.transpose(dst[:, c * P:(c + 1) * P], src[:, c * P:(c + 1) * P], ident[:])
                return ins

            def flat(t):
                return t[:].rearrange("p c d -> p (c d)")

            pe.wait_ge(s_w, 16 * N_WLOAD)
            pe.wait_ge(s_pre, 8 + 2)
            a34 = col[:, CI["l3_a1"]:CI["l3_a1"] + 2]
            mm(bank[7][:, 0:2], l2w[:], col[:, CI["a1"]:CI["a1"] + 2], True, True)
            mm(bank[7][:, 2:4], l3w[:], a34, True, True)
            mm(bank[7][:, 4:6], AT[:, 0, 0:P], a34, True, True).then_inc(s_prep, 1)
            pe.wait_ge(s_pre, PRE_STEPS)
            pe.wait_ge(s_half, 4)

            def aggregate(b):
                pe.wait_ge(s_adj, 16 * (b + 1))
                pe.wait_ge(s_x, 32 * (b + 1))
                for c in range(C):
                    ins = mm(bank[4][:], xk[:, c, :], adj[:, adj_slot(b), c, :], c == 0, c == C - 1)
                ins.then_inc(s_agg, 1)

            def hid(b):
                pe.wait_ge(s_h0p, 2 * (b + 1))
                if not (isinstance(b, int) and b == 0):
                    pe.wait_ge(s_msgb, b)
                for h in range(2):
                    hs = slice(h * D, (h + 1) * D)
                    mm3(bank[3 + h][:], [w[:, hs] for w in w1p], [x[:] for x in h0p], True, True).then_inc(s_hid, 1)

            def y_rows(b):
                pe.wait_ge(s_hidr, 2 * (b + 1))
                if not (isinstance(b, int) and b == 0):
                    pe.wait_ge(s_exp, C * (b - 1) + 1)
                for c in range(C):
                    for h in range(2):
                        ins = mm(bank[6][:, c * D:(c + 1) * D], hidT[:, h, c * P:(c + 1) * P], w2s[:, h, :],
                                 h == 0, h == 1)
                ins.then_inc(s_y, 1)

            def turn_x1(b):
                pe.wait_ge(s_ln1, C * (b + 1))
                turn4(bank[3], flat(yk)).then_inc(s_x1t, 1)

            def turn_v(b):
                pe.wait_ge(s_gru, 6 * (b + 1))
                turn4(bank[5], vT).then_inc(s_tv, 1)

            def turn_x2(b):
                pe.wait_ge(s_ln2, C * (b + 1))
                turn4(bank[5], flat(x2k)).then_inc(s_x2t, 1)

            def third_in(b):
                pe.wait_ge(s_x2T, b + 1)
                if isinstance(b, int) and b == B - 1:
                    pe.wait_ge(s_gh, B)
                else:
                    pe.wait_ge(s_exp, C * (b + 1) + 3)
                for c in range(C):
                    ins = mm(bank[7][:, c * D:(c + 1) * D], x2T[:, c * P:(c + 1) * P], l2wt[:], True, True)
                ins.then_inc(s_wh, 1)
                for c in range(C):
                    ins = mm(bank[1][:, 2 * c:2 * c + 2], x2T[:, c * P:(c + 1) * P], v12[:], True, True)
                ins.then_inc(s_e, 1)

            def iteration(t, p, first, last):
                xT1 = x1T[:, p, :]
                x1 = [x[:] for x in x1p[p]]
                pe.wait_ge(s_x1T, 2 * (t + 1))
                mm(bank[1][SE, :], wse[:], xT1, True, True).then_inc(s_s, 1)
                for c in range(C):
                    ins = mm(bank[3][:, c * D:(c + 1) * D], xT1[:, c * P:(c + 1) * P], wmsg[:], True, True)
                ins.then_inc(s_msg, 1)
                pe.wait_ge(s_x1l, t + 1)
                if not first:
                    pe.wait_ge(s_xnl, t)
                mm3(bank[2][:], [w[:] for w in conv1p], x1, True, True).then_inc(s_c1, 1)
                if not last:
                    if not first:
                        pe.wait_ge(s_tr, t)
                    aggregate(t + 1)
                if not first:
                    turn_v(t - 1)
                pe.wait_ge(s_c1l, t + 1)
                if not first:
                    pe.wait_ge(s_cvx, t)

                def conv(k0, k1):
                    for k in range(k0, k1):
                        ins = mm3(bank[0][:], [w[:, k, :] for w in conv2p], [x[:, k:k + N] for x in c1p],
                                  k == 0, k == TAPS - 1)
                    return ins

                conv(0, 7)
                if not first:
                    pe.wait_ge(s_gh, t)
                pe.wait_ge(s_slr, S_STEPS * (t + 1))
                for c in range(C):
                    mm(bank[DIST[c]][:], Lt[0:64, c * P:(c + 1) * P], Rt[0:64, :], True, True).then_inc(s_dist, 1)
                conv(7, 9)
                if not last:
                    hid(t + 1)
                conv(9, 13)
                if not last:
                    y_rows(t + 1)
                if not first:
                    turn_x2(t - 1)
                conv(13, TAPS).then_inc(s_cv, 1)
                if not first:
                    third_in(t - 1)
                pe.wait_ge(s_A, C * (t + 1))
                pe.wait_ge(s_msgr, t + 1)
                for c in range(C):
                    ins = mm(bank[2][:], msg[:, c, :], AT[:, c, :], c == 0, c == C - 1)
                ins.then_inc(s_nmp, 1)
                if not last:
                    turn_x1(t + 1)
                if not first:
                    pe.wait_ge(s_whk, t)
                    pe.wait_ge(s_x2T, t)
                else:
                    pe.wait_ge(s_exp, C)
                mm3(bank[7][:], [w[:, 2 * D:3 * D] for w in whhp], x1, True, True).then_inc(s_gate, 1)
                if not last:
                    pe.wait_ge(s_hidr, 2 * (t + 2))
                    pe.wait_ge(s_ysb, t + 2)

                def gate_part(g, w, x, start, stop):
                    gs = slice(g * D, (g + 1) * D)
                    return mm3(bank[4 + g][:], [v[:, gs] for v in w], x, start, stop)

                for g in range(2):
                    gate_part(g, whhp, x1, True, False)
                pe.wait_ge(s_xcl, t + 1)
                for g in range(3):
                    gate_part(g, [w[:, 0, :] for w in wihp], [x[:] for x in xcp], g == 2, False)
                pe.wait_ge(s_xnl, t + 1)
                for g in range(3):
                    gate_part(g, [w[:, 1, :] for w in wihp], [x[:] for x in xnp_], False, True).then_inc(s_gate, 1)

            aggregate(0)
            pe.wait_ge(s_split, 2 * len(SPLITS))
            hid(0)
            y_rows(0)
            turn_x1(0)
            iterations(pe, iteration)
            turn_v(B - 1)
            turn_x2(B - 1)
            third_in(B - 1)

            pe.wait_ge(s_ps, 2)
            mm(bank[1][:, 0:B * C], ones[:], e1[:], True, True).then_inc(s_mbp, 1)
            pe.transpose(bank[0][0:B * C, 0:P], e1[:], ident[:]).then_inc(s_ET, 1)
            pe.wait_ge(s_ps, 9)
            mm(bank[2][:, 0:B * C], ones[:], e1c[:], True, True).then_inc(s_vp, 1)

            def third_turn(t, first):
                if not first:
                    pe.wait_ge(s_ex, C * t)
                for k in range(C):
                    pe.wait_ge(s_z, C * t + k + 1)
                    for c in range(C):
                        ins = pe.transpose(bank[c][:, k * P:(k + 1) * P], zT[:, k, c * P:(c + 1) * P], ident[:])
                        if k == C - 1:
                            ins.then_inc(s_zt, 1)

            def third_turn_back(t):
                for c in range(C):
                    if c == 3:
                        pe.wait_ge(s_pa, C * t + 1)
                    for k in range(C):
                        if c == 0:
                            pe.wait_ge(s_dg, C * t + k + 1)
                        ins = mm(bank[PB[c]][:, k * P:(k + 1) * P], PTs[k][:, c * P:(c + 1) * P],
                                 diag[:, k * P:(k + 1) * P], True, True)
                    ins.then_inc(s_pt, 1)

            def third_product(t, first):
                pe.wait_ge(s_whl, 16 * (t + 1))
                if not first:
                    pe.wait_ge(s_hpe, t)
                for c in range(C):
                    pe.wait_ge(s_pa, C * t + c + 1)
                    ins = mm(bank[7][:], whk[:, c, :], PA[c], c == 0, c == C - 1)
                ins.then_inc(s_hp, 1)

            third_turn(0, True)
            third_turn_back(0)
            third_turn(1, False)
            third_product(0, True)
            with pe.Fori(1, B - 1) as t:
                third_turn_back(t)
                third_turn(t + 1, False)
                third_product(t, False)
            third_turn_back(B - 1)
            third_product(B - 1, False)

            def head_turn(b, first):
                pe.wait_ge(s_el, b + 1)
                if not first:
                    pe.wait_ge(s_y3, b)
                turn4(bank[0], elT).then_inc(s_et, 1)

            def head_turn_x3(b, p):
                pe.wait_ge(s_ln3, C * (b + 1))
                turn4(bank[1], x3k[p][:, :, :].rearrange("p c d -> p (c d)")).then_inc(s_x3t, 1)

            def head_ef(b):
                pe.wait_ge(s_x3T, b + 1)
                if not (isinstance(b, int) and b == 0):
                    pe.wait_ge(s_efx, 2 * b)
                for c in range(C):
                    ins = mm(bank[7][:, 2 * c:2 * c + 2], x3T[:, c * P:(c + 1) * P], v34[:], True, True)
                ins.then_inc(s_e3, 1)

            def head_h(b):
                if not (isinstance(b, int) and b == 0):
                    pe.wait_ge(s_g, C * b)
                for c in range(C):
                    mm(bank[2][:, c * D:(c + 1) * D], x3T[:, c * P:(c + 1) * P], l3wt[:], True, False)
                    ins = mm(bank[2][:, c * D:(c + 1) * D], ones[0:1, :], row[0:1, RI["W_b"], :], False, True)
                ins.then_inc(s_h3, 1)

            def tail_den(t, age):
                pe.wait_ge(s_den, C * (t + 1))
                if age:
                    pe.wait_ge(s_y4, C * t)
                for c in range(C):
                    ins = mm(bank[6][:, c:c + 1], den[:, c * P:(c + 1) * P], ones[:, 0:1], True, True)
                ins.then_inc(s_dt, 1)

            def tail_num(t, c0, c1):
                for c in range(c0, c1):
                    ins = mm(bank[3][:], gB[:, c, :], adj[:, t, c, :], c == 0, c == C - 1)
                return ins

            def fourth(t, p, age, left):
                if left > 1:
                    head_turn(t + 2, False)
                pe.wait_ge(s_g, C * (t + 1))
                if age:
                    pe.wait_ge(s_numc, t)
                tail_num(t, 0, 2)
                if left > 0:
                    head_turn_x3(t + 1, 1 - p)
                tail_num(t, 2, C).then_inc(s_num, 1)
                if left > 0:
                    head_ef(t + 1)
                    head_h(t + 1)
                tail_den(t, age)
                pe.wait_ge(s_numc, t + 1)
                turn4(bank[5], numT).then_inc(s_nt, 1)

            head_turn(0, True)
            head_turn(1, False)
            head_turn_x3(0, 0)
            head_ef(0)
            head_h(0)
            last_layer(pe, fourth)


def s_columns(w_se):
    out = np.zeros((w_se.shape[1], 64), w_se.dtype)
    for block in (0, 32):
        for m in range(12):
            out[:, block + m] = w_se[m % 3]
    return out


def distance_rows(b_se, factors):
    out = np.zeros((64, 7), b_se.dtype)
    for block in (0, 32):
        for m in range(12):
            out[block + m, 0] = b_se[m % 3]
    out[:, 1:] = factors
    return out


def kernel(**inputs):
    import concourse.bacc as bacc
    from concourse.bass_utils import run_bass_kernel_spmd

    a = {k: np.asarray(v) for k, v in inputs.items()}
    factors = np.zeros((64, 6), np.float32)
    for d in range(3):
        for part in range(4):
            factors[3 * part + d] = [part % 2 == 0, part % 2, 0, 2 * (part < 2), 2 * (part > 1), 0]
        for part in range(2):
            factors[32 + 3 * part + d] = [part == 0, part, 0, 0, 0, -1]
            factors[38 + 3 * part + d] = [0, 0, -1, part == 0, part, 0]
    B, N, D = a["x"].shape

    def parts(v, n):
        return [v[i * P:(i + 1) * P] for i in range(n)]

    cols = {"g3": a["L2_gnn_g3"], "b3": a["L2_gnn_b3"], "a1": a["L2_gnn_a1"], "a2": a["L2_gnn_a2"],
            "l3_a1": a["L3_gnn_a_w"][:D], "l3_a2": a["L3_gnn_a_w"][D:], "W_b": a["L3_gnn_W_b"]}
    for i, v in enumerate(parts(a["L0_gnn_b1"], 2)):
        cols[f"b1_{i}"] = v
    for k in ("bn1", "bn2"):
        for s in "gbmv":
            cols[f"{k}_{s}"] = a[f"L1_gnn_{k}_{s}"]
    for k in ("b_ih", "b_hh"):
        for g, v in zip("rzn", parts(a[f"L1_gnn_{k}"], 3)):
            cols[f"{k}_{g}"] = v
    for new, old in (("g1", "g1"), ("be1", "b1"), ("g2", "g2"), ("be2", "b2")):
        for i, v in enumerate(parts(a[f"L2_gnn_{old}"], N // P)):
            cols[f"{new}_{i}"] = v
    arrays = {
        "x_tok": a["x"], "x_fm": a["x"].transpose(0, 2, 1), "adj_t": a["adj"].transpose(0, 2, 1),
        "w1": a["L0_gnn_W1"], "w2": a["L0_gnn_W2"],
        "cols": np.stack([cols[c] for c in COLS], axis=1),
        "rows": np.stack([a["L0_gnn_b2"], a["L1_gnn_b_msg"], a["L3_gnn_W_b"]]),
        "scal": np.concatenate([a["L0_gnn_eps"], a["L3_gnn_a_b"]]),
        "masks": distance_rows(a["L1_gnn_b_se"], factors), "w_se": s_columns(a["L1_gnn_w_se"]),
        "conv1": a["L1_gnn_conv1_w"][:, :, 0].T, "conv2": a["L1_gnn_conv2_w"].transpose(1, 2, 0),
        "w_msg": a["L1_gnn_w_msg"].T, "w_ih": a["L1_gnn_w_ih"].T, "w_hh": a["L1_gnn_w_hh"].T,
        "l2_w": a["L2_gnn_W"], "l2_wt": a["L2_gnn_W"].T, "l3_w": a["L3_gnn_W_w"], "l3_wt": a["L3_gnn_W_w"].T,
        "ident_in": np.eye(P, dtype=np.float32),
    }
    arrays = {k: np.ascontiguousarray(v) for k, v in arrays.items()}
    nc = bacc.Bacc("TRN2", target_bir_lowering=False, num_devices=1)
    args = [nc.dram_tensor(k, v.shape, mybir.dt.from_np(v.dtype), kind="ExternalInput").ap()
            for k, v in arrays.items()]
    out = nc.dram_tensor("out", (B, N, D), F32, kind="ExternalOutput").ap()
    build(nc, *args, out)
    r = run_bass_kernel_spmd(nc, [arrays], core_ids=[0])
    return r.results[0]["out"]
```

```python
from contextlib import ExitStack

import numpy as np
import concourse.bass as bass
from concourse import mybir

P = 128
ALU = mybir.AluOpType
ACT = mybir.ActivationFunctionType
AX = mybir.AxisListType
F32 = mybir.dt.float32
F32R = mybir.dt.float32r
I32 = mybir.dt.int32

LN_EPS = 1e-5
SLOPE = 0.2
RSQRT_MAGIC = float(0x5F3759DF)
RSQRT_STEPS = 11
STAT_STEPS = 4 + 1 + 4 + 3
ROOT_STEPS = 12

COLS = ["b1_0", "b1_1", "bn1_v", "bn2_v", "bn1_g", "bn2_g", "bn1_m", "bn2_m", "bn1_b", "bn2_b",
        "b_ih_r", "b_ih_z", "b_ih_n", "b_hh_r", "b_hh_z", "b_hh_n", "g3", "b3", "a1", "a2", "l3_a1", "l3_a2", "W_b",
        "g1_0", "g1_1", "g1_2", "g1_3", "be1_0", "be1_1", "be1_2", "be1_3",
        "g2_0", "g2_1", "g2_2", "g2_3", "be2_0", "be2_1", "be2_2", "be2_3"]
CI = {n: i for i, n in enumerate(COLS)}
ROWS = ["b2", "b_msg", "W_b"]
RI = {n: i for i, n in enumerate(ROWS)}


class Steps:

    def __init__(self, eng, sem, b, per_batch):
        self.eng, self.sem, self.base, self.per, self.k = eng, sem, b * per_batch, per_batch, 0

    def did(self, ins):
        ins.then_inc(self.sem, 1)
        self.k += 1

    def wait(self):
        self.eng.wait_ge(self.sem, self.base + self.k)

    def end(self):
        assert self.k == self.per, (self.k, self.per)


class NormTiles:

    def __init__(self, bn, mv, v, y, h, a):
        self.bn, self.mv, self.v, self.y, self.h, self.a = bn, mv, v, y, h, a


def rsqrt(eng, st, v, y, tmp, var, eps):
    st.did(eng.tensor_scalar(v, var, eps, None, ALU.add))
    st.wait()
    st.did(eng.tensor_scalar(y.bitcast(I32), v.bitcast(I32), -0.5, RSQRT_MAGIC, ALU.mult, ALU.add))
    for _ in range(3):
        st.wait()
        st.did(eng.scalar_tensor_tensor(out=tmp, in0=y, scalar=-0.5, in1=y, op0=ALU.mult, op1=ALU.mult))
        st.wait()
        st.did(eng.tensor_tensor(tmp, tmp, v, ALU.mult))
        st.wait()
        st.did(eng.scalar_tensor_tensor(out=y, in0=tmp, scalar=1.5, in1=y, op0=ALU.add, op1=ALU.mult))
    st.wait()


def norm_stats(eng, st, src, t):
    for c in range(4):
        st.did(eng.bn_stats(t.bn[:, c, :], src[:, c, :]))
    st.wait()
    st.did(eng.memset(t.v[:, 0:1], 0.0))
    for c in range(4):
        st.did(eng.bn_aggr(t.mv[:, c, :], t.bn[:, c, :]))
    st.wait()
    st.did(eng.tensor_scalar(t.v[:, :], t.mv[:, :, 1], LN_EPS, None, ALU.add))
    st.wait()
    st.did(eng.tensor_scalar(t.y[:, :].bitcast(I32), t.v[:, :].bitcast(I32), -0.5, RSQRT_MAGIC, ALU.mult, ALU.add))
    st.did(eng.tensor_scalar(t.h[:, :], t.v[:, :], -0.5, None, ALU.mult))
    st.end()


def norm_root(pool, st, t, c15):
    for i in range(3):
        if i:
            st.wait()
        st.did(pool.tensor_tensor(t.a[:, :], t.y[:, :], t.y[:, :], ALU.mult))
        st.wait()
        st.did(pool.tensor_tensor(t.a[:, :], t.a[:, :], t.h[:, :], ALU.mult))
        st.wait()
        st.did(pool.tensor_tensor(t.a[:, :], t.a[:, :], c15[:, :], ALU.add))
        st.wait()
        st.did(pool.tensor_tensor(t.y[:, :], t.y[:, :], t.a[:, :], ALU.mult))


def norm_shift(pool, st, t, zero):
    st.wait()
    st.did(pool.tensor_tensor(t.a[:, :], t.mv[:, :, 0], t.y[:, :], ALU.mult))
    st.wait()
    st.did(pool.tensor_tensor(t.h[:, :], zero[:, :], t.a[:, :], ALU.subtract))
    st.end()


def norm_apply(eng, sem, dst, src, t):
    for c in range(4):
        eng.tensor_scalar(dst[:, c, :], src[:, c, :], t.mv[:, c, 0:1], t.y[:, c:c + 1],
                          ALU.subtract, ALU.mult).then_inc(sem, 1)


def build(nc, x_tok, x_fm, adj_t, w1, w2, cols, rows, scal, masks, w_se, conv1, conv2, w_msg, w_ih, w_hh,
          l2_w, l2_wt, l3_w, l3_wt, ident_in, out):
    B, N, D = x_tok.shape
    C = N // P
    TAPS = conv2.shape[1]
    PAD = TAPS // 2
    BN = B * N
    PAIRS = TAPS // 2
    M = N // 2
    L = M + PAD

    with ExitStack() as ctx:
        def sb(name, shape, dt=F32):
            return ctx.enter_context(nc.sbuf_tensor(name, shape, dt))

        def sem(name):
            return ctx.enter_context(nc.semaphore(name))

        x2_dram = nc.dram_tensor("x2_dram", (B, P, C * D), F32).ap()
        wh_dram = nc.dram_tensor("wh_dram", (B, P, C * D), F32).ap()
        hp_dram = nc.dram_tensor("hp_dram", (B, P, N), F32).ap()
        ei_dram = nc.dram_tensor("ei_dram", (B, 1, N), F32).ap()

        bank = [ctx.enter_context(nc.psum_tensor(f"bank{i}", [P, 512], F32)) for i in range(8)]

        def tok(t):
            return t[:, :].rearrange("p (c d) -> p c d", c=C)

        def pair(name, shape):
            return tmp.enter_context(nc.sbuf_tensor(name + "_hi", shape, F32R)), \
                tmp.enter_context(nc.sbuf_tensor(name + "_lo", shape, F32R))

        with ExitStack() as tmp:
            w1p = pair("w1", [P, 2 * D])
            conv1p = pair("conv1", [P, D])
            conv2p = pair("conv2", [P, TAPS + PAIRS, D])
            wihp = pair("wih", [P, 2, 3 * D])
            whhp = pair("whh", [P, 3 * D])
            w2s = tmp.enter_context(nc.sbuf_tensor("w2s", [P, 2, D], F32))
            wmsg = tmp.enter_context(nc.sbuf_tensor("wmsg", [P, D], F32))
        WSLOTS = 5
        RING = B - WSLOTS

        def adj_slot(b):
            return (b + RING - WSLOTS) % RING + WSLOTS

        adj = sb("adj", [P, B, C, N])

        with ExitStack() as tmp:
            h0p = pair("h0", [P, N])
            x1p = [pair(f"x1_{i}", [P, N]) for i in range(2)]
            c1p = pair("c1", [P, 3, L])
            xcp = pair("xc", [P, N])
            xnp_ = pair("xn", [P, N])
        zT = sb("zT", [P, C, N])
        PTs = [sb(f"PT{i}", [P, N]) for i in range(C)]
        ebc = [sb(f"ebc{i}", [P, N]) for i in range(2)]
        outk_ = sb("outk", [P, C, D])
        st2_ = sb("st2", [P, C, B, 6])
        ET = sb("ET", [B * C, P])
        e1c = sb("e1c", [P, B * C])
        dj = sb("dj", [P, C, B])
        djq = sb("djq", [P, C, B])
        t1 = sb("t1", [P, C, B])
        tt1 = sb("tt1", [P, B, C])
        tt1k = sb("tt1k", [P, 2, B, C])
        st3 = sb("st3", [P, B, 6])
        e1 = sb("e1", [P, B * C])
        ejT = sb("ejT", [P, C, B])
        xk = sb("xk", [P, C, D])
        xT = sb("xT", [P, N])
        col = sb("col", [P, len(COLS)])
        row = sb("row", [P, len(ROWS), D])
        sc = sb("sc", [P, 2])
        l2w = sb("l2w", [P, D])
        l2wt = sb("l2wt", [P, D + 2])
        l3w = sb("l3w", [P, D])
        l3wt = sb("l3wt", [P, D])
        ident = sb("ident", [P, P])
        ones = sb("ones", [P, P])

        eps1 = sb("eps1", [P, 1])
        bnv = sb("bnv", [P, 2])
        bnr = sb("bnr", [P, 2])
        bnt = sb("bnt", [P, 2])
        bnsc = sb("bnsc", [P, 2])
        bnbi = sb("bnbi", [P, 2])
        half_b = sb("half_b", [P, 2])
        v34 = sb("v34", [P, 2])
        ec = sb("ec", [P, 2])

        wse = sb("wse", [P, 64])
        mask = sb("mask", [P, 7])
        Sx = sb("Sx", [P, N])
        Rt = sb("Rt", [P, N], F32R)
        Lt = sb("Lt", [P, N], F32R)

        hidT = sb("hidT", [P, 2, N])
        yk = sb("yk", [P, C, D])
        x1T = sb("x1T", [P, 2, N])
        zero = sb("zero", [P, 1])
        gate = sb("gate", [P, 1])
        msg = sb("msg", [P, C, D])
        AT = sb("AT", [P, C, N])
        trT = sb("trT", [P, N])
        tzT = sb("tzT", [P, N])
        ghT = sb("ghT", [P, N])
        nT = sb("nT", [P, N])
        x2k = sb("x2k", [P, C, D])
        c1w = sb("c1w", [P, N + 2 * PAD])
        x2T = c1w[:, PAD:PAD + N]
        whk = sb("whk", [P, C, D])
        E12 = sb("E12", [P, B, C, 2])
        c15 = sb("c15", [P, C])
        zero4 = sb("zero4", [P, C])

        def norm_tiles(name):
            return NormTiles(bn=sb(name + "_bn", [P, C, 6]), mv=sb(name + "_mv", [P, C, 2]),
                             v=sb(name + "_v", [P, C]), y=sb(name + "_y", [P, C]),
                             h=sb(name + "_h", [P, C]), a=sb(name + "_a", [P, C]))

        na = norm_tiles("na")
        nb = norm_tiles("nb")
        lv = sb("lv", [P, C])
        lr = sb("lr", [P, C])
        lt = sb("lt", [P, C])

        mb = sb("mb", [P, B])
        mtot = sb("mtot", [P, 1])
        vare = sb("vare", [P, 1])
        mbc = sb("mbc", [P, B])
        mj = sb("mj", [P, C])
        vj = sb("vj", [P, C])
        s1 = sb("s1", [P, C])
        s1k = sb("s1k", [P, 2, C])
        st2 = st2_
        mv2 = sb("mv2", [P, C, 2])
        c2 = sb("c2", [P, C])
        d2 = sb("d2", [P, C])
        mv3 = sb("mv3", [P, 2])
        a3 = sb("a3", [P, 4])
        nmax = sb("nmax", [P, C])
        rsum = sb("rsum", [P, C])
        rrec = sb("rrec", [P, C])

        h0T = x2T
        c1d = hidT[:, :, 0:L]
        xcT = trT
        vT = ghT
        LT = AT
        hpT = nT
        diag = tzT
        LR = hidT
        SE = slice(64, P)

        s_w = sem("s_w")
        s_adj = sem("s_adj")
        s_adj2 = sem("s_adj2")
        s_w2 = sem("s_w2")
        s_w3 = sem("s_w3")
        s_split = sem("s_split")
        s_x = sem("s_x")
        s_pre = sem("s_pre")
        s_prep = sem("s_prep")
        s_half = sem("s_half")
        s_agg = sem("s_agg")
        s_h0 = sem("s_h0")
        s_hid = sem("s_hid")
        s_hidr = sem("s_hidr")
        s_y = sem("s_y")
        s_xb = sem("s_xb")
        s_ysb = sem("s_ysb")
        s_ln1 = sem("s_ln1")
        s_st = {n: sem(f"s_stat{n}") for n in (1, 2, 3, 4)}
        s_rt = {n: sem(f"s_root{n}") for n in (1, 2, 3, 4)}
        s_x1t = sem("s_x1t")
        s_x1T = sem("s_x1T")
        s_s = sem("s_s")
        s_srow = sem("s_srow")
        s_slr = sem("s_slr")
        s_c1 = sem("s_c1")
        s_c1T = sem("s_c1T")
        s_c1l = sem("s_c1l")
        s_x1l = sem("s_x1l")
        s_h0p = sem("s_h0p")
        s_xcl = sem("s_xcl")
        s_xnl = sem("s_xnl")
        s_msg = sem("s_msg")
        s_msgb = sem("s_msgb")
        s_msgr = sem("s_msgr")
        s_dist = sem("s_dist")
        s_exp = sem("s_exp")
        s_A = sem("s_A")
        s_cv = sem("s_cv")
        s_cvx = sem("s_cvx")
        s_xc = sem("s_xc")
        s_nmp = sem("s_nmp")
        s_xn = sem("s_xn")
        s_gate = sem("s_gate")
        s_gh = sem("s_gh")
        s_tr = sem("s_tr")
        s_tz = sem("s_tz")
        s_gru = sem("s_gru")
        s_n = sem("s_n")
        s_tv = sem("s_tv")
        s_ln2 = sem("s_ln2")
        s_x2t = sem("s_x2t")
        s_x2T = sem("s_x2T")
        s_wh = sem("s_wh")
        s_whk = sem("s_whk")
        s_ec = sem("s_ec")
        s_x2st = sem("s_x2st")
        s_whst = sem("s_whst")

        DIST = [1, 6, 7, 2]
        STAT3 = 1 + RSQRT_STEPS + 4
        STAT1 = 22 + RSQRT_STEPS + 4
        LB = 2 + 2 * 2
        TURNS = (2, 3, 0, 1)
        PB = [4, 5, 6, 4]
        PA = [yk[:].rearrange("p c d -> p (c d)"), x2k[:].rearrange("p c d -> p (c d)"), x1T[:, 0, :], x1T[:, 1, :]]

        block = ctx.enter_context(nc.Block())
        WEIGHT_LOADS = 13
        PRE_STEPS = 6 + 3 + RSQRT_STEPS + 4
        GATES = 4
        S_STEPS = 7

        def iterations(eng, iteration):
            iteration(0, 0, True, False)
            with eng.Fori(0, (B - 2) // 2) as i:
                iteration(i * 2 + 1, 1, False, False)
                iteration(i * 2 + 2, 0, False, False)
            iteration(B - 1, 1, False, True)

        def last_layer(eng, iteration):
            for t in range(3):
                iteration(t, t % 2, t, 4)
            with eng.Fori(0, (B - 8) // 2) as i:
                iteration(i * 2 + 3, 1, 3, 4)
                iteration(i * 2 + 4, 0, 3, 4)
            for t in range(B - 5, B):
                iteration(t, t % 2, 3, B - 1 - t)

        s_ET = sem("s_ET")
        s_ETc = sem("s_ETc")
        s_eist = sem("s_eist")
        s_mbp = sem("s_mbp")
        s_ps = sem("s_ps")
        s_vp = sem("s_vp")
        s_ebc = sem("s_ebc")
        s_lB = sem("s_lB")
        s_bB = sem("s_bB")
        s_mB = sem("s_mB")
        s_aB = sem("s_aB")
        s_mC = sem("s_mC")
        s_st2 = sem("s_st2")
        s_ebcC = sem("s_ebcC")
        s_whl = sem("s_whl")
        s_lC = sem("s_lC")
        s_aC = sem("s_aC")
        s_z = sem("s_z")
        s_zt = sem("s_zt")
        s_mx = sem("s_mx")
        s_ex = sem("s_ex")
        s_rr = sem("s_rr")
        s_dg = sem("s_dg")
        s_pt = sem("s_pt")
        s_pa = sem("s_pa")
        s_hp = sem("s_hp")
        s_hpe = sem("s_hpe")
        s_hps = sem("s_hps")
        s_hpst = sem("s_hpst")
        s_st3 = sem("s_st3")
        s_hl = sem("s_hl")
        s_x2l = sem("s_x2l")
        s_elu = sem("s_elu")
        s_el = sem("s_el")
        s_et = sem("s_et")
        s_y3 = sem("s_y3")
        s_ln3 = sem("s_ln3")
        s_x3t = sem("s_x3t")
        s_x3T = sem("s_x3T")
        s_h3 = sem("s_h3")
        s_e3 = sem("s_e3")
        s_efx = sem("s_efx")
        s_g = sem("s_g")
        s_num = sem("s_num")
        s_den = sem("s_den")
        s_numc = sem("s_numc")
        s_nt = sem("s_nt")
        s_dt = sem("s_dt")
        s_wr = sem("s_wr")
        s_y4 = sem("s_y4")
        s_ln4 = sem("s_ln4")
        s_out = sem("s_out")
        s_on = sem("s_on")

        hT, x2l, elT, pT4, eT4, y3 = xT, xk, hidT[:, 0, :], hidT[:, 1, :], zT[:, 0, :], [yk[:], tok(Sx)]
        x3T = x1T[:, 0, :]
        den = msg[:].rearrange("p c d -> p (c d)")
        gB = whk
        numT = x1T[:, 1, :]
        fx = sb("fx", [P, 2, 2, C])
        fw = sb("fw", [P, 3, C])
        y4 = [AT[:, i, :].rearrange("p (c d) -> p c d", c=C) for i in (1, 3)]
        outk = outk_[:, :, :]
        x3k = [x2k, AT[:, 2, :].rearrange("p (c d) -> p c d", c=C)]

        def raw(at, n):
            return adj[:, WSLOTS:WSLOTS + 3].rearrange("p s c n -> p (s c n)")[:, at:at + n]

        SPLITS = ((w1p, 0), (conv2p, 12 * D), (conv1p, 2 * D), (whhp, 3 * D), (wihp, 6 * D))
        N_SPLIT = 2 * len(SPLITS) + 1

        def c1_phases():
            by_parity = c1w[:, :].rearrange("p (m r) -> p m r", r=2)
            return by_parity[:, :, 0], by_parity[:, :, 1], by_parity[:, 1:L, 0]

        def wh_psum(c):
            return bank[7][:, c * (D + 2):(c + 1) * (D + 2)] if c < C - 1 else bank[1][:, 0:D + 2]

        def by_parity(t):
            return t.rearrange("p (m r) -> p r m", r=2)

        def flat_of(t):
            return t[:, :] if len(t.shape) == 2 else t[:, :, :].rearrange("p a b -> p (a b)")

        def hi_size(t):
            return int(np.prod(t.shape[1:]))

        @block.sync
        def _(sp):
            def load_adj(b):
                sp.dma_start(adj[:, adj_slot(b)], adj_t[b].rearrange("(c p) i -> p c i", p=P)).then_inc(s_adj, 16)

            def load_x(b):
                sp.dma_start(xk[:], x_tok[b].rearrange("(c p) d -> p c d", p=P)).then_inc(s_x, 16)
                sp.dma_start(xT[:], x_fm[b]).then_inc(s_x, 16)

            load_x(0)
            load_adj(0)

            for dst, src in ((col[:], cols), (sc[:, :], scal.rearrange("(a r) -> a r", a=1).broadcast_to((P, 2))),
                             (raw(0, 2 * D), w1), (l2w[:], l2_w), (l3w[:], l3_w), (ident[:], ident_in),
                             (w2s[:], w2.rearrange("(h p) d -> p h d", p=P)),
                             (row[:, :, :], rows.rearrange("(a r) d -> a r d", a=1).broadcast_to((P, len(ROWS), D))),
                             (mask[SE, :], masks), (wse[:], w_se), (wmsg[:], w_msg),
                             (l2wt[:, 0:D], l2_wt), (l3wt[:], l3_wt)):
                sp.dma_start(dst, src).then_inc(s_w, 16)
            sp.dma_start(raw(12 * D, TAPS * D).rearrange("p (k d) -> p k d", d=D), conv2).then_inc(s_w2, 16)
            for dst, src in ((raw(2 * D, D), conv1), (raw(3 * D, 3 * D), w_hh),
                             (raw(6 * D, 6 * D).rearrange("p (q g) -> p q g", q=2),
                              w_ih.rearrange("(q p) g -> p q g", p=P))):
                sp.dma_start(dst, src).then_inc(s_w3, 16)
            sp.wait_ge(s_adj, 16)
            load_adj(1)

            def store_x2(b):
                sp.wait_ge(s_ln2, C * (b + 1))
                sp.dma_start(x2_dram[b], x2k[:].rearrange("p c d -> p (c d)")).then_inc(s_x2st, 16)

            def store_wh(b):
                sp.wait_ge(s_whk, 2 * (b + 1))
                sp.dma_start(wh_dram[b], whk[:].rearrange("p c d -> p (c d)")).then_inc(s_whst, 16)

            def sp_iteration(t, p, first, last):
                if not last:
                    sp.wait_ge(s_ysb, t + 1)
                    load_x(t + 1)
                if first:
                    sp.wait_ge(s_split, N_SPLIT)
                if not first:
                    if not last:
                        sp.wait_ge(s_adj, 16 * (t + 1))
                        load_adj(t + 1)
                    store_x2(t - 1)
                    store_wh(t - 1)

            iterations(sp, sp_iteration)
            store_x2(B - 1)
            store_wh(B - 1)

            sp.wait_ge(s_ETc, 1)
            sp.dma_start(ei_dram.rearrange("b a (c p) -> (b a c) p", p=P), ET[:]).then_inc(s_eist, 16)
            sp.wait_ge(s_eist, 16)
            sp.wait_ge(s_whst, 16 * B)
            sp.wait_ge(s_x2st, 16 * B)

            def load_ebc(b, p, s):
                sp.dma_start(ebc[p][:], ei_dram[b].broadcast_to((P, N))).then_inc(s, 16)

            load_ebc(0, 0, s_ebc)
            sp.wait_ge(s_ebc, 16)
            load_ebc(1, 1, s_ebc)

            def load_ebc_pair(b):
                for p in range(2):
                    sp.wait_ge(s_lB, LB * (b + p - 1))
                    sp.wait_ge(s_ebc, 16 * (b + p))
                    load_ebc(b + p, p, s_ebc)

            sp.wait_ge(s_gate, GATES * B)
            with sp.Fori(0, WSLOTS) as i:
                load_ebc_pair(i * 2 + 2)
                sp.dma_start(adj[:, i], adj_t[i].rearrange("(c p) i -> p c i", p=P)).then_inc(s_adj2, 16)
            with sp.Fori(WSLOTS, (B - 2) // 2) as i:
                load_ebc_pair(i * 2 + 2)

            sp.wait_ge(s_lB, LB * B)
            load_ebc(0, 0, s_ebcC)
            sp.dma_start(whk[:].rearrange("p c d -> p (c d)"), wh_dram[0]).then_inc(s_whl, 16)
            sp.wait_ge(s_ebcC, 16)
            load_ebc(1, 1, s_ebcC)

            def load_ebc_again(b, p):
                sp.wait_ge(s_lC, LB * (b - 1))
                sp.wait_ge(s_ebcC, 16 * b)
                load_ebc(b, p, s_ebcC)

            load_ebc_again(2, 0)

            def third(t, p, more):
                if more > 1:
                    load_ebc_again(t + 3, 1 - p)
                sp.wait_ge(s_hpe, t + 1)
                sp.dma_start(hp_dram[t], hpT[:]).then_inc(s_hpst, 16)
                if more > 0:
                    sp.dma_start(whk[:].rearrange("p c d -> p (c d)"), wh_dram[t + 1]).then_inc(s_whl, 16)

            with sp.Fori(0, (B - 4) // 2) as i:
                third(i * 2, 0, 2)
                third(i * 2 + 1, 1, 2)
            third(B - 4, 0, 2)
            third(B - 3, 1, 1)
            third(B - 2, 0, 1)
            third(B - 1, 1, 0)

            sp.wait_ge(s_hpst, 16 * B)

            def load_h(b):
                if not (isinstance(b, int) and b == 0):
                    sp.wait_ge(s_elu, 3 * b)
                sp.dma_start(hT[:], hp_dram[b]).then_inc(s_hl, 16)

            def load_x2(b):
                if not (isinstance(b, int) and b == 0):
                    sp.wait_ge(s_y3, b)
                sp.dma_start(x2l[:].rearrange("p c d -> p (c d)"), x2_dram[b]).then_inc(s_x2l, 16)

            def fourth(t, p, age, left):
                if left > 2:
                    load_x2(t + 3)
                if left > 3:
                    load_h(t + 4)
                if age > 1:
                    store_out(t - 2)

            def store_out(b):
                sp.wait_ge(s_ln4, C * (b + 1))
                sp.dma_start(out[b].rearrange("(c p) d -> p c d", p=P), outk).then_inc(s_out, 16)

            for b in range(3):
                load_h(b)
                load_x2(b)
            load_h(3)
            last_layer(sp, fourth)
            store_out(B - 2)
            store_out(B - 1)
            sp.wait_ge(s_out, 16 * B)

        @block.gpsimd
        def _(pool):
            pool.wait_ge(s_w, 16 * WEIGHT_LOADS)

            pool.wait_ge(s_pre, PRE_STEPS)

            def make_xb(b):
                pool.wait_ge(s_x, 32 * (b + 1))
                pool.wait_ge(s_agg, b + 1)
                pool.tensor_tensor(xk[:], xk[:], row[:, RI["b2"]:RI["b2"] + 1, :].broadcast_to((P, C, D)),
                                   ALU.add).then_inc(s_xb, 1)

            def x1_low(b, p):
                pool.wait_ge(s_x1T, 2 * (b + 1))
                pool.tensor_tensor(x1p[p][1][:], x1T[:, p, :], x1p[p][0][:].bitcast(F32),
                                   ALU.subtract).then_inc(s_x1l, 1)

            def c1_low(b):
                pool.wait_ge(s_c1T, 4 * b + 1)
                even, odd, later = c1_phases()
                pool.tensor_tensor(c1d[:, 0, 0:L], even, odd, ALU.subtract).then_inc(s_c1l, 1)
                pool.tensor_tensor(c1d[:, 1, 0:L - 1], later, odd[:, 0:L - 1], ALU.subtract).then_inc(s_c1l, 1)
                for k, (whole, n) in enumerate(((c1d[:, 0, :], L), (c1d[:, 1, :], L - 1), (odd, L))):
                    pool.wait_ge(s_c1T, 4 * b + k + 2)
                    pool.tensor_tensor(c1p[1][:, k, 0:n], whole[:, 0:n], c1p[0][:, k, 0:n].bitcast(F32),
                                       ALU.subtract).then_inc(s_c1l, 1)

            def relu_msg(b):
                pool.wait_ge(s_msgb, b + 1)
                pool.tensor_tensor(gate[:], zero[:], zero[:], ALU.add)
                pool.tensor_scalar(msg[:], msg[:], 0.0, None, ALU.max).then_inc(s_msgr, 1)

            def root(n, b, tiles):
                pool.wait_ge(s_st[n], STAT_STEPS * (b + 1))
                st = Steps(pool, s_rt[n], b, ROOT_STEPS)
                norm_root(pool, st, tiles, c15)
                st.end()

            def root_shift(b):
                pool.wait_ge(s_st[4], STAT_STEPS * (b + 1))
                st = Steps(pool, s_rt[4], b, ROOT_STEPS + 2)
                norm_root(pool, st, nb, c15)
                norm_shift(pool, st, nb, zero4)

            def iteration(t, p, first, last):
                c1_low(t)
                if not first:
                    root(2, t - 1, nb)
                relu_msg(t)
                if not last:
                    make_xb(t + 1)
                    root(1, t + 1, na)
                    x1_low(t + 1, 1 - p)

            make_xb(0)
            root(1, 0, na)
            x1_low(0, 0)
            iterations(pool, iteration)
            root(2, B - 1, nb)

            with pool.Fori(0, B) as b:
                for i in range(2):
                    pool.wait_ge(s_lB, LB * b + 3 * (i + 1))
                    pool.tensor_tensor(LT[:, 2 + i, :], LT[:, 2 + i, :], zT[:, 2 + i, :], ALU.add).then_inc(s_aB, 1)

            pool.wait_ge(s_st2, 1)

            def scores(t):
                for i, c in enumerate(TURNS):
                    if c < 2:
                        pool.wait_ge(s_mC, 2 * t + c + 1)
                    else:
                        pool.wait_ge(s_lC, LB * t + 2 * (i + 1))
                        pool.tensor_tensor(LT[:, c, :], LT[:, c, :], LR[:, c - 2, :], ALU.add).then_inc(s_aC, 1)
                        pool.wait_ge(s_aC, 2 * t + i + 1)
                    if not isinstance(t, int):
                        pool.wait_ge(s_zt, C * t)
                    if i or not isinstance(t, int):
                        pool.wait_ge(s_z, C * t + i)
                    pool.tensor_tensor(gate[:], zero[:], zero[:], ALU.add)
                    pool.tensor_scalar(zT[:, c, :], LT[:, c, :], c2[:, c:c + 1], d2[:, c:c + 1],
                                       ALU.mult, ALU.add).then_inc(s_z, 1)

            scores(0)
            with pool.Fori(1, B) as t:
                scores(t)

            def elu_sum(b):
                pool.wait_ge(s_elu, 3 * (b + 1))
                if not (isinstance(b, int) and b == 0):
                    pool.wait_ge(s_et, b)
                pool.tensor_tensor(elT, eT4, pT4, ALU.add).then_inc(s_el, 1)

            def fourth(t, p, age, left):
                if left > 1:
                    root(3, t + 2, na)
                if left > 2:
                    elu_sum(t + 3)
                if age:
                    root_shift(t - 1)

            elu_sum(0)
            root(3, 0, na)
            elu_sum(1)
            root(3, 1, na)
            elu_sum(2)
            last_layer(pool, fourth)
            root_shift(B - 1)

        @block.scalar
        def _(act):
            act.wait_ge(s_w, 16 * WEIGHT_LOADS)
            act.wait_ge(s_pre, PRE_STEPS)

            def hidden(b):
                for h in range(2):
                    act.wait_ge(s_hid, 2 * b + h + 1)
                    if not (isinstance(b, int) and b == 0):
                        act.wait_ge(s_y, b)
                    act.activation(hidT[:, h, :], bank[3 + h][:], ACT.Relu,
                                   bias=col[:, CI["b1_0"] + h:CI["b1_0"] + h + 1]).then_inc(s_hidr, 1)

            def x1_t(b, p, old):
                act.wait_ge(s_x1t, b + 1)
                if old:
                    act.wait_ge(s_gru, 6 * (b - 1))
                act.copy(x1p[p][0][:], bank[3][:]).then_inc(s_x1T, 1)
                act.copy(x1T[:, p, :], bank[3][:]).then_inc(s_x1T, 1)

            def x2_t(b):
                act.wait_ge(s_x2t, b + 1)
                if not (isinstance(b, int) and b == 0):
                    act.wait_ge(s_wh, b)
                act.copy(x2T, bank[5][:]).then_inc(s_x2T, 1)

            def iteration(t, p, first, last):
                act.wait_ge(s_s, t + 1)
                if not first:
                    act.wait_ge(s_slr, S_STEPS * t)
                act.activation(Sx[SE, :], bank[1][SE, :], ACT.Identity, bias=mask[SE, 0:1]).then_inc(s_srow, 1)
                act.wait_ge(s_c1, t + 1)
                if not first:
                    act.wait_ge(s_cv, 2 * t)
                act.activation(c1w[:, PAD:PAD + N], bank[2][:], ACT.Relu, bias=bnbi[:, 0:1],
                               scale=bnsc[:, 0:1]).then_inc(s_c1T, 1)
                for k in range(2):
                    act.wait_ge(s_c1l, 5 * t + k + 1)
                    act.copy(c1p[0][:, k, 0:L - k], c1d[:, k, 0:L - k]).then_inc(s_c1T, 1)
                act.wait_ge(s_c1T, 4 * t + 1)
                act.copy(c1p[0][:, 2, :], c1_phases()[1]).then_inc(s_c1T, 1)
                for c in range(C):
                    act.wait_ge(s_dist, C * t + c + 1)
                    if not first:
                        act.wait_ge(s_nmp, t)
                    act.activation(AT[:, c, :], bank[DIST[c]][:], ACT.Exp).then_inc(s_exp, 1)
                if not last:
                    hidden(t + 1)
                if not first:
                    x2_t(t - 1)
                act.wait_ge(s_cvx, 2 * (t + 1))
                if not first:
                    act.wait_ge(s_gate, GATES * t)
                act.activation(xcp[0][:], xcT[:], ACT.Relu, bias=bnbi[:, 1:2]).then_inc(s_xc, 1)
                act.activation(xcT[:], xcT[:], ACT.Relu, bias=bnbi[:, 1:2]).then_inc(s_xc, 1)
                act.wait_ge(s_nmp, t + 1)
                act.copy(xnp_[0][:], bank[2][:]).then_inc(s_xn, 1)
                if not last:
                    x1_t(t + 1, 1 - p, not first)
                act.wait_ge(s_gate, GATES * t + 1)
                if not first:
                    act.wait_ge(s_tv, t)
                act.activation(ghT[:], bank[7][:], ACT.Identity,
                               bias=col[:, CI["b_hh_n"]:CI["b_hh_n"] + 1]).then_inc(s_gh, 1)
                act.wait_ge(s_gate, GATES * t + 2)
                act.wait_ge(s_xcl, t + 1)
                act.activation(trT[:], bank[4][:], ACT.Tanh, bias=half_b[:, 0:1], scale=0.5).then_inc(s_tr, 1)
                act.wait_ge(s_gate, GATES * t + 3)
                act.activation(tzT[:], bank[5][:], ACT.Tanh, bias=half_b[:, 1:2], scale=0.5).then_inc(s_tz, 1)
                act.wait_ge(s_gru, 6 * t + 2)
                act.activation(nT[:], nT[:], ACT.Tanh,
                               bias=col[:, CI["b_ih_n"]:CI["b_ih_n"] + 1]).then_inc(s_n, 1)

            hidden(0)
            x1_t(0, 0, False)
            iterations(act, iteration)
            x2_t(B - 1)

            act.wait_ge(s_ET, 1)
            act.copy(ET[:], bank[0][0:B * C, 0:P]).then_inc(s_ETc, 1)

            def normed(b, p, c, s):
                act.activation(LT[:, c, :], ebc[p][:], ACT.Identity, bias=tt1[:, b, c:c + 1],
                               scale=s1[:, c:c + 1]).then_inc(s, 1)

            act.wait_ge(s_ps, STAT1)

            def leaky_parts(b, p, c, relu, s):
                for k, (dst, f) in enumerate(((LT[:, c, :], ACT.Identity), (relu, ACT.Relu))):
                    act.activation(dst, ebc[p][:], f, bias=tt1k[:, k, b, c:c + 1],
                                   scale=s1k[:, k, c:c + 1]).then_inc(s, 1)

            def stats_tiles(b, p, first):
                act.wait_ge(s_ebc, 16 * (b + 1))
                for i, c in enumerate((0, 2, 1, 3)):
                    if not first:
                        act.wait_ge(s_bB, C * (b - 1) + i + 1)
                    if c < 2:
                        normed(b, p, c, s_lB)
                    else:
                        leaky_parts(b, p, c, zT[:, c, :], s_lB)

            stats_tiles(0, 0, True)
            stats_tiles(1, 1, False)
            with act.Fori(0, (B - 2) // 2) as i:
                stats_tiles(i * 2 + 2, 0, False)
                stats_tiles(i * 2 + 3, 1, False)

            def normed_all(b, p):
                act.wait_ge(s_ebcC, 16 * (b + 1))
                for i, c in enumerate(TURNS):
                    if not (isinstance(b, int) and b == 0):
                        act.wait_ge(s_z, C * (b - 1) + i + 1)
                    if c < 2:
                        normed(b, p, c, s_lC)
                    else:
                        leaky_parts(b, p, c, LR[:, c - 2, :], s_lC)

            def product_out(t):
                act.wait_ge(s_hp, t + 1)
                if not (isinstance(t, int) and t == 0):
                    act.wait_ge(s_hpst, 16 * t)
                    act.wait_ge(s_hps, t)
                act.copy(hpT[:], bank[7][:]).then_inc(s_hpe, 1)

            def third(t, p, first, last):
                for c in range(C):
                    act.wait_ge(s_mx, C * t + c + 1)
                    if not first:
                        act.wait_ge(s_pt, C * t)
                    act.activation(PTs[c][:], bank[c][:], ACT.Exp, bias=nmax[:, c:c + 1],
                                   accum_out=rsum[:, c:c + 1]).then_inc(s_ex, 1)
                if not first:
                    product_out(t - 1)
                if not last:
                    normed_all(t + 2, p)

            act.wait_ge(s_bB, C * B)
            normed_all(0, 0)
            normed_all(1, 1)
            third(0, 0, True, False)
            third(1, 1, False, False)
            with act.Fori(0, (B - 4) // 2) as i:
                third(i * 2 + 2, 0, False, False)
                third(i * 2 + 3, 1, False, False)
            third(B - 2, 0, False, True)
            third(B - 1, 1, False, True)
            product_out(B - 1)

            act.wait_ge(s_st3, STAT3)

            def elu(b):
                act.wait_ge(s_hl, 16 * (b + 1))
                if not (isinstance(b, int) and b == 0):
                    act.wait_ge(s_el, b)
                act.activation(pT4, hT[:], ACT.Relu, bias=a3[:, 1:2], scale=a3[:, 0:1]).then_inc(s_elu, 1)
                act.activation(eT4, hT[:], ACT.Relu, bias=a3[:, 3:4], scale=a3[:, 2:3]).then_inc(s_elu, 1)
                act.wait_ge(s_elu, 3 * b + 2)
                act.activation(eT4, eT4, ACT.Exp, scale=-1.0).then_inc(s_elu, 1)

            def copy_x3(b):
                act.wait_ge(s_x3t, b + 1)
                if not (isinstance(b, int) and b == 0):
                    act.wait_ge(s_h3, b)
                act.copy(x3T, bank[1][:]).then_inc(s_x3T, 1)

            def head_e(b, p, old):
                act.wait_ge(s_e3, b + 1)
                if old:
                    act.wait_ge(s_y4, C * (b - 1))
                ef = bank[7][:, 0:2 * C].rearrange("p (c k) -> p c k", c=C)
                for k in range(2):
                    act.activation(fx[:, p, k, :], ef[:, :, k], ACT.Exp, bias=ec[:, k:k + 1]).then_inc(s_efx, 1)

            def weigh(b, p):
                act.wait_ge(s_h3, b + 1)
                act.wait_ge(s_efx, 2 * (b + 1))
                if not (isinstance(b, int) and b == 0):
                    act.wait_ge(s_num, b)
                for c in range(C):
                    act.activation(gB[:, c, :], tok(bank[2])[:, c, :], ACT.Copy,
                                   scale=fx[:, p, 1, c:c + 1]).then_inc(s_g, 1)

            def first_denominator(b, p):
                if not (isinstance(b, int) and b == 0):
                    act.wait_ge(s_dt, b)
                act.activation(den, adj[:, b, 0, :], ACT.Copy, scale=fx[:, p, 1, 0:1]).then_inc(s_den, 1)

            def norm4(b, p, later):
                act.wait_ge(s_rt[4], (ROOT_STEPS + 2) * (b + 1))
                if later:
                    act.wait_ge(s_out, 16 * b)
                for c in range(C):
                    act.activation(outk[:, c, :], y4[p][:, c, :], ACT.Identity, bias=nb.h[:, c:c + 1],
                                   scale=nb.y[:, c:c + 1]).then_inc(s_ln4, 1)

            def fourth(t, p, age, left):
                if left > 2:
                    elu(t + 3)
                if left > 0:
                    copy_x3(t + 1)
                if age > 1:
                    norm4(t - 2, p, age > 2)
                act.wait_ge(s_num, t + 1)
                if age:
                    act.wait_ge(s_nt, t)
                act.copy(numT, bank[3][:]).then_inc(s_numc, 1)
                if left > 0:
                    head_e(t + 1, 1 - p, age)
                if left > 0:
                    weigh(t + 1, 1 - p)
                    first_denominator(t + 1, 1 - p)

            elu(0)
            elu(1)
            elu(2)
            copy_x3(0)
            head_e(0, 0, False)
            weigh(0, 0)
            first_denominator(0, 0)
            last_layer(act, fourth)
            norm4(B - 2, 0, True)
            norm4(B - 1, 1, True)

        @block.vector
        def _(dve):
            pre = Steps(dve, s_pre, 0, PRE_STEPS)
            pre.did(dve.memset(ones[:], 1.0))
            pre.did(dve.memset(zero[:], 0.0))
            pre.did(dve.memset(c15[:], 1.5))
            pre.did(dve.memset(zero4[:], 0.0))
            pre.did(dve.memset(c1w[:, 0:PAD], 0.0))
            pre.did(dve.memset(c1w[:, PAD + N:], 0.0))
            dve.wait_ge(s_w, 16 * WEIGHT_LOADS)
            pre.wait()
            pre.did(dve.tensor_scalar(eps1[:], sc[:, 0:1], 1.0, None, ALU.add))
            pre.did(dve.tensor_scalar(AT[:, 0, 0:P], ones[:], col[:, CI["W_b"]:CI["W_b"] + 1], None, ALU.mult))
            pre.did(dve.tensor_tensor(half_b[:], col[:, CI["b_ih_r"]:CI["b_ih_r"] + 2],
                                      col[:, CI["b_hh_r"]:CI["b_hh_r"] + 2], ALU.add))
            rsqrt(dve, pre, bnv[:], bnr[:], bnt[:], col[:, CI["bn1_v"]:CI["bn1_v"] + 2], LN_EPS)
            pre.did(dve.tensor_tensor(bnsc[:], bnr[:], col[:, CI["bn1_g"]:CI["bn1_g"] + 2], ALU.mult))
            pre.wait()
            pre.did(dve.tensor_tensor(bnt[:], bnsc[:], col[:, CI["bn1_m"]:CI["bn1_m"] + 2], ALU.mult))
            pre.wait()
            dve.wait_ge(s_prep, 1)
            dve.tensor_copy(l2wt[:, D:], bank[7][:, 0:2]).then_inc(s_half, 1)
            dve.tensor_copy(v34[:], bank[7][:, 2:4]).then_inc(s_half, 1)
            dve.tensor_scalar(ec[:, 0:1], bank[7][:, 4:5], sc[:, 1:2], None, ALU.add).then_inc(s_half, 1)
            dve.tensor_copy(ec[:, 1:2], bank[7][:, 5:6]).then_inc(s_half, 1)
            pre.did(dve.tensor_tensor(bnbi[:], col[:, CI["bn1_b"]:CI["bn1_b"] + 2], bnt[:], ALU.subtract))
            pre.did(dve.tensor_scalar(half_b[:], half_b[:], 0.5, None, ALU.mult))
            pre.end()
            def split(i, done):
                (hi, lo), at = SPLITS[i]
                w = raw(at, hi_size(hi))
                hi, lo = flat_of(hi), flat_of(lo)
                dve.tensor_copy(hi, w).then_inc(s_split, 1)
                dve.wait_ge(s_split, done + 1)
                dve.tensor_tensor(lo, w, hi.bitcast(F32), ALU.subtract).then_inc(s_split, 1)

            def add_taps():
                taps = raw(12 * D, (TAPS + PAIRS) * D).rearrange("p (k d) -> p k d", d=D)
                of_pair = taps[:, 0:2 * PAIRS, :].rearrange("p (j r) d -> p j r d", r=2)
                dve.tensor_tensor(taps[:, TAPS:, :], of_pair[:, :, 0, :], of_pair[:, :, 1, :],
                                  ALU.add).then_inc(s_split, 1)
                dve.wait_ge(s_split, 3)

            def make_h0(b):
                dve.wait_ge(s_agg, b + 1)
                if not (isinstance(b, int) and b == 0):
                    dve.wait_ge(s_c1l, 5 * b)
                dve.wait_ge(s_x, 32 * (b + 1))
                if not (isinstance(b, int) and b == 0):
                    dve.wait_ge(s_hid, 2 * b)
                dve.scalar_tensor_tensor(out=h0T, in0=xT[:], scalar=eps1[:, 0:1], in1=bank[4][:],
                                         op0=ALU.mult, op1=ALU.add).then_inc(s_h0, 1)
                dve.wait_ge(s_h0, b + 1)
                dve.tensor_copy(h0p[0][:], h0T).then_inc(s_h0p, 1)
                dve.wait_ge(s_h0p, 2 * b + 1)
                dve.tensor_tensor(h0p[1][:], h0T, h0p[0][:].bitcast(F32), ALU.subtract).then_inc(s_h0p, 1)

            def make_x1(b):
                dve.wait_ge(s_y, b + 1)
                dve.wait_ge(s_xb, b + 1)
                if not (isinstance(b, int) and b == 0):
                    dve.wait_ge(s_x1t, b)
                dve.tensor_tensor(yk[:], tok(bank[6]), xk[:], ALU.add).then_inc(s_ysb, 1)
                dve.wait_ge(s_ysb, b + 1)
                norm_stats(dve, Steps(dve, s_st[1], b, STAT_STEPS), yk, na)

            def finish_x1(b):
                dve.wait_ge(s_rt[1], ROOT_STEPS * (b + 1))
                norm_apply(dve, s_ln1, yk, yk, na)

            def make_x2(b):
                dve.wait_ge(s_tv, b + 1)
                norm_stats(dve, Steps(dve, s_st[2], b, STAT_STEPS), tok(bank[5]), nb)

            def finish_x2(b):
                dve.wait_ge(s_rt[2], ROOT_STEPS * (b + 1))
                if not (isinstance(b, int) and b == 0):
                    dve.wait_ge(s_x2st, 16 * b)
                    dve.wait_ge(s_x2t, b)
                norm_apply(dve, s_ln2, x2k, tok(bank[5]), nb)

            def keep_wh(b):
                dve.wait_ge(s_wh, b + 1)
                if not (isinstance(b, int) and b == 0):
                    dve.wait_ge(s_whst, 16 * b)
                for c0, c1, src in ((0, C - 1, bank[7][:, 0:(C - 1) * (D + 2)]), (C - 1, C, bank[1][:, 0:D + 2])):
                    src = src.rearrange("p (c k) -> p c k", k=D + 2)
                    dve.tensor_copy(whk[:, c0:c1, :], src[:, :, 0:D]).then_inc(s_whk, 1)
                    dve.tensor_copy(E12[:, b, c0:c1], src[:, :, D:]).then_inc(s_ec, 1)

            def iteration(t, p, first, last):
                dve.wait_ge(s_srow, t + 1)
                if not first:
                    dve.wait_ge(s_dist, C * t)
                st = Steps(dve, s_slr, t, S_STEPS)
                st.did(dve.tensor_tensor(Sx[96:P, :], Sx[96:P, :], Sx[96:P, :], ALU.mult))
                st.wait()
                st.did(dve.tensor_copy(Rt[SE, :], Sx[SE, :]))
                st.wait()
                st.did(dve.tensor_tensor(Lt[SE, :], Sx[SE, :], Rt[SE, :].bitcast(F32), ALU.subtract))
                for side, k in ((Rt, 1), (Lt, 4)):
                    st.wait()
                    st.did(dve.tensor_scalar(Sx[SE, :], Rt[SE, :].bitcast(F32), mask[SE, k:k + 1],
                                             mask[SE, k + 2:k + 3], ALU.mult, ALU.add))
                    st.wait()
                    st.did(dve.scalar_tensor_tensor(out=side[0:64, :], in0=Lt[SE, :].bitcast(F32),
                                                    scalar=mask[SE, k + 1:k + 2], in1=Sx[SE, :],
                                                    op0=ALU.mult, op1=ALU.add))
                st.end()
                if not first:
                    make_x2(t - 1)
                dve.wait_ge(s_msg, t + 1)
                if not first:
                    dve.wait_ge(s_nmp, t)
                dve.tensor_tensor(msg[:], tok(bank[3]), row[:, RI["b_msg"]:RI["b_msg"] + 1, :].broadcast_to((P, C, D)),
                                  ALU.add).then_inc(s_msgb, 1)
                if not last:
                    make_h0(t + 1)
                for c in range(C):
                    if c == 2 and not first:
                        finish_x2(t - 1)
                    dve.wait_ge(s_exp, C * t + c + 1)
                    dve.wait_ge(s_adj, 16 * (t + 1))
                    dve.tensor_tensor(AT[:, c, :], AT[:, c, :], adj[:, adj_slot(t), c, :], ALU.mult).then_inc(s_A, 1)
                dve.wait_ge(s_cv, 2 * t + 1)
                dve.scalar_tensor_tensor(out=by_parity(xcT[:]), scalar=bnsc[:, 1:2], in1=by_parity(x1T[:, p, :]),
                                         in0=bank[0][:].rearrange("p (r m) -> p r m", r=2),
                                         op0=ALU.mult, op1=ALU.add).then_inc(s_cvx, 1)
                if not last:
                    make_x1(t + 1)
                if not first:
                    keep_wh(t - 1)
                dve.wait_ge(s_cv, 2 * (t + 1))
                dve.wait_ge(s_cvx, 2 * t + 1)
                dve.scalar_tensor_tensor(out=by_parity(xcT[:]), scalar=bnsc[:, 1:2], in1=by_parity(xcT[:]),
                                         in0=bank[1][:, M:].rearrange("p (a m) -> p a m", a=1).broadcast_to((P, 2, M)),
                                         op0=ALU.mult, op1=ALU.add).then_inc(s_cvx, 1)
                dve.wait_ge(s_xc, 2 * (t + 1))
                if not first:
                    dve.wait_ge(s_gate, GATES * t)
                dve.tensor_tensor(xcp[1][:], xcT[:], xcp[0][:].bitcast(F32), ALU.subtract).then_inc(s_xcl, 1)
                if not last:
                    finish_x1(t + 1)
                dve.wait_ge(s_xn, t + 1)
                dve.tensor_tensor(xnp_[1][:], bank[2][:], xnp_[0][:].bitcast(F32), ALU.subtract).then_inc(s_xnl, 1)
                st = Steps(dve, s_gru, t, 6)
                dve.wait_ge(s_gh, t + 1)
                dve.wait_ge(s_tr, t + 1)
                st.did(dve.scalar_tensor_tensor(out=nT[:], in0=trT[:], scalar=1.0, in1=ghT[:],
                                                op0=ALU.add, op1=ALU.mult))
                st.wait()
                dve.wait_ge(s_gate, GATES * (t + 1))
                st.did(dve.scalar_tensor_tensor(out=nT[:], in0=nT[:], scalar=0.5, in1=bank[6][:],
                                                op0=ALU.mult, op1=ALU.add))
                dve.wait_ge(s_n, t + 1)
                st.did(dve.tensor_tensor(ghT[:], x1T[:, p, :], nT[:], ALU.subtract))
                st.wait()
                dve.wait_ge(s_tz, t + 1)
                st.did(dve.scalar_tensor_tensor(out=ghT[:], in0=tzT[:], scalar=1.0, in1=ghT[:],
                                                op0=ALU.add, op1=ALU.mult))
                st.did(dve.tensor_tensor(nT[:], x1T[:, p, :], nT[:], ALU.add))
                st.wait()
                if not first:
                    dve.wait_ge(s_tv, t)
                st.did(dve.scalar_tensor_tensor(out=vT[:], in0=ghT[:], scalar=0.5, in1=nT[:],
                                                op0=ALU.mult, op1=ALU.add))
                st.end()

            split(0, 0)
            make_h0(0)
            dve.wait_ge(s_w2, 16)
            add_taps()
            split(1, 3)
            make_x1(0)
            dve.wait_ge(s_w3, 16 * 3)
            for i in range(2, len(SPLITS)):
                split(i, 2 * i + 1)
            finish_x1(0)
            iterations(dve, iteration)
            make_x2(B - 1)
            finish_x2(B - 1)
            keep_wh(B - 1)

            st = Steps(dve, s_ps, 0, STAT1)
            dve.wait_ge(s_ec, 2 * B)
            st.did(dve.tensor_copy(e1[:], E12[:, :, :, 0].rearrange("p b c -> p (b c)")))
            st.did(dve.tensor_copy(ejT[:], E12[:, :, :, 1].rearrange("p b c -> p c b")))
            st.wait()
            dve.wait_ge(s_mbp, 1)
            st.did(dve.tensor_reduce(mb[:], bank[1][:, 0:B * C].rearrange("p (b c) -> p b c", c=C), AX.X, ALU.add))
            st.wait()
            st.did(dve.tensor_scalar(mb[:], mb[:], 1.0 / N, None, ALU.mult))
            st.wait()
            st.did(dve.tensor_reduce(mtot[:], mb[:], AX.X, ALU.add))
            st.wait()
            st.did(dve.tensor_scalar(mtot[:], mtot[:], 1.0 / B, None, ALU.mult))
            st.wait()
            st.did(dve.tensor_scalar(e1c[:], e1[:], mtot[:, 0:1], None, ALU.subtract))
            st.did(dve.tensor_scalar(mbc[:], mb[:], mtot[:, 0:1], None, ALU.subtract))
            st.wait()
            st.did(dve.tensor_tensor(e1c[:], e1c[:], e1c[:], ALU.mult))
            st.did(dve.tensor_reduce(mj[:], ejT[:], AX.X, ALU.add))
            st.wait()
            st.did(dve.tensor_scalar(mj[:], mj[:], 1.0 / B, None, ALU.mult))
            st.wait()
            st.did(dve.tensor_tensor(dj[:], ejT[:], mj[:].rearrange("p (c a) -> p c a", a=1).broadcast_to((P, C, B)),
                                     ALU.subtract))
            st.wait()
            st.did(dve.scalar_tensor_tensor(out=djq[:],
                                            in0=mbc[:].rearrange("p (a b) -> p a b", a=1).broadcast_to((P, C, B)),
                                            scalar=2.0, in1=dj[:], op0=ALU.mult, op1=ALU.add))
            st.wait()
            st.did(dve.tensor_tensor(djq[:], djq[:], dj[:], ALU.mult))
            dve.wait_ge(s_vp, 1)
            st.did(dve.tensor_reduce(vare[:], bank[2][:, 0:B * C], AX.X, ALU.add))
            st.wait()
            st.did(dve.tensor_reduce(vj[:], djq[:], AX.X, ALU.add))
            st.did(dve.tensor_scalar(vare[:], vare[:], 1.0 / BN, None, ALU.mult))
            st.wait()
            st.did(dve.tensor_scalar(vj[:], vj[:], 1.0 / B, vare[:, 0:1], ALU.mult, ALU.add))
            st.wait()
            rsqrt(dve, st, lv[:], lr[:], lt[:], vj[:], LN_EPS)
            st.did(dve.tensor_tensor(s1[:], lr[:], col[:, CI["g1_0"]:CI["g1_0"] + C], ALU.mult))
            st.did(dve.tensor_scalar(t1[:], dj[:], mtot[:, 0:1], None, ALU.subtract))
            st.wait()
            st.did(dve.tensor_tensor(t1[:], t1[:], s1[:].rearrange("p (c a) -> p c a", a=1).broadcast_to((P, C, B)),
                                     ALU.mult))
            st.wait()
            st.did(dve.tensor_tensor(tt1[:], t1[:].rearrange("p c b -> p b c"),
                                     col[:, CI["be1_0"]:CI["be1_0"] + C].rearrange("p (a c) -> p a c", a=1)
                                     .broadcast_to((P, B, C)), ALU.add))
            st.wait()
            for k, part in enumerate((SLOPE, 1 - SLOPE)):
                st.did(dve.tensor_scalar(s1k[:, k, :], s1[:], part, None, ALU.mult))
                st.did(dve.tensor_scalar(tt1k[:, k], tt1[:], part, None, ALU.mult))
            st.end()

            def leaky(c, done):
                dve.scalar_tensor_tensor(out=LT[:, c, :], in0=LT[:, c, :], scalar=SLOPE, in1=LT[:, c, :],
                                         op0=ALU.mult, op1=ALU.max).then_inc(done, 1)

            def counted(b, c):
                if c < 2:
                    dve.wait_ge(s_mB, 2 * b + c + 1)
                else:
                    dve.wait_ge(s_aB, 2 * b + c - 1)
                dve.bn_stats(st2[:, c, b, :], LT[:, c, :]).then_inc(s_bB, 1)

            def count_batch(b, first):
                dve.wait_ge(s_lB, LB * b + 1)
                leaky(0, s_mB)
                if not first:
                    counted(b - 1, 3)
                counted(b, 0)
                dve.wait_ge(s_lB, LB * b + 4)
                leaky(1, s_mB)
                counted(b, 2)
                counted(b, 1)

            count_batch(0, True)
            with dve.Fori(1, B) as b:
                count_batch(b, False)
            counted(B - 1, 3)
            dve.wait_ge(s_bB, C * B)
            s2 = Steps(dve, s_on, 0, C + RSQRT_STEPS + 2)
            for c in range(C):
                s2.did(dve.bn_aggr(mv2[:, c, :], st2[:, c, :, :].rearrange("p b s -> p (b s)")))
            s2.wait()
            rsqrt(dve, s2, lv[:], lr[:], lt[:], mv2[:, :, 1], LN_EPS)
            s2.did(dve.tensor_tensor(c2[:], lr[:], col[:, CI["g2_0"]:CI["g2_0"] + C], ALU.mult))
            s2.wait()
            s2.did(dve.tensor_tensor(d2[:], c2[:], mv2[:, :, 0], ALU.mult))
            s2.wait()
            dve.tensor_tensor(d2[:], col[:, CI["be2_0"]:CI["be2_0"] + C], d2[:], ALU.subtract).then_inc(s_st2, 1)
            s2.end()

            def third_leaky(t, c):
                dve.wait_ge(s_lC, LB * t + 5 + c)
                leaky(c, s_mC)

            def row_max(t, c, first):
                dve.wait_ge(s_zt, C * t + c + 1)
                if not first:
                    dve.wait_ge(s_ex, C * t)
                dve.tensor_reduce(nmax[:, c:c + 1], bank[c][:], AX.X, ALU.max, negate=True).then_inc(s_mx, 1)

            def row_diag(t, c):
                dve.wait_ge(s_ex, C * t + c + 1)
                dve.reciprocal(rrec[:, c:c + 1], rsum[:, c:c + 1]).then_inc(s_rr, 1)
                dve.wait_ge(s_rr, C * t + c + 1)
                dve.tensor_scalar(diag[:, c * P:(c + 1) * P], ident[:], rrec[:, c:c + 1], None,
                                  ALU.mult).then_inc(s_dg, 1)

            def masked(t, c):
                dve.wait_ge(s_pt, C * t + c + 1)
                dve.tensor_tensor(PA[c], bank[PB[c]][:], adj[:, t, c, :], ALU.mult).then_inc(s_pa, 1)

            def third_stats(t):
                dve.wait_ge(s_hpe, t + 1)
                dve.bn_stats(st3[:, t, :], hpT[:]).then_inc(s_hps, 1)

            def third(t, first, last):
                for c in range(C):
                    row_max(t, c, first)
                for c in range(C):
                    row_diag(t, c)
                if not last:
                    for c in range(2):
                        third_leaky(t + 1, c)
                masked(t, 0)
                masked(t, 1)
                if not first:
                    third_stats(t - 1)
                masked(t, 2)
                masked(t, 3)

            dve.wait_ge(s_adj2, 16 * WSLOTS)
            for c in range(2):
                third_leaky(0, c)
            third(0, True, False)
            with dve.Fori(1, B - 1) as t:
                third(t, False, False)
            third(B - 1, False, True)
            third_stats(B - 1)

            s3 = Steps(dve, s_st3, 0, STAT3)
            dve.wait_ge(s_hps, B)
            s3.did(dve.bn_aggr(mv3[:], st3[:, :, :].rearrange("p b s -> p (b s)")))
            s3.wait()
            rsqrt(dve, s3, lv[:, 0:1], lr[:, 0:1], lt[:, 0:1], mv3[:, 1:2], LN_EPS)
            s3.did(dve.tensor_tensor(a3[:, 0:1], lr[:, 0:1], col[:, CI["g3"]:CI["g3"] + 1], ALU.mult))
            s3.wait()
            s3.did(dve.tensor_tensor(lt[:, 0:1], a3[:, 0:1], mv3[:, 0:1], ALU.mult))
            s3.wait()
            s3.did(dve.tensor_tensor(a3[:, 1:2], col[:, CI["b3"]:CI["b3"] + 1], lt[:, 0:1], ALU.subtract))
            s3.wait()
            s3.did(dve.tensor_scalar(a3[:, 2:4], a3[:, 0:2], -1.0, None, ALU.mult))
            s3.end()

            def head(b, p):
                if not (isinstance(b, int) and b < 2):
                    dve.wait_ge(s_ln3, C * (b - 1))
                dve.wait_ge(s_et, b + 1)
                dve.wait_ge(s_x2l, 16 * (b + 1))
                dve.scalar_tensor_tensor(out=y3[p], in0=tok(bank[0]), scalar=-1.0, in1=x2l[:], op0=ALU.add,
                                         op1=ALU.add).then_inc(s_y3, 1)
                dve.wait_ge(s_y3, b + 1)
                if not (isinstance(b, int) and b == 0):
                    dve.wait_ge(s_ln3, C * b)
                norm_stats(dve, Steps(dve, s_st[3], b, STAT_STEPS), y3[p], na)

            def head_x3(b, p):
                dve.wait_ge(s_rt[3], ROOT_STEPS * (b + 1))
                norm_apply(dve, s_ln3, x3k[p], y3[p], na)

            def denominator(b, p):
                for c in range(1, C):
                    dve.wait_ge(s_den, C * b + c)
                    dve.scalar_tensor_tensor(out=den, in0=adj[:, b, c, :], scalar=fx[:, p, 1, c:c + 1], in1=den,
                                             op0=ALU.mult, op1=ALU.add).then_inc(s_den, 1)

            def weights(t, p):
                dve.wait_ge(s_dt, t + 1)
                dve.tensor_tensor(fw[:, 0, :], bank[6][:, 0:C], fx[:, p, 0, :], ALU.mult).then_inc(s_wr, 1)
                dve.wait_ge(s_wr, 3 * t + 1)
                dve.reciprocal(fw[:, 1, :], fw[:, 0, :]).then_inc(s_wr, 1)
                dve.wait_ge(s_wr, 3 * t + 2)
                dve.tensor_tensor(fw[:, 2, :], fw[:, 1, :], fx[:, p, 0, :], ALU.mult).then_inc(s_wr, 1)

            def tail(t, p, age):
                dve.wait_ge(s_wr, 3 * t + 3)
                dve.wait_ge(s_nt, t + 1)
                if age > 1:
                    dve.wait_ge(s_ln4, C * (t - 1))
                for c in range(C):
                    dve.scalar_tensor_tensor(out=y4[p][:, c, :], in0=tok(bank[5])[:, c, :], scalar=fw[:, 2, c:c + 1],
                                             in1=x3k[p][:, c, :], op0=ALU.mult, op1=ALU.add).then_inc(s_y4, 1)

            def tail_stats(b, p, age):
                dve.wait_ge(s_y4, C * (b + 1))
                if age > 1:
                    dve.wait_ge(s_ln4, C * b)
                norm_stats(dve, Steps(dve, s_st[4], b, STAT_STEPS), y4[p], nb)

            def fourth(t, p, age, left):
                if left > 1:
                    head(t + 2, p)
                denominator(t, p)
                if age:
                    tail_stats(t - 1, 1 - p, age)
                weights(t, p)
                tail(t, p, age)
                if left > 1:
                    dve.wait_ge(s_y4, C * (t + 1))
                    head_x3(t + 2, p)

            head(0, 0)
            head_x3(0, 0)
            head(1, 1)
            head_x3(1, 1)
            last_layer(dve, fourth)
            tail_stats(B - 1, 1, 3)

        @block.tensor
        def _(pe):
            def mm(out_, w, x, start, stop):
                return pe.matmul(out_, w, x, start=start, stop=stop)

            def mm3(out_, w, x, start, stop):
                pe.matmul(out_, w[0], x[0], start=start, stop=False)
                pe.matmul(out_, w[0], x[1], start=False, stop=False)
                return pe.matmul(out_, w[1], x[0], start=False, stop=stop)

            def turn4(dst, src):
                for c in range(C):
                    ins = pe.transpose(dst[:, c * P:(c + 1) * P], src[:, c * P:(c + 1) * P], ident[:])
                return ins

            def flat(t):
                return t[:].rearrange("p c d -> p (c d)")

            def aggregate(b):
                pe.wait_ge(s_adj, 16 * (b + 1))
                pe.wait_ge(s_x, 32 * (b + 1))
                for c in range(C):
                    ins = mm(bank[4][:], xk[:, c, :], adj[:, adj_slot(b), c, :], c == 0, c == C - 1)
                ins.then_inc(s_agg, 1)

            aggregate(0)
            pe.wait_ge(s_w, 16 * WEIGHT_LOADS)
            pe.wait_ge(s_pre, 6 + 2)
            a34 = col[:, CI["l3_a1"]:CI["l3_a1"] + 2]
            mm(bank[7][:, 0:2], l2w[:], col[:, CI["a1"]:CI["a1"] + 2], True, True)
            mm(bank[7][:, 2:4], l3w[:], a34, True, True)
            mm(bank[7][:, 4:6], AT[:, 0, 0:P], a34, True, True).then_inc(s_prep, 1)
            pe.wait_ge(s_pre, PRE_STEPS)
            pe.wait_ge(s_half, 4)

            def hid(b):
                pe.wait_ge(s_h0p, 2 * (b + 1))
                if not (isinstance(b, int) and b == 0):
                    pe.wait_ge(s_msgb, b)
                for h in range(2):
                    hs = slice(h * D, (h + 1) * D)
                    mm3(bank[3 + h][:], [w[:, hs] for w in w1p], [x[:] for x in h0p], True, True).then_inc(s_hid, 1)

            def y_rows(b):
                pe.wait_ge(s_hidr, 2 * (b + 1))
                if not (isinstance(b, int) and b == 0):
                    pe.wait_ge(s_exp, C * (b - 1) + 2)
                for c in range(C):
                    for h in range(2):
                        ins = mm(bank[6][:, c * D:(c + 1) * D], hidT[:, h, c * P:(c + 1) * P], w2s[:, h, :],
                                 h == 0, h == 1)
                ins.then_inc(s_y, 1)

            def turn_x1(b):
                pe.wait_ge(s_ln1, C * (b + 1))
                turn4(bank[3], flat(yk)).then_inc(s_x1t, 1)

            def turn_v(b):
                pe.wait_ge(s_gru, 6 * (b + 1))
                turn4(bank[5], vT).then_inc(s_tv, 1)

            def turn_x2(b):
                pe.wait_ge(s_ln2, C * (b + 1))
                turn4(bank[5], flat(x2k)).then_inc(s_x2t, 1)

            def third_in(b):
                pe.wait_ge(s_x2T, b + 1)
                if isinstance(b, int) and b == B - 1:
                    pe.wait_ge(s_gh, B)
                else:
                    pe.wait_ge(s_exp, C * (b + 1) + 3)
                for c in range(C):
                    ins = mm(wh_psum(c), x2T[:, c * P:(c + 1) * P], l2wt[:], True, True)
                ins.then_inc(s_wh, 1)

            def iteration(t, p, first, last):
                xT1 = x1T[:, p, :]
                x1 = [x[:] for x in x1p[p]]
                pe.wait_ge(s_x1T, 2 * (t + 1))
                mm(bank[1][SE, :], wse[:], xT1, True, True).then_inc(s_s, 1)
                for c in range(C):
                    ins = mm(bank[3][:, c * D:(c + 1) * D], xT1[:, c * P:(c + 1) * P], wmsg[:], True, True)
                ins.then_inc(s_msg, 1)
                pe.wait_ge(s_x1l, t + 1)
                if not first:
                    pe.wait_ge(s_xnl, t)
                mm3(bank[2][:], [w[:] for w in conv1p], x1, True, True).then_inc(s_c1, 1)
                if not last:
                    if not first:
                        pe.wait_ge(s_tr, t)
                    aggregate(t + 1)
                if not first:
                    turn_v(t - 1)
                if not first:
                    pe.wait_ge(s_cvx, 2 * t)

                def conv(part, k0, k1):
                    taps = (range(0, TAPS, 2), range(1, TAPS, 2), [*range(TAPS, TAPS + PAIRS), TAPS - 1])[part]
                    dst = (bank[0][:, 0:M], bank[0][:, M:], bank[1][:, M:])[part]
                    pe.wait_ge(s_c1l, 5 * t + part + 3)
                    for k in range(k0, min(k1, len(taps))):
                        ins = mm3(dst, [w[:, taps[k], :] for w in conv2p], [x[:, part, k:k + M] for x in c1p],
                                  k == 0, k == len(taps) - 1)
                    return ins

                conv(0, 0, TAPS)
                conv(1, 0, 4)
                if not first:
                    pe.wait_ge(s_gh, t)
                pe.wait_ge(s_slr, S_STEPS * (t + 1))
                for c in range(C):
                    mm(bank[DIST[c]][:], Lt[0:64, c * P:(c + 1) * P], Rt[0:64, :], True, True).then_inc(s_dist, 1)
                conv(1, 4, TAPS).then_inc(s_cv, 1)
                pe.wait_ge(s_exp, C * t + 1)
                conv(2, 0, 4)
                if not last:
                    hid(t + 1)
                conv(2, 4, 7)
                if not last:
                    y_rows(t + 1)
                if not first:
                    turn_x2(t - 1)
                conv(2, 7, TAPS).then_inc(s_cv, 1)
                if not first:
                    third_in(t - 1)
                pe.wait_ge(s_A, C * (t + 1))
                pe.wait_ge(s_msgr, t + 1)
                for c in range(C):
                    ins = mm(bank[2][:], msg[:, c, :], AT[:, c, :], c == 0, c == C - 1)
                ins.then_inc(s_nmp, 1)
                if not first:
                    pe.wait_ge(s_ec, 2 * t)
                    pe.wait_ge(s_x2T, t)
                else:
                    pe.wait_ge(s_exp, C)
                mm3(bank[7][:], [w[:, 2 * D:3 * D] for w in whhp], x1, True, True).then_inc(s_gate, 1)
                if not last:
                    pe.wait_ge(s_hidr, 2 * (t + 2))
                    pe.wait_ge(s_ysb, t + 2)

                def gate_part(g, w, x, start, stop):
                    gs = slice(g * D, (g + 1) * D)
                    return mm3(bank[4 + g][:], [v[:, gs] for v in w], x, start, stop)

                for g in range(2):
                    gate_part(g, whhp, x1, True, False)
                if not last:
                    turn_x1(t + 1)
                pe.wait_ge(s_xcl, t + 1)
                for g in range(3):
                    gate_part(g, [w[:, 0, :] for w in wihp], [x[:] for x in xcp], g == 2, False)
                pe.wait_ge(s_xnl, t + 1)
                for g in range(3):
                    gate_part(g, [w[:, 1, :] for w in wihp], [x[:] for x in xnp_], False, True).then_inc(s_gate, 1)

            pe.wait_ge(s_split, 2)
            hid(0)
            y_rows(0)
            turn_x1(0)
            pe.wait_ge(s_split, N_SPLIT)
            iterations(pe, iteration)
            turn_v(B - 1)
            turn_x2(B - 1)
            third_in(B - 1)

            pe.wait_ge(s_ps, 2)
            mm(bank[1][:, 0:B * C], ones[:], e1[:], True, True).then_inc(s_mbp, 1)
            pe.transpose(bank[0][0:B * C, 0:P], e1[:], ident[:]).then_inc(s_ET, 1)
            pe.wait_ge(s_ps, 9)
            mm(bank[2][:, 0:B * C], ones[:], e1c[:], True, True).then_inc(s_vp, 1)

            def third_turn(t, first):
                if not first:
                    pe.wait_ge(s_ex, C * t)
                for i, k in enumerate(TURNS):
                    pe.wait_ge(s_z, C * t + i + 1)
                    for c in range(C):
                        ins = pe.transpose(bank[c][:, k * P:(k + 1) * P], zT[:, k, c * P:(c + 1) * P], ident[:])
                        if i == C - 1:
                            ins.then_inc(s_zt, 1)

            def third_turn_back(t):
                for c in range(C):
                    if c == 3:
                        pe.wait_ge(s_pa, C * t + 1)
                    for k in range(C):
                        if c == 0:
                            pe.wait_ge(s_dg, C * t + k + 1)
                        ins = mm(bank[PB[c]][:, k * P:(k + 1) * P], PTs[k][:, c * P:(c + 1) * P],
                                 diag[:, k * P:(k + 1) * P], True, True)
                    ins.then_inc(s_pt, 1)

            def third_product(t, first):
                pe.wait_ge(s_whl, 16 * (t + 1))
                if not first:
                    pe.wait_ge(s_hpe, t)
                for c in range(C):
                    pe.wait_ge(s_pa, C * t + c + 1)
                    ins = mm(bank[7][:], whk[:, c, :], PA[c], c == 0, c == C - 1)
                ins.then_inc(s_hp, 1)

            third_turn(0, True)
            third_turn_back(0)
            third_turn(1, False)
            third_product(0, True)
            with pe.Fori(1, B - 1) as t:
                third_turn_back(t)
                third_turn(t + 1, False)
                third_product(t, False)
            third_turn_back(B - 1)
            third_product(B - 1, False)

            def head_turn(b, first):
                pe.wait_ge(s_el, b + 1)
                if not first:
                    pe.wait_ge(s_y3, b)
                turn4(bank[0], elT).then_inc(s_et, 1)

            def head_turn_x3(b, p):
                pe.wait_ge(s_ln3, C * (b + 1))
                turn4(bank[1], x3k[p][:, :, :].rearrange("p c d -> p (c d)")).then_inc(s_x3t, 1)

            def head_ef(b):
                pe.wait_ge(s_x3T, b + 1)
                if not (isinstance(b, int) and b == 0):
                    pe.wait_ge(s_efx, 2 * b)
                for c in range(C):
                    ins = mm(bank[7][:, 2 * c:2 * c + 2], x3T[:, c * P:(c + 1) * P], v34[:], True, True)
                ins.then_inc(s_e3, 1)

            def head_h(b):
                if not (isinstance(b, int) and b == 0):
                    pe.wait_ge(s_g, C * b)
                for c in range(C):
                    mm(bank[2][:, c * D:(c + 1) * D], x3T[:, c * P:(c + 1) * P], l3wt[:], True, False)
                    ins = mm(bank[2][:, c * D:(c + 1) * D], ones[0:1, :], row[0:1, RI["W_b"], :], False, True)
                ins.then_inc(s_h3, 1)

            def tail_den(t):
                pe.wait_ge(s_den, C * (t + 1))
                for c in range(C):
                    ins = mm(bank[6][:, c:c + 1], den[:, c * P:(c + 1) * P], ones[:, 0:1], True, True)
                ins.then_inc(s_dt, 1)

            def tail_num(t, c0, c1):
                for c in range(c0, c1):
                    ins = mm(bank[3][:], gB[:, c, :], adj[:, t, c, :], c == 0, c == C - 1)
                return ins

            def fourth(t, p, age, left):
                if left > 1:
                    head_turn(t + 2, False)
                pe.wait_ge(s_g, C * (t + 1))
                if age:
                    pe.wait_ge(s_numc, t)
                tail_num(t, 0, 2)
                if left > 0:
                    head_turn_x3(t + 1, 1 - p)
                tail_num(t, 2, C).then_inc(s_num, 1)
                if left > 0:
                    head_ef(t + 1)
                    head_h(t + 1)
                pe.wait_ge(s_numc, t + 1)
                if age:
                    pe.wait_ge(s_y4, C * t)
                turn4(bank[5], numT).then_inc(s_nt, 1)
                tail_den(t)

            head_turn(0, True)
            head_turn(1, False)
            head_turn_x3(0, 0)
            head_ef(0)
            head_h(0)
            last_layer(pe, fourth)


def s_columns(w_se):
    out = np.zeros((w_se.shape[1], 64), w_se.dtype)
    for block in (0, 32):
        for m in range(12):
            out[:, block + m] = w_se[m % 3]
    return out


def distance_rows(b_se, factors):
    out = np.zeros((64, 7), b_se.dtype)
    for block in (0, 32):
        for m in range(12):
            out[block + m, 0] = b_se[m % 3]
    out[:, 1:] = factors
    return out


def kernel(**inputs):
    import concourse.bacc as bacc
    from concourse.bass_utils import run_bass_kernel_spmd

    a = {k: np.asarray(v) for k, v in inputs.items()}
    factors = np.zeros((64, 6), np.float32)
    for d in range(3):
        for part in range(4):
            factors[3 * part + d] = [part % 2 == 0, part % 2, 0, 2 * (part < 2), 2 * (part > 1), 0]
        for part in range(2):
            factors[32 + 3 * part + d] = [part == 0, part, 0, 0, 0, -1]
            factors[38 + 3 * part + d] = [0, 0, -1, part == 0, part, 0]
    B, N, D = a["x"].shape

    def parts(v, n):
        return [v[i * P:(i + 1) * P] for i in range(n)]

    cols = {"g3": a["L2_gnn_g3"], "b3": a["L2_gnn_b3"], "a1": a["L2_gnn_a1"], "a2": a["L2_gnn_a2"],
            "l3_a1": a["L3_gnn_a_w"][:D], "l3_a2": a["L3_gnn_a_w"][D:], "W_b": a["L3_gnn_W_b"]}
    for i, v in enumerate(parts(a["L0_gnn_b1"], 2)):
        cols[f"b1_{i}"] = v
    for k in ("bn1", "bn2"):
        for s in "gbmv":
            cols[f"{k}_{s}"] = a[f"L1_gnn_{k}_{s}"]
    for k in ("b_ih", "b_hh"):
        for g, v in zip("rzn", parts(a[f"L1_gnn_{k}"], 3)):
            cols[f"{k}_{g}"] = v
    for new, old in (("g1", "g1"), ("be1", "b1"), ("g2", "g2"), ("be2", "b2")):
        for i, v in enumerate(parts(a[f"L2_gnn_{old}"], N // P)):
            cols[f"{new}_{i}"] = v
    arrays = {
        "x_tok": a["x"], "x_fm": a["x"].transpose(0, 2, 1), "adj_t": a["adj"].transpose(0, 2, 1),
        "w1": a["L0_gnn_W1"], "w2": a["L0_gnn_W2"],
        "cols": np.stack([cols[c] for c in COLS], axis=1),
        "rows": np.stack([a["L0_gnn_b2"], a["L1_gnn_b_msg"], a["L3_gnn_W_b"]]),
        "scal": np.concatenate([a["L0_gnn_eps"], a["L3_gnn_a_b"]]),
        "masks": distance_rows(a["L1_gnn_b_se"], factors), "w_se": s_columns(a["L1_gnn_w_se"]),
        "conv1": a["L1_gnn_conv1_w"][:, :, 0].T, "conv2": a["L1_gnn_conv2_w"].transpose(1, 2, 0),
        "w_msg": a["L1_gnn_w_msg"].T, "w_ih": a["L1_gnn_w_ih"].T, "w_hh": a["L1_gnn_w_hh"].T,
        "l2_w": a["L2_gnn_W"], "l2_wt": a["L2_gnn_W"].T, "l3_w": a["L3_gnn_W_w"], "l3_wt": a["L3_gnn_W_w"].T,
        "ident_in": np.eye(P, dtype=np.float32),
    }
    arrays = {k: np.ascontiguousarray(v) for k, v in arrays.items()}
    nc = bacc.Bacc("TRN2", target_bir_lowering=False, num_devices=1)
    args = [nc.dram_tensor(k, v.shape, mybir.dt.from_np(v.dtype), kind="ExternalInput").ap()
            for k, v in arrays.items()]
    out = nc.dram_tensor("out", (B, N, D), F32, kind="ExternalOutput").ap()
    build(nc, *args, out)
    r = run_bass_kernel_spmd(nc, [arrays], core_ids=[0])
    return r.results[0]["out"]
```
